# Optimizing a Trainium2 kernel written in Bass

```python
import numpy as np
import jax
import jax.numpy as jnp

def _softmax(x, axis=-1):
    return jax.nn.softmax(x, axis=axis)

def _gelu(x):
    return jax.nn.gelu(x, approximate=True)

def _silu(x):
    return jax.nn.silu(x)

def _sigmoid(x):
    return jax.nn.sigmoid(x)

def _layernorm(x, axis=-1, eps=1e-05):
    m = jnp.mean(x, axis=axis, keepdims=True)
    v = jnp.var(x, axis=axis, keepdims=True)
    return (x - m) / jnp.sqrt(v + eps)

def _scatter_add(tgt, idx, src, axis=0):
    return tgt.at[idx].add(src)

def _segment_sum(src, seg, n):
    return jax.ops.segment_sum(src, seg, n)
kernel_name = 'mk_decoder_postln_d1_seqx_r4_eae3f8'

def setup_inputs(seed: int=0):
    np.random.seed(seed)
    _w = jnp.asarray

    def _rec_inputs():
        import jax
        import jax.numpy as jnp
        _rk = jax.random.key(seed)
        x = 7.22e-05 + 1 * jax.random.normal(jax.random.fold_in(_rk, 1), (64, 128, 256), jnp.float32)
        _lenS = 128 - jax.random.randint(jax.random.fold_in(_rk, 7), (64,), 0, max(1, 128 // 4) + 1, jnp.int32)
        _lenS2 = 128 - jax.random.randint(jax.random.fold_in(_rk, 8), (64,), 0, max(1, 128 // 4) + 1, jnp.int32)
        _ctx_768P = jax.random.normal(jax.random.fold_in(_rk, 11), (64, 16, 192), jnp.float32)
        _ctx_768c = jax.random.dirichlet(jax.random.fold_in(_rk, 511), 0.3 * jnp.ones((16,), jnp.float32), (64, 128))
        _ctx_768t = jnp.einsum('bsk,bkd->bsd', _ctx_768c, _ctx_768P)
        _ctx_768t = _ctx_768t * jax.lax.rsqrt(jnp.mean(jnp.square(_ctx_768t)) + 1e-12) * 0.953939
        ctx_768 = 2.09791e-05 + 1.00001 * (_ctx_768t + 0.3 * jax.random.normal(jax.random.fold_in(_rk, 611), (64, 128, 192), jnp.float32))
        return (x, ctx_768)
    x, ctx_768 = _rec_inputs()

    def _L0_attn_setup():
        import jax, jax.numpy as jnp
        import numpy as np
        LN_EPS = 1e-05

        def _layernorm(x, gamma, beta):
            mu = jnp.mean(x, axis=-1, keepdims=True)
            var = jnp.var(x, axis=-1, keepdims=True)
            return (x - mu) * jax.lax.rsqrt(var + LN_EPS) * gamma + beta
        key = jax.random.key(seed)
        ks = jax.random.split(key, 6)
        B, T, C = (4, 1024, 256)
        xavier = float(np.sqrt(6.0 / (C + C)))
        inp = {'x': jax.random.normal(ks[0], (B, T, C), dtype=jnp.float32), 'time_decay': jnp.zeros((C,), dtype=jnp.float32), 'time_first': jnp.ones((C,), dtype=jnp.float32), 'Wk': jax.random.uniform(ks[1], (C, C), jnp.float32, -xavier, xavier), 'Wv': jax.random.uniform(ks[2], (C, C), jnp.float32, -xavier, xavier), 'Wr': jax.random.uniform(ks[3], (C, C), jnp.float32, -xavier, xavier), 'Wo': jax.random.uniform(ks[4], (C, C), jnp.float32, -xavier, xavier), 'ln_gamma': jnp.ones((C,), dtype=jnp.float32), 'ln_beta': jnp.zeros((C,), dtype=jnp.float32)}
        return inp
    _L0_attn_all = _L0_attn_setup()
    _L0_attn_in = {k: v for k, v in _L0_attn_all.items() if k in ('time_decay', 'time_first', 'Wk', 'Wv', 'Wr', 'Wo', 'ln_gamma', 'ln_beta')}
    del _L0_attn_all

    def _L0_xattn_setup():
        import jax, jax.numpy as jnp
        import numpy as np
        HEADS = 8
        DIM_HEAD = 64
        SCALE = DIM_HEAD ** (-0.5)
        key = jax.random.key(seed)
        ks = jax.random.split(key, 7)
        b, n, m = (4, 512, 256)
        qd, cd, inner = (256, 192, HEADS * DIM_HEAD)
        s = lambda fan_in: 1.0 / np.sqrt(fan_in)
        return {'x': jax.random.normal(ks[0], (b, n, qd), jnp.float32), 'context': jax.random.normal(ks[1], (b, m, cd), jnp.float32), 'Wq': jax.random.normal(ks[2], (qd, inner), jnp.float32) * s(qd), 'Wk': jax.random.normal(ks[3], (cd, inner), jnp.float32) * s(cd), 'Wv': jax.random.normal(ks[4], (cd, inner), jnp.float32) * s(cd), 'Wout': jax.random.normal(ks[5], (inner, qd), jnp.float32) * s(inner), 'bout': jax.random.normal(ks[6], (qd,), jnp.float32) * 0.01}
    _L0_xattn_all = _L0_xattn_setup()
    _L0_xattn_in = {k: v for k, v in _L0_xattn_all.items() if k in ('Wq', 'Wk', 'Wv', 'Wout', 'bout')}
    del _L0_xattn_all

    def _L0_ffn_setup():
        import jax, jax.numpy as jnp
        import numpy as np
        B, S, D = (2, 512, 256)
        E, G, K = (32, 8, 4)
        H, SH = (512, 512)
        CAP_FACTOR = 1.25

        def _l2norm(v):
            n = jnp.linalg.norm(v, axis=-1, keepdims=True)
            return v / jnp.maximum(n, 1e-12)
        key = jax.random.key(seed)
        ks = jax.random.split(key, 10)
        x = jax.random.normal(ks[0], (B, S, D), jnp.float32)
        group_centroids = jax.random.normal(ks[1], (G, D), jnp.float32) * 0.02
        expert_centroids = jax.random.normal(ks[2], (E, D), jnp.float32) * 0.02
        bias = jnp.zeros((E,), jnp.float32)
        sd_in = 1.0 / np.sqrt(D).astype(np.float32)
        sd_h = 1.0 / np.sqrt(H).astype(np.float32)
        wg = jax.random.normal(ks[3], (E, D, H), jnp.float32) * sd_in
        wu = jax.random.normal(ks[4], (E, D, H), jnp.float32) * sd_in
        wd = jax.random.normal(ks[5], (E, H, D), jnp.float32) * sd_h
        sg = jax.random.normal(ks[6], (D, SH), jnp.float32) * sd_in
        su = jax.random.normal(ks[7], (D, SH), jnp.float32) * sd_in
        sd_w = jax.random.normal(ks[8], (SH, D), jnp.float32) * sd_h
        return dict(x=x, group_centroids=group_centroids, expert_centroids=expert_centroids, bias=bias, wg=wg, wu=wu, wd=wd, sg=sg, su=su, sd=sd_w)
    _L0_ffn_all = _L0_ffn_setup()
    _L0_ffn_in = {k: v for k, v in _L0_ffn_all.items() if k in ('group_centroids', 'expert_centroids', 'bias', 'wg', 'wu', 'wd', 'sg', 'su', 'sd')}
    del _L0_ffn_all
    return {'x': x, 'ctx_768': ctx_768, 'L0_attn_time_decay': _L0_attn_in['time_decay'], 'L0_attn_time_first': _L0_attn_in['time_first'], 'L0_attn_Wk': _L0_attn_in['Wk'], 'L0_attn_Wv': _L0_attn_in['Wv'], 'L0_attn_Wr': _L0_attn_in['Wr'], 'L0_attn_Wo': _L0_attn_in['Wo'], 'L0_attn_ln_gamma': _L0_attn_in['ln_gamma'], 'L0_attn_ln_beta': _L0_attn_in['ln_beta'], 'L0_xattn_Wq': _L0_xattn_in['Wq'], 'L0_xattn_Wk': _L0_xattn_in['Wk'], 'L0_xattn_Wv': _L0_xattn_in['Wv'], 'L0_xattn_Wout': _L0_xattn_in['Wout'], 'L0_xattn_bout': _L0_xattn_in['bout'], 'L0_ffn_group_centroids': _L0_ffn_in['group_centroids'], 'L0_ffn_expert_centroids': _L0_ffn_in['expert_centroids'], 'L0_ffn_bias': _L0_ffn_in['bias'], 'L0_ffn_wg': _L0_ffn_in['wg'], 'L0_ffn_wu': _L0_ffn_in['wu'], 'L0_ffn_wd': _L0_ffn_in['wd'], 'L0_ffn_sg': _L0_ffn_in['sg'], 'L0_ffn_su': _L0_ffn_in['su'], 'L0_ffn_sd': _L0_ffn_in['sd']}

def reference(x, ctx_768, L0_attn_time_decay, L0_attn_time_first, L0_attn_Wk, L0_attn_Wv, L0_attn_Wr, L0_attn_Wo, L0_attn_ln_gamma, L0_attn_ln_beta, L0_xattn_Wq, L0_xattn_Wk, L0_xattn_Wv, L0_xattn_Wout, L0_xattn_bout, L0_ffn_group_centroids, L0_ffn_expert_centroids, L0_ffn_bias, L0_ffn_wg, L0_ffn_wu, L0_ffn_wd, L0_ffn_sg, L0_ffn_su, L0_ffn_sd):
    import jax
    import jax.numpy as jnp

    def _L0_attn_ref(x, time_decay, time_first, Wk, Wv, Wr, Wo, ln_gamma, ln_beta):
        import jax, jax.numpy as jnp
        import numpy as np
        LN_EPS = 1e-05

        def _layernorm(x, gamma, beta):
            mu = jnp.mean(x, axis=-1, keepdims=True)
            var = jnp.var(x, axis=-1, keepdims=True)
            return (x - mu) * jax.lax.rsqrt(var + LN_EPS) * gamma + beta
        B, T, C = x.shape
        xn = _layernorm(x, ln_gamma, ln_beta)
        k = jnp.einsum('btc,dc->btd', xn, Wk)
        v = jnp.einsum('btc,dc->btd', xn, Wv)
        r = jnp.einsum('btc,dc->btd', xn, Wr)
        td = jax.nn.sigmoid(time_decay)
        tf = jax.nn.sigmoid(time_first)
        kv = k * v
        t_idx = jnp.arange(T, dtype=x.dtype)[None, :, None]
        weighted_kv = kv * jnp.power(td[None, None, :], t_idx)
        csum = jnp.cumsum(weighted_kv, axis=1)
        shifted = jnp.concatenate([jnp.zeros((B, 1, C), dtype=x.dtype), csum[:, :-1]], axis=1)
        wkv = tf * kv + td * shifted
        out = jnp.einsum('btc,dc->btd', jax.nn.sigmoid(r) * wkv, Wo)
        return out

    def _L0_xattn_ref(x, context, Wq, Wk, Wv, Wout, bout):
        import jax, jax.numpy as jnp
        import numpy as np
        HEADS = 8
        DIM_HEAD = 64
        SCALE = DIM_HEAD ** (-0.5)
        b, n, _ = x.shape
        m = context.shape[1]
        q = (x @ Wq).reshape(b, n, HEADS, DIM_HEAD)
        k = (context @ Wk).reshape(b, m, HEADS, DIM_HEAD)
        v = (context @ Wv).reshape(b, m, HEADS, DIM_HEAD)
        sim = jnp.einsum('bihd,bjhd->bhij', q, k) * SCALE
        attn = jax.nn.softmax(sim, axis=-1)
        out = jnp.einsum('bhij,bjhd->bihd', attn, v).reshape(b, n, HEADS * DIM_HEAD)
        return out @ Wout + bout

    def _L0_ffn_ref(x, group_centroids, expert_centroids, bias, wg, wu, wd, sg, su, sd):
        import jax, jax.numpy as jnp
        import numpy as np
        B, S, D = (2, 512, 256)
        E, G, K = (32, 8, 4)
        H, SH = (512, 512)
        CAP_FACTOR = 1.25

        def _l2norm(v):
            n = jnp.linalg.norm(v, axis=-1, keepdims=True)
            return v / jnp.maximum(n, 1e-12)
        b, s, d = x.shape
        xf = x.reshape(-1, d)
        N = xf.shape[0]
        shared = jax.nn.silu(xf @ sg) * (xf @ su) @ sd
        xn = _l2norm(xf)
        group_scores = xn @ _l2norm(group_centroids).T
        n_top_groups = max(1, G // 2)
        _, top_group_idx = jax.lax.top_k(group_scores, n_top_groups)
        expert_scores = xn @ _l2norm(expert_centroids).T + bias
        expert_to_group = jnp.arange(E) // (E // G)
        sel = jnp.zeros((N, G), xf.dtype).at[jnp.arange(N)[:, None], top_group_idx].set(1.0)
        group_mask = sel[:, expert_to_group]
        masked = expert_scores * group_mask + (1.0 - group_mask) * -1000000000.0
        top_scores, top_idx = jax.lax.top_k(masked, K)
        gates = jax.nn.softmax(top_scores, axis=-1)
        capacity = max(1, int(N / E * K * CAP_FACTOR))
        flat_e = top_idx.reshape(-1)
        flat_g = gates.reshape(-1)
        tok = jnp.repeat(jnp.arange(N), K)
        onehot = jax.nn.one_hot(flat_e, E, dtype=jnp.int32)
        pos = jnp.cumsum(onehot, axis=0)[jnp.arange(N * K), flat_e] - 1
        keep = pos < capacity
        e_s = jnp.where(keep, flat_e, E)
        p_s = jnp.where(keep, pos, 0)
        buf = jnp.zeros((E + 1, capacity, d), xf.dtype).at[e_s, p_s].set(xf[tok])[:E]
        h = jax.nn.silu(jnp.einsum('ecd,edh->ech', buf, wg)) * jnp.einsum('ecd,edh->ech', buf, wu)
        out_e = jnp.einsum('ech,ehd->ecd', h, wd)
        gathered = out_e[flat_e, jnp.minimum(pos, capacity - 1)]
        contrib = gathered * (flat_g * keep.astype(xf.dtype))[:, None]
        routed = jnp.zeros_like(xf).at[tok].add(contrib)
        return (shared + routed).reshape(b, s, d)
    x = _layernorm(x + _L0_attn_ref(x, L0_attn_time_decay, L0_attn_time_first, L0_attn_Wk, L0_attn_Wv, L0_attn_Wr, L0_attn_Wo, L0_attn_ln_gamma, L0_attn_ln_beta), axis=-1)
    x = _layernorm(x + _L0_xattn_ref(x, ctx_768, L0_xattn_Wq, L0_xattn_Wk, L0_xattn_Wv, L0_xattn_Wout, L0_xattn_bout), axis=-1)
    x = _layernorm(x + _L0_ffn_ref(x, L0_ffn_group_centroids, L0_ffn_expert_centroids, L0_ffn_bias, L0_ffn_wg, L0_ffn_wu, L0_ffn_wd, L0_ffn_sg, L0_ffn_su, L0_ffn_sd), axis=-1)
    return x

_drawn_inputs = setup_inputs


def setup_inputs(seed=0):
    import zlib

    import numpy as np

    out = dict(_drawn_inputs(seed))
    spreads = {'L0_attn_time_decay': (0.0, 0.1),
     'L0_attn_time_first': (1.0, 0.2),
     'L0_attn_ln_gamma': (1.0, 0.2),
     'L0_attn_ln_beta': (0.0, 0.1),
     'L0_ffn_bias': (0.0, 0.1)}
    factors = {}
    for name, (base, spread) in spreads.items():
        noise = np.random.default_rng([zlib.crc32(name.encode()), seed]).standard_normal(out[name].shape)
        drawn = base * np.exp(spread * noise) if base else spread * noise
        out[name] = jnp.asarray(drawn.astype(out[name].dtype))
    for name, factor in factors.items():
        out[name] = (out[name] * factor).astype(out[name].dtype)
    return out
```

```python
from contextlib import ExitStack

import concourse.bass as bass
from concourse import mybir

F32 = mybir.dt.float32
I32 = mybir.dt.int32
U32 = mybir.dt.uint32
ALU = mybir.AluOpType
ACT = mybir.ActivationFunctionType
AX = mybir.AxisListType

P = 128
B, T, D = 64, 128, 256
TG = 4
NG = B // TG
GW = TG * T
GX = TG * D
DC = D // P
CD, CC = 192, 96
HEADS, DH = 8, 64
INNER = HEADS * DH
IC = INNER // P
HID = 512
HC = HID // P
E, G, K = 32, 8, 4
EG = E // G
NTOP = G // 2
CAP = int(B * T / E * K * 1.25)
ST = CAP // P
SLOTS = E * CAP
FAR = 4 * SLOTS
EPS = 1e-5
SCALE = DH ** -0.5
NEG = 1e9


def rows(x, g, j=0, n=TG):
    return x[:, bass.ds(g * GX + j * D, n * D)]


def grouped(ap, n=TG):
    return ap.rearrange("p (t d) -> p t d", t=n)


def apart(eng, past):
    eng.sem_inc(past, 1)


ONE = 1
DMA = 16


def begin(eng, *counts, dma=()):
    for c in counts:
        eng.sem_inc(c, ONE)
    for c in dma:
        eng.sem_inc(c, DMA)


class Parts:

    def __init__(self, nc, ctx, tag):
        self.nc, self.ctx, self.tag = nc, ctx, tag

    def sb(self, name, shape, dt=F32):
        return self.ctx.enter_context(self.nc.sbuf_tensor(self.tag + name, shape, dt))

    def bank(self, name):
        return self.ctx.enter_context(self.nc.psum_tensor(self.tag + name, [P, 512], F32))

    def sem(self, name):
        return self.ctx.enter_context(self.nc.semaphore(self.tag + name))


def setup_stage(nc, k, dram):
    with ExitStack() as ctx:
        p = Parts(nc, ctx, "c_")
        td, tf = p.sb("td", [P, DC]), p.sb("tf", [P, DC])
        zero, ones = p.sb("zero", [P, T]), p.sb("ones", [P, T])
        cen, sq = p.sb("cen", [G + E, D]), p.sb("sq", [G + E, D])
        nrm = p.sb("nrm", [G + E, 4])
        half = p.sb("half", [P, 1])
        tp = p.bank("tp")
        vec_in, cen_in = p.sem("vec_in"), p.sem("cen_in")
        fill, ident, sig, tri = p.sem("fill"), p.sem("ident"), p.sem("sig"), p.sem("tri")
        table, cent, root, cen_t = p.sem("table"), p.sem("cent"), p.sem("root"), p.sem("cen_t")
        iot, squared = p.sem("iot"), p.sem("squared")

        with nc.Block() as block:
            @block.sync
            def _(sp):
                with nc.allow_non_contiguous_dma(reason="short vectors"):
                    for dst, src in ((td, dram["td"]), (tf, dram["tf"]), (k.gam, dram["gam"]), (k.bet, dram["bet"])):
                        sp.dma_start(dst[:], src.rearrange("(c p) -> p c", p=P)).then_inc(vec_in, 16)
                sp.dma_start(cen[0:G, :], dram["gcen"]).then_inc(cen_in, 16)
                sp.dma_start(cen[G:G + E, :], dram["ecen"]).then_inc(cen_in, 16)
                sp.dma_start(k.ebias[:], dram["ebias"].rearrange("(a e) -> a e", a=1).to_broadcast([P, E])).then_inc(vec_in, 16)
                sp.dma_start(k.bout[:], dram["bout"].rearrange("(a e) -> a e", a=1).to_broadcast([P, D])).then_inc(vec_in, 16)
                sp.wait_ge(vec_in, 96)

            @block.gpsimd
            def _(pool):
                pool.memset(k.ident[:], 0.0).then_inc(fill, 1)
                pool.memset(k.before[:], 1.0).then_inc(fill, 1)
                pool.memset(k.ones[:], 1.0).then_inc(fill, 1)
                pool.memset(k.mhalf[:], -0.5).then_inc(fill, 1)
                pool.memset(half[:], 0.5).then_inc(fill, 1)
                pool.memset(k.keep[:], 1.0).then_inc(fill, 1)
                pool.wait_ge(fill, 6)
                pool.affine_select(out=k.ident[:], in_=k.ident[:], compare_op=ALU.not_equal, fill=1.0, base=0,
                                   pattern=[[-1, P]], channel_multiplier=1).then_inc(ident, 1)
                pool.affine_select(out=k.before[:], in_=k.before[:], compare_op=ALU.is_gt, fill=0.0, base=0,
                                   pattern=[[1, P]], channel_multiplier=-1).then_inc(tri, 1)
                first = k.keep[:].rearrange("p (b t) -> p b t", b=TG)[:, :, 0:1]
                pool.memset(first, 0.0).then_inc(tri, 1)
                pool.iota(k.iota_e[:], pattern=[[1, E]], base=0, channel_multiplier=0,
                          allow_small_or_imprecise_dtypes=True).then_inc(iot, 1)
                pool.iota(k.tok[:], pattern=[[T, TG]], base=0, channel_multiplier=1).then_inc(iot, 1)
                pool.wait_ge(cent, 1)
                pool.tensor_tensor(nrm[:, 1:2], nrm[:, 0:1], half[0:G + E, :], ALU.pow).then_inc(root, 1)

            @block.scalar
            def _(act):
                act.wait_ge(vec_in, 96)
                act.activation(k.td[:], td[:], ACT.Sigmoid).then_inc(sig, 1)
                act.activation(k.tf[:], tf[:], ACT.Sigmoid).then_inc(sig, 1)

            @block.vector
            def _(dve):
                dve.memset(zero[:], 0.0).then_inc(table, 1)
                dve.memset(ones[:], 1.0).then_inc(table, 1)
                dve.memset(k.count[:], 0.0).then_inc(table, 1)
                dve.memset(k.wkv_in[:], 0.0).then_inc(table, 1)
                dve.wait_ge(table, 2)
                dve.wait_ge(sig, 2)
                for c in range(DC):
                    dve.tensor_scalar(k.decay[:, c, :], ones[:], k.td[:, c:c + 1], None, ALU.mult).then_inc(table, 1)
                    dve.wait_ge(table, 5 + 3 * c)
                    dve.tensor_tensor_scan(k.decay[:, c, :], k.decay[:, c, :], zero[:], 1.0, ALU.mult, ALU.add).then_inc(table, 1)
                    dve.wait_ge(table, 6 + 3 * c)
                    dve.memset(k.decay[:, c, T - 1:T], 0.0).then_inc(table, 1)
                dve.wait_ge(cen_in, 32)
                dve.tensor_tensor(sq[:], cen[:], cen[:], ALU.mult).then_inc(squared, 1)
                dve.wait_ge(squared, 1)
                dve.tensor_reduce(nrm[:, 0:1], sq[:], AX.X, ALU.add).then_inc(cent, 1)
                dve.wait_ge(root, 1)
                dve.tensor_scalar(nrm[:, 2:3], nrm[:, 1:2], 1e-12, None, ALU.max).then_inc(cent, 1)
                dve.wait_ge(cent, 2)
                dve.reciprocal(nrm[:, 3:4], nrm[:, 2:3]).then_inc(cent, 1)
                dve.wait_ge(cent, 3)
                dve.tensor_scalar(cen[:], cen[:], nrm[:, 3:4], None, ALU.mult).then_inc(cent, 1)
                dve.wait_ge(cen_t, 1)
                dve.tensor_copy(k.cent[:], tp[:, 0:DC * (G + E)].rearrange("p (c e) -> p c e", c=DC)).then_inc(cent, 1)

            @block.tensor
            def _(pe):
                pe.wait_ge(ident, 1)
                pe.wait_ge(cent, 4)
                for c in range(DC):
                    last = pe.transpose(tp[:, c * (G + E):(c + 1) * (G + E)], cen[:, c * P:(c + 1) * P],
                                        k.ident[0:G + E, 0:G + E])
                last.then_inc(cen_t, 1)


def mixer_stage(nc, k, dram):
    with ExitStack() as ctx:
        p = Parts(nc, ctx, "m_")
        w = {n: p.sb("w" + n, [P, DC, D]) for n in "kvro"}
        xn, xnt = p.sb("xn", [P, TG, D]), p.sb("xnt", [P, DC, GW])
        sr, kv = p.sb("sr", [P, DC, GW]), p.sb("kv", [P, DC, GW])
        kc = p.sb("kc", [P, DC, GW])
        run, y = p.sb("run", [P, DC, GW]), p.sb("y", [P, DC, GW])
        stat, stat2 = p.sb("stat", [P, TG, 6]), p.sb("stat2", [P, TG, 6])
        mv, mv2 = p.sb("mv", [P, TG, 2]), p.sb("mv2", [P, TG, 2])
        ve, ve2 = p.sb("ve", [P, TG]), p.sb("ve2", [P, TG])
        rs, rs2 = p.sb("rs", [P, TG]), p.sb("rs2", [P, TG])
        bank_t, bank_o = p.bank("t"), p.bank("o")
        bank = [{n: p.bank(f"{n}{c}") for n in "kvr"} for c in range(DC)]
        w_in, x_in = p.sem("w_in"), p.sem("x_in")
        stat_rdy, mv_rdy, ve_rdy, rs_rdy = p.sem("stat"), p.sem("mv"), p.sem("ve"), p.sem("rs")
        xn_rdy, t_done, xnt_rdy = p.sem("xn"), p.sem("t_done"), p.sem("xnt")
        kvr_done, kv_rdy, sr_rdy = p.sem("kvr"), p.sem("kv"), p.sem("sr")
        w_rdy, run_rdy, wkv_rdy, y_rdy = p.sem("w"), p.sem("run"), p.sem("wkv"), p.sem("y")
        o_done, h_rdy, stat2_rdy, mv2_rdy = p.sem("o_done"), p.sem("h"), p.sem("stat2"), p.sem("mv2")
        ve2_rdy, rs2_rdy, x1_rdy, kc_rdy = p.sem("ve2"), p.sem("rs2"), p.sem("x1"), p.sem("kc")

        with nc.Block() as block:
            @block.sync
            def _(sp):
                begin(sp, dma=(x_in, w_in,))
                sp.dma_start(grouped(rows(k.x, 0)), dram["x"].rearrange("b t d -> t b d")[:, 0:TG, :]).then_inc(x_in, 16)
                for n in "kvro":
                    sp.dma_start(w[n][:], dram["w" + n].rearrange("(c p) n -> p c n", p=P)).then_inc(w_in, 16)
                with sp.Fori(1, NG) as g:
                    sp.wait_ge(x_in, DMA + 16 * g)
                    sp.dma_start(grouped(rows(k.x, g)),
                                 dram["x"].rearrange("b t d -> t b d")[:, bass.ds(g * TG, TG), :]).then_inc(x_in, 16)

            @block.tensor
            def _(pe):
                begin(pe, t_done, kvr_done, o_done)
                def turn(g, c):
                    if c == 0:
                        pe.wait_ge(xn_rdy, ONE + g + 1)
                    pe.wait_ge(xnt_rdy, ONE + DC * g + c)
                    for j in range(TG):
                        last = pe.transpose(bank_t[:, j * P:(j + 1) * P], xn[:, j, c * P:(c + 1) * P], k.ident[:])
                    last.then_inc(t_done, 1)

                def project(g):
                    pe.wait_ge(xnt_rdy, ONE + DC * (g + 1))
                    pe.wait_ge(kv_rdy, ONE + DC * g)
                    pe.wait_ge(sr_rdy, ONE + DC * g)
                    for c in range(DC):
                        for n in "kvr":
                            for q in range(DC):
                                last = pe.matmul(bank[c][n][:], w[n][:, q, c * P:(c + 1) * P], xnt[:, q, :],
                                                 start=(q == 0), stop=(q == DC - 1))
                            last.then_inc(kvr_done, 1)

                def mix(g, h):
                    pe.wait_ge(y_rdy, ONE + DC * (g + 1))
                    pe.wait_ge(h_rdy, ONE + 2 * g + h)
                    for j in range(2 * h, 2 * h + 2):
                        for q in range(DC):
                            last = pe.matmul(bank_o[:, (j % 2) * D:(j % 2 + 1) * D], y[:, q, j * T:(j + 1) * T],
                                             w["o"][:, q, :], start=(q == 0), stop=(q == DC - 1))
                    last.then_inc(o_done, 1)

                turn(0, 0)
                turn(0, 1)
                pe.wait_ge(w_in, DMA + 64)
                project(0)
                turn(1, 0)
                turn(1, 1)
                with pe.Fori(1, NG - 1) as g:
                    project(g)
                    turn(g + 1, 0)
                    mix(g - 1, 0)
                    turn(g + 1, 1)
                    mix(g - 1, 1)
                project(NG - 1)
                for g in (NG - 2, NG - 1):
                    mix(g, 0)
                    mix(g, 1)

            @block.scalar
            def _(act):
                begin(act, xnt_rdy, sr_rdy, kc_rdy)
                def norm_out(g):
                    for c in range(DC):
                        act.wait_ge(t_done, ONE + DC * g + c + 1)
                        act.wait_ge(kvr_done, ONE + 3 * DC * g)
                        act.activation(xnt[:, c, :], bank_t[:], ACT.Identity, bias=k.bet[:, c:c + 1],
                                       scale=k.gam[:, c:c + 1]).then_inc(xnt_rdy, 1)

                def gate(g):
                    for c in range(DC):
                        act.wait_ge(kvr_done, ONE + 3 * DC * g + 3 * c + 1)
                        act.wait_ge(kv_rdy, ONE + DC * g + c)
                        act.activation(kc[:, c, :], bank[c]["k"][:], ACT.Copy).then_inc(kc_rdy, 1)
                        act.wait_ge(kvr_done, ONE + 3 * DC * g + 3 * c + 3)
                        act.wait_ge(y_rdy, ONE + DC * g)
                        act.activation(sr[:, c, :], bank[c]["r"][:], ACT.Sigmoid).then_inc(sr_rdy, 1)

                norm_out(0)
                with act.Fori(0, NG - 1) as g:
                    gate(g)
                    norm_out(g + 1)
                gate(NG - 1)

            @block.gpsimd
            def _(pool):
                begin(pool, ve_rdy, rs_rdy, w_rdy, y_rdy, ve2_rdy, rs2_rdy)
                def rstd(g, mv_s, ve_s, rs_s, mv_t, ve_t, rs_t):
                    pool.wait_ge(mv_s, ONE + g + 1)
                    apart(pool, k.past_pool)
                    pool.tensor_scalar(ve_t[:], mv_t[:, :, 1], EPS, None, ALU.add).then_inc(ve_s, 1)
                    pool.wait_ge(ve_s, ONE + g + 1)
                    pool.tensor_tensor(rs_t[:], ve_t[:], k.mhalf[:], ALU.pow).then_inc(rs_s, 1)

                def decayed(g, c):
                    pool.wait_ge(kv_rdy, ONE + DC * g + c + 1)
                    pool.wait_ge(run_rdy, ONE + DC * g)
                    pool.tensor_tensor(k.wkv_in[:, c, 1:GW + 1].rearrange("p (b t) -> p b t", b=TG),
                                       kv[:, c, :].rearrange("p (b t) -> p b t", b=TG),
                                       k.decay[:, c, None, :].to_broadcast([P, TG, T]), ALU.mult).then_inc(w_rdy, 1)

                def gated(g, c):
                    pool.wait_ge(wkv_rdy, ONE + DC * g + c + 1)
                    pool.wait_ge(sr_rdy, ONE + DC * g + c + 1)
                    pool.wait_ge(o_done, ONE + 2 * g)
                    pool.tensor_tensor(y[:, c, :], run[:, c, :], sr[:, c, :], ALU.mult).then_inc(y_rdy, 1)

                def recur(g, more=True):
                    for c in range(DC):
                        decayed(g, c)
                    if more:
                        rstd(g + 1, mv_rdy, ve_rdy, rs_rdy, mv, ve, rs)
                    for c in range(DC):
                        gated(g, c)

                rstd(0, mv_rdy, ve_rdy, rs_rdy, mv, ve, rs)
                recur(0)
                with pool.Fori(1, NG - 1) as g:
                    recur(g)
                    rstd(g - 1, mv2_rdy, ve2_rdy, rs2_rdy, mv2, ve2, rs2)
                recur(NG - 1, False)
                for g in (NG - 2, NG - 1):
                    rstd(g, mv2_rdy, ve2_rdy, rs2_rdy, mv2, ve2, rs2)

            @block.vector
            def _(dve):
                begin(dve, stat_rdy, mv_rdy, xn_rdy, kv_rdy, run_rdy, wkv_rdy, h_rdy, stat2_rdy, mv2_rdy)
                def moments(g, st, mvt, st_s, mv_s):
                    apart(dve, k.past_dve)
                    for j in range(TG):
                        dve.bn_stats(st[:, j, :], rows(k.x, g, j, 1)).then_inc(st_s, 1)
                    for j in range(TG):
                        dve.wait_ge(st_s, ONE + TG * g + j + 1)
                        apart(dve, k.past_dve)
                        last = dve.bn_aggr(mvt[:, j, :], st[:, j, :])
                    last.then_inc(mv_s, 1)

                def moments_in(g):
                    dve.wait_ge(x_in, DMA + 16 * (g + 1))
                    moments(g, stat, mv, stat_rdy, mv_rdy)

                def norm_in(g):
                    dve.wait_ge(rs_rdy, ONE + g + 1)
                    dve.wait_ge(t_done, ONE + DC * g)
                    for j in range(TG):
                        last = dve.tensor_scalar(xn[:, j, :], rows(k.x, g, j, 1), mv[:, j, 0:1], rs[:, j:j + 1],
                                                 ALU.subtract, ALU.mult)
                    last.then_inc(xn_rdy, 1)

                def recur(g, more=True):
                    for c in range(DC):
                        dve.wait_ge(kvr_done, ONE + 3 * DC * g + 3 * c + 2)
                        dve.wait_ge(w_rdy, ONE + DC * g)
                        dve.wait_ge(kc_rdy, ONE + DC * g + c + 1)
                        dve.tensor_tensor(kv[:, c, :], kc[:, c, :], bank[c]["v"][:], ALU.mult).then_inc(kv_rdy, 1)
                    if more:
                        moments_in(g + 1)
                    for c in range(DC):
                        dve.wait_ge(w_rdy, ONE + DC * g + c + 1)
                        dve.wait_ge(y_rdy, ONE + DC * g)
                        dve.tensor_tensor_scan(run[:, c, :], k.keep[:], k.wkv_in[:, c, 0:GW], 0.0,
                                               ALU.mult, ALU.add).then_inc(run_rdy, 1)
                        dve.wait_ge(run_rdy, ONE + DC * g + c + 1)
                        dve.scalar_tensor_tensor(run[:, c, :], kv[:, c, :], k.tf[:, c:c + 1], run[:, c, :],
                                                 ALU.mult, ALU.add).then_inc(wkv_rdy, 1)

                def norm_out(g):
                    for h in range(2):
                        dve.wait_ge(o_done, ONE + 2 * g + h + 1)
                        dve.tensor_tensor(rows(k.x, g, 2 * h, 2), bank_o[:], rows(k.x, g, 2 * h, 2), ALU.add)\
                           .then_inc(h_rdy, 1)
                    dve.wait_ge(h_rdy, ONE + 2 * (g + 1))
                    moments(g, stat2, mv2, stat2_rdy, mv2_rdy)
                    dve.wait_ge(rs2_rdy, ONE + g + 1)
                    for j in range(TG):
                        last = dve.tensor_scalar(rows(k.x, g, j, 1), rows(k.x, g, j, 1), mv2[:, j, 0:1],
                                                 rs2[:, j:j + 1], ALU.subtract, ALU.mult)
                    last.then_inc(x1_rdy, 1)

                moments_in(0)
                norm_in(0)
                recur(0)
                norm_in(1)
                with dve.Fori(1, NG - 1) as g:
                    recur(g)
                    norm_in(g + 1)
                    norm_out(g - 1)
                recur(NG - 1, False)
                norm_out(NG - 2)
                norm_out(NG - 1)

def attention_stage(nc, k, dram):
    with ExitStack() as ctx:
        p = Parts(nc, ctx, "a_")
        wq, wk, wv = p.sb("wq", [P, DC, INNER]), p.sb("wk", [CC, 2, INNER]), p.sb("wv", [CC, 2, INNER])
        wo = p.sb("wo", [P, IC, D])
        xs, xt = p.sb("xs", [P, TG, D]), p.sb("xt", [P, DC, GW])
        ct = [p.sb(f"ct{i}", [CC, 2, GW]) for i in range(2)]
        qt = [p.sb(f"qt{i}", [P, IC, GW]) for i in range(2)]
        kt = [p.sb(f"kt{i}", [P, IC, GW]) for i in range(2)]
        vv = [p.sb(f"vv{i}", [P, TG, INNER]) for i in range(2)]
        prob, prob_t = p.sb("prob", [P, HEADS, T]), p.sb("prob_t", [P, HEADS, T])
        ot = p.sb("ot", [P, IC, T])
        top, nbias = p.sb("top", [P, HEADS]), p.sb("nbias", [P, HEADS])
        den, rden = p.sb("den", [P, HEADS]), p.sb("rden", [P, HEADS])
        stat, mv = p.sb("stat", [P, TG, 6]), p.sb("mv", [P, TG, 2])
        ve, rs = p.sb("ve", [P, TG]), p.sb("rs", [P, TG])
        bank_a = [p.bank(f"a{i}") for i in range(2)]
        bank_s = [p.bank(f"s{i}") for i in range(2)]
        bank_t = [p.bank(f"t{i}") for i in range(2)]
        bank_v, bank_o = p.bank("v"), p.bank("o")
        w_in, wo_in = p.sem("w_in"), p.sem("wo_in")
        c_in = [p.sem(f"c_in{i}") for i in range(2)]
        a_done, a_out = p.sem("a_done"), p.sem("a_out")
        s_done, top_rdy, nb_rdy, e_rdy = p.sem("s_done"), p.sem("top"), p.sem("nb"), p.sem("e")
        rden_rdy, n_rdy, t_done, t_out = p.sem("rden"), p.sem("n"), p.sem("t_done"), p.sem("t_out")
        v_done, ot_rdy, o_done, h_rdy = p.sem("v_done"), p.sem("ot"), p.sem("o_done"), p.sem("h")
        xb_rdy, stat_rdy, mv_rdy, ve_rdy = p.sem("xb"), p.sem("stat"), p.sem("mv"), p.sem("ve")
        rs_rdy, x2_rdy, x2_out, xs_rdy = p.sem("rs"), p.sem("x2"), p.sem("x2_out"), p.sem("xs")

        JOBS = [("t", 0), ("t", 1)] + [("q", m) for m in range(IC)] + [("k", m) for m in range(IC)] \
            + [("v", b) for b in range(TG)]
        NJ = len(JOBS)
        Q_LAST = 2 + IC - 1
        PARTS = [range(0, 4), range(4, 7), range(7, 10), range(10, 14)]
        assert NJ % 2 == 0 and PARTS[-1][-1] == NJ - 1

        ctx_d = dram["ctx"].rearrange("(c p) n -> p c n", p=CC)

        def groups(eng, slot, part):
            for q in range(4):
                part(0, 0, q)
            for b in range(TG):
                slot(0, 0, b, lambda b=b: part(1, 1, b), b == 0)
            with eng.Fori(0, (NG - 2) // 2) as i:
                for par in (1, 0):
                    g = 2 * i + (1 if par else 2)
                    for b in range(TG):
                        slot(g, par, b, lambda g=g, par=par, b=b: part(g + 1, 1 - par, b), False)
            for b in range(TG):
                slot(NG - 1, 1, b, lambda: None, False)

        with nc.Block() as block:
            @block.sync
            def _(sp):
                begin(sp, dma=(w_in, wo_in, *c_in, x2_out,))
                sp.dma_start(wq[:], dram["wq"].rearrange("(c p) n -> p c n", p=P)).then_inc(w_in, 16)
                sp.dma_start(wk[:], dram["wxk"].rearrange("(c p) n -> p c n", p=CC)).then_inc(w_in, 16)
                sp.dma_start(ct[0][:], ctx_d[:, :, 0:GW]).then_inc(c_in[0], 16)
                sp.dma_start(wv[:], dram["wxv"].rearrange("(c p) n -> p c n", p=CC)).then_inc(w_in, 16)
                sp.dma_start(wo[:], dram["wout"].rearrange("(c p) n -> p c n", p=P)).then_inc(wo_in, 16)
                sp.dma_start(ct[1][:], ctx_d[:, :, GW:2 * GW]).then_inc(c_in[1], 16)

                def store(g):
                    sp.wait_ge(x2_rdy, ONE + g + 1)
                    sp.dma_start(k.x2_d[bass.ds(g * GW, GW), :].rearrange("(b t) d -> t b d", b=TG),
                                 grouped(rows(k.x, g))).then_inc(x2_out, 16)

                with sp.Fori(0, (NG - 2) // 2) as i:
                    for par in range(2):
                        g = 2 * i + par
                        sp.wait_ge(a_done, ONE + NJ * (g + 1))
                        sp.dma_start(ct[par][:], ctx_d[:, :, bass.ds((g + 2) * GW, GW)]).then_inc(c_in[par], 16)
                        store(g)
                store(NG - 2)
                store(NG - 1)
                sp.wait_ge(x2_out, DMA + 16 * NG)

            @block.tensor
            def _(pe):
                begin(pe, a_done, s_done, t_done, v_done, o_done)
                def part(g, par, q):
                    for n in PARTS[q]:
                        kind, m = JOBS[n]
                        out = bank_a[n % 2]
                        pe.wait_ge(a_out, ONE + NJ * g + n)
                        if kind == "t":
                            pe.wait_ge(xs_rdy, ONE + g + 1)
                            for j in range(TG):
                                last = pe.transpose(out[:, j * P:(j + 1) * P], xs[:, j, m * P:(m + 1) * P], k.ident[:])
                        elif kind == "q":
                            pe.wait_ge(a_out, ONE + NJ * g + 2 + 1)
                            for c in range(DC):
                                last = pe.matmul(out[:], wq[:, c, m * P:(m + 1) * P], xt[:, c, :],
                                                 start=(c == 0), stop=(c == DC - 1))
                        elif kind == "k":
                            if m == 0:
                                ctx_landed(pe, g, par)
                            for c in range(2):
                                last = pe.matmul(out[:], wk[:, c, m * P:(m + 1) * P], ct[par][:, c, :],
                                                 start=(c == 0), stop=(c == 1))
                        else:
                            for c in range(2):
                                last = pe.matmul(out[:], ct[par][:, c, m * T:(m + 1) * T], wv[:, c, :],
                                                 start=(c == 0), stop=(c == 1))
                        last.then_inc(a_done, 1)

                def ctx_landed(pe, g, par):
                    pe.wait_ge(c_in[par], DMA + 8 * (g - par) + 16)

                def out_rows(s):
                    pe.wait_ge(ot_rdy, ONE + s + 1)
                    pe.wait_ge(h_rdy, ONE + s)
                    for m in range(IC):
                        last = pe.matmul(bank_o[:, 0:D], ot[:, m, :], wo[:, m, :], start=(m == 0), stop=(m == IC - 1))
                    last.then_inc(o_done, 1)

                def slot(g, par, b, fill, first):
                    s = g * TG + b
                    pe.wait_ge(a_out, ONE + NJ * (g + 1) + 1)
                    pe.wait_ge(e_rdy, ONE + s)
                    for m in range(IC):
                        for r in range(2):
                            last = pe.matmul(bank_s[r][:, m * T:(m + 1) * T],
                                             qt[par][r * DH:(r + 1) * DH, m, b * T:(b + 1) * T],
                                             kt[par][r * DH:(r + 1) * DH, m, b * T:(b + 1) * T],
                                             start=True, stop=True)
                    last.then_inc(s_done, 1)
                    fill()
                    pe.wait_ge(t_out, ONE + 2 * s)
                    for r in range(2):
                        pe.wait_ge(n_rdy, ONE + 2 * s + r + 1)
                        for m in range(IC):
                            last = pe.transpose(bank_t[r][:, m * T:(m + 1) * T], prob[:, r * IC + m, :], k.ident[:])
                        last.then_inc(t_done, 1)
                    if not first:
                        out_rows(s - 1)
                    pe.wait_ge(t_out, ONE + 2 * s + 2)
                    pe.wait_ge(ot_rdy, ONE + s)
                    for m in range(IC):
                        for r in range(2):
                            h = 2 * m + r
                            last = pe.matmul(bank_v[r * DH:(r + 1) * DH, m * T:(m + 1) * T],
                                             vv[par][:, b, h * DH:(h + 1) * DH], prob_t[:, r * IC + m, :],
                                             start=True, stop=True)
                    last.then_inc(v_done, 1)

                pe.wait_ge(w_in, DMA + 48)
                pe.wait_ge(wo_in, DMA + 16)
                groups(pe, slot, part)
                out_rows(B - 1)

            @block.scalar
            def _(act):
                begin(act, e_rdy, t_out)
                def slot(g, par, b, fill, first):
                    s = g * TG + b
                    act.wait_ge(nb_rdy, ONE + s + 1)
                    act.wait_ge(t_done, ONE + 2 * s)
                    act.wait_ge(rden_rdy, ONE + s)
                    for r in range(2):
                        for m in range(IC):
                            h = r * IC + m
                            last = act.activation(prob[:, h, :], bank_s[r][:, m * T:(m + 1) * T], ACT.Exp,
                                                  bias=nbias[:, h:h + 1], scale=SCALE, accum_out=den[:, h:h + 1])
                    last.then_inc(e_rdy, 1)
                    act.wait_ge(v_done, ONE + s)
                    for r in range(2):
                        act.wait_ge(t_done, ONE + 2 * s + r + 1)
                        act.activation(prob_t[:, r * IC:(r + 1) * IC, :],
                                       bank_t[r][:].rearrange("p (m t) -> p m t", m=IC), ACT.Copy).then_inc(t_out, 1)

                groups(act, slot, lambda g, par, q: None)

            @block.gpsimd
            def _(pool):
                begin(pool, xs_rdy, xb_rdy, ve_rdy, rs_rdy)
                def stage(g):
                    pool.tensor_copy(xs[:], grouped(rows(k.x, g))).then_inc(xs_rdy, 1)
                    pool.tensor_tensor(grouped(rows(k.x, g)), grouped(rows(k.x, g)),
                                       k.bout[:, None, :].to_broadcast([P, TG, D]), ALU.add).then_inc(xb_rdy, 1)

                def rstd(g):
                    pool.wait_ge(mv_rdy, ONE + g + 1)
                    apart(pool, k.past_pool)
                    pool.tensor_scalar(ve[:], mv[:, :, 1], EPS, None, ALU.add).then_inc(ve_rdy, 1)
                    pool.wait_ge(ve_rdy, ONE + g + 1)
                    pool.tensor_tensor(rs[:], ve[:], k.mhalf[:], ALU.pow).then_inc(rs_rdy, 1)

                stage(0)
                pool.wait_ge(a_done, ONE + 2)
                stage(1)
                with pool.Fori(0, NG - 2) as g:
                    pool.wait_ge(a_done, ONE + NJ * (g + 1) + 2)
                    stage(g + 2)
                    rstd(g)
                rstd(NG - 2)
                rstd(NG - 1)

            @block.vector
            def _(dve):
                begin(dve, a_out, top_rdy, nb_rdy, rden_rdy, n_rdy, h_rdy, stat_rdy, mv_rdy, x2_rdy, ot_rdy)
                dve.sem_inc(a_out, 1)

                def part(g, par, q):
                    for n in PARTS[q]:
                        kind, m = JOBS[n]
                        dve.wait_ge(a_done, ONE + NJ * g + n + 1)
                        out = {"t": xt, "q": qt[par], "k": kt[par], "v": vv[par]}[kind]
                        dve.tensor_copy(out[:, m, :], bank_a[n % 2][:]).then_inc(a_out, 1)

                def finish(g, b):
                    s = g * TG + b
                    dve.wait_ge(o_done, ONE + s + 1)
                    dve.wait_ge(xb_rdy, ONE + g + 1)
                    row = k.x[:, bass.ds(s * D, D)]
                    dve.tensor_tensor(row, bank_o[:, 0:D], row, ALU.add).then_inc(h_rdy, 1)
                    dve.wait_ge(h_rdy, ONE + s + 1)
                    apart(dve, k.past_dve)
                    dve.bn_stats(stat[:, b, :], row).then_inc(stat_rdy, 1)
                    dve.wait_ge(stat_rdy, ONE + s + 1)
                    apart(dve, k.past_dve)
                    last = dve.bn_aggr(mv[:, b, :], stat[:, b, :])
                    if b == TG - 1:
                        last.then_inc(mv_rdy, 1)

                def normed(g):
                    dve.wait_ge(rs_rdy, ONE + g + 1)
                    for j in range(TG):
                        last = dve.tensor_scalar(rows(k.x, g, j, 1), rows(k.x, g, j, 1), mv[:, j, 0:1],
                                                 rs[:, j:j + 1], ALU.subtract, ALU.mult)
                    last.then_inc(x2_rdy, 1)

                def slot(g, par, b, fill, first):
                    s = g * TG + b
                    dve.wait_ge(s_done, ONE + s + 1)
                    for r in range(2):
                        last = dve.tensor_reduce(top[:, r * IC:(r + 1) * IC],
                                                 bank_s[r][:].rearrange("p (m t) -> p m t", m=IC), AX.X, ALU.max)
                    last.then_inc(top_rdy, 1)
                    dve.wait_ge(top_rdy, ONE + s + 1)
                    dve.wait_ge(e_rdy, ONE + s)
                    dve.tensor_scalar(nbias[:], top[:], -SCALE, None, ALU.mult).then_inc(nb_rdy, 1)
                    if b == 0:
                        dve.wait_ge(v_done, ONE + s)
                    fill()
                    dve.wait_ge(e_rdy, ONE + s + 1)
                    dve.reciprocal(rden[:], den[:]).then_inc(rden_rdy, 1)
                    dve.wait_ge(rden_rdy, ONE + s + 1)
                    for r in range(2):
                        part_ = prob[:, r * IC:(r + 1) * IC, :]
                        dve.tensor_tensor(part_, part_, rden[:, r * IC:(r + 1) * IC, None].to_broadcast([P, IC, T]),
                                          ALU.mult).then_inc(n_rdy, 1)
                    if not first:
                        finish(g - 1, TG - 1) if b == 0 else finish(g, b - 1)
                        if b == 0:
                            normed(g - 1)
                    dve.wait_ge(v_done, ONE + s + 1)
                    dve.tensor_copy(ot[:], bank_v[:].rearrange("p (m t) -> p m t", m=IC)).then_inc(ot_rdy, 1)

                groups(dve, slot, part)
                finish(NG - 1, TG - 1)
                normed(NG - 1)


def router_stage(nc, k, dram):
    with ExitStack() as ctx:
        p = Parts(nc, ctx, "r_")
        xs, xt = p.sb("xs", [P, TG, D]), p.sb("xt", [P, DC, GW])
        sqr = p.sb("sqr", [P, TG, D])
        ssq, nrm, rn = p.sb("ssq", [P, TG]), p.sb("nrm", [P, TG]), p.sb("rn", [P, TG])
        half = p.sb("half", [P, TG])
        sc = p.sb("sc", [P, TG, G + E])
        gtop, gidx, gsel = p.sb("gtop", [P, TG, 8]), p.sb("gidx", [P, TG, 8], U32), p.sb("gsel", [P, TG, NTOP])
        geq, gmask, gpen = p.sb("geq", [P, TG, G, NTOP]), p.sb("gmask", [P, TG, G]), p.sb("gpen", [P, TG, G])
        es = p.sb("es", [P, TG, E])
        etop, eidx, esel = p.sb("etop", [P, TG, 8]), p.sb("eidx", [P, TG, 8], U32), p.sb("esel", [P, TG, K])
        dif, ex = p.sb("dif", [P, TG, K]), p.sb("ex", [P, TG, K])
        esum, er = p.sb("esum", [P, TG]), p.sb("er", [P, TG])
        hot, hit = p.sb("hot", [P, TG, K, E]), p.sb("hit", [P, TG, K, E])
        mask, sofar = p.sb("mask", [P, TG, E]), p.sb("sofar", [P, TG, E])
        pos, kept, posc = p.sb("pos", [P, TG, K]), p.sb("kept", [P, TG, K]), p.sb("posc", [P, TG, K])
        base = p.sb("base", [P, TG, K])
        far, slot_i = p.sb("far", [P, TG, K]), p.sb("slot_i", [P, TG, K], I32)
        blank = p.sb("blank", [P, SLOTS // P], I32)
        bank_t = [p.bank(f"t{i}") for i in range(2)]
        bank_s, bank_p = p.bank("s"), p.bank("p")
        t_done, xt_rdy, sc_done, p_done = p.sem("t_done"), p.sem("xt"), p.sem("sc_done"), p.sem("p_done")
        ssq_rdy, nrm_rdy, ex_rdy = p.sem("ssq"), p.sem("nrm"), p.sem("ex")
        step, mask_rdy, pos_rdy, slot_rdy = p.sem("step"), p.sem("mask"), p.sem("pos"), p.sem("slot")
        xs_rdy, posc_rdy, hand_rdy = p.sem("xs"), p.sem("posc"), p.sem("hand")
        scattered, dif_rdy, tok_rdy = p.sem("scattered"), p.sem("dif"), p.sem("tok")
        blank_rdy, blanked, half_rdy = p.sem("blank_rdy"), p.sem("blanked"), p.sem("half")
        STEPS = 29

        with nc.Block() as block:
            @block.sync
            def _(sp):
                begin(sp, dma=(blanked,))
                sp.wait_ge(blank_rdy, ONE + 1)
                sp.dma_start(k.slot_tok.rearrange("(p n) a -> p (n a)", p=P), blank[:]).then_inc(blanked, 16)
                sp.wait_ge(blanked, DMA + 16)

            @block.tensor
            def _(pe):
                begin(pe, t_done, sc_done, p_done)
                with pe.Fori(0, NG) as g:
                    for c in range(DC):
                        pe.wait_ge(xs_rdy, ONE + g + 1)
                        pe.wait_ge(xt_rdy, ONE + DC * g)
                        for j in range(TG):
                            last = pe.transpose(bank_t[c][:, j * P:(j + 1) * P], xs[:, j, c * P:(c + 1) * P], k.ident[:])
                        last.then_inc(t_done, 1)
                    pe.wait_ge(xt_rdy, ONE + DC * (g + 1))
                    pe.wait_ge(pos_rdy, ONE + g)
                    for j in range(TG):
                        for c in range(DC):
                            last = pe.matmul(bank_s[:, j * (G + E):(j + 1) * (G + E)], xt[:, c, j * T:(j + 1) * T],
                                             k.cent[:, c, :], start=(c == 0), stop=(c == DC - 1))
                    last.then_inc(sc_done, 1)
                    pe.wait_ge(mask_rdy, ONE + g + 1)
                    pe.matmul(bank_p[:, 0:TG * E], k.before[:], mask[:].rearrange("p t e -> p (t e)"),
                              start=True, stop=False)
                    pe.matmul(bank_p[:, 0:TG * E], k.ones[:], sofar[:].rearrange("p t e -> p (t e)"),
                              start=False, stop=True).then_inc(p_done, 1)

            @block.scalar
            def _(act):
                begin(act, xt_rdy, ssq_rdy, ex_rdy)
                with act.Fori(0, NG) as g:
                    for c in range(DC):
                        act.wait_ge(t_done, ONE + DC * g + c + 1)
                        act.wait_ge(sc_done, ONE + g)
                        act.activation(xt[:, c, :], bank_t[c][:], ACT.Copy).then_inc(xt_rdy, 1)
                    act.wait_ge(xs_rdy, ONE + g + 1)
                    act.wait_ge(nrm_rdy, ONE + g)
                    for j in range(TG):
                        last = act.activation(sqr[:, j, :], xs[:, j, :], ACT.Square, accum_out=ssq[:, j:j + 1])
                    last.then_inc(ssq_rdy, 1)
                    act.wait_ge(dif_rdy, ONE + g + 1)
                    act.activation(ex[:], dif[:], ACT.Exp).then_inc(ex_rdy, 1)

            @block.gpsimd
            def _(pool):
                begin(pool, blank_rdy, half_rdy, xs_rdy, nrm_rdy, tok_rdy)
                pool.memset(blank[:], 0).then_inc(blank_rdy, 1)
                pool.memset(half[:], 0.5).then_inc(half_rdy, 1)
                pool.wait_ge(half_rdy, ONE + 1)
                pool.tensor_copy(xs[:], grouped(rows(k.x, 0))).then_inc(xs_rdy, 1)

                def scatter(g, more):
                    pool.wait_ge(ssq_rdy, ONE + g + 1)
                    pool.wait_ge(step, ONE + STEPS * g)
                    pool.tensor_tensor(nrm[:], ssq[:], half[:], ALU.pow).then_inc(nrm_rdy, 1)
                    if more:
                        pool.wait_ge(t_done, ONE + DC * (g + 1))
                        pool.tensor_copy(xs[:], grouped(rows(k.x, g + 1))).then_inc(xs_rdy, 1)
                    pool.wait_ge(slot_rdy, ONE + g + 1)
                    pool.wait_ge(tok_rdy, ONE + g)
                    pool.wait_ge(blanked, DMA + 16)
                    apart(pool, k.past_pool)
                    for j in range(TG):
                        for q in range(K):
                            pool.indirect_dma_start(
                                k.slot_tok, bass.IndirectOffsetOnAxis(ap=slot_i[:, j, q:q + 1], axis=0),
                                k.tok[:, j:j + 1], None, bounds_check=SLOTS - 1, oob_is_err=False)\
                                .then_inc(scattered, 16)
                    pool.wait_ge(scattered, 16 * TG * K * (g + 1))
                    apart(pool, k.past_pool)
                    pool.tensor_scalar(k.tok[:], k.tok[:], float(GW), None, ALU.add).then_inc(tok_rdy, 1)

                with pool.Fori(0, NG - 1) as g:
                    scatter(g, True)
                scatter(NG - 1, False)

            @block.vector
            def _(dve):
                begin(dve, step, mask_rdy, pos_rdy, slot_rdy, posc_rdy, dif_rdy)
                with dve.Fori(0, NG) as g:
                    done = [0]

                    def then(ins):
                        done[0] += 1
                        ins.then_inc(step, 1)
                        dve.wait_ge(step, ONE + STEPS * g + done[0])

                    io_g = k.iota_e[:, None, 0:G, None]
                    dve.wait_ge(nrm_rdy, ONE + g + 1)
                    then(dve.tensor_scalar(rn[:], nrm[:], 1e-12, None, ALU.max))
                    then(dve.reciprocal(rn[:], rn[:]))
                    dve.wait_ge(sc_done, ONE + g + 1)
                    then(dve.tensor_tensor(sc[:], bank_s[:, 0:TG * (G + E)].rearrange("p (t e) -> p t e", t=TG),
                                           rn[:, :, None].to_broadcast([P, TG, G + E]), ALU.mult))
                    apart(dve, k.past_dve)
                    for j in range(TG):
                        last = dve.max(gtop[:, j, :], sc[:, j, 0:G])
                    then(last)
                    apart(dve, k.past_dve)
                    for j in range(TG):
                        last = dve.max_index(gidx[:, j, :], gtop[:, j, :], sc[:, j, 0:G])
                    then(last)
                    then(dve.tensor_copy(gsel[:], gidx[:, :, 0:NTOP]))
                    then(dve.tensor_tensor(geq[:], io_g.to_broadcast([P, TG, G, NTOP]),
                                           gsel[:, :, None, :].to_broadcast([P, TG, G, NTOP]), ALU.is_equal))
                    then(dve.tensor_reduce(gmask[:], geq[:], AX.X, ALU.add))
                    then(dve.tensor_scalar(gpen[:], gmask[:], -1.0, NEG, ALU.add, ALU.mult))
                    then(dve.tensor_tensor(es[:], sc[:, :, G:], k.ebias[:, None, :].to_broadcast([P, TG, E]), ALU.add))
                    for j in range(TG):
                        last = dve.tensor_tensor(es[:, j, :].rearrange("p (g e) -> p g e", g=G),
                                                 es[:, j, :].rearrange("p (g e) -> p g e", g=G),
                                                 gmask[:, j, :, None].to_broadcast([P, G, EG]), ALU.mult)
                    then(last)
                    for j in range(TG):
                        last = dve.tensor_tensor(es[:, j, :].rearrange("p (g e) -> p g e", g=G),
                                                 es[:, j, :].rearrange("p (g e) -> p g e", g=G),
                                                 gpen[:, j, :, None].to_broadcast([P, G, EG]), ALU.add)
                    then(last)
                    apart(dve, k.past_dve)
                    for j in range(TG):
                        last = dve.max(etop[:, j, :], es[:, j, :])
                    then(last)
                    dve.wait_ge(ex_rdy, ONE + g)
                    dve.tensor_tensor(dif[:], etop[:, :, 0:K], etop[:, :, 0:1].to_broadcast([P, TG, K]),
                                      ALU.subtract).then_inc(dif_rdy, 1)
                    for j in range(TG):
                        last = dve.max_index(eidx[:, j, :], etop[:, j, :], es[:, j, :])
                    then(last)
                    then(dve.tensor_copy(esel[:], eidx[:, :, 0:K]))
                    for j in range(TG):
                        last = dve.tensor_tensor(hot[:, j, :, :], k.iota_e[:, None, :].to_broadcast([P, K, E]),
                                                 esel[:, j, :, None].to_broadcast([P, K, E]), ALU.is_equal)
                    then(last)
                    dve.wait_ge(p_done, ONE + g)
                    then(dve.tensor_reduce(mask[:], hot[:].rearrange("p t q e -> p t e q"), AX.X, ALU.add))
                    then(dve.tensor_copy(sofar[:, 0, :], k.count[:]))
                    for j in range(1, TG):
                        then(dve.tensor_tensor(sofar[:, j, :], sofar[:, j - 1, :], mask[:, j - 1, :], ALU.add))
                    dve.tensor_tensor(k.count[:], sofar[:, TG - 1, :], mask[:, TG - 1, :], ALU.add)\
                       .then_inc(mask_rdy, 1)
                    then(dve.tensor_scalar(base[:], esel[:], float(CAP), None, ALU.mult))
                    dve.wait_ge(ex_rdy, ONE + g + 1)
                    then(dve.tensor_reduce(esum[:], ex[:], AX.X, ALU.add))
                    then(dve.reciprocal(er[:], esum[:]))
                    then(dve.tensor_tensor(dif[:], ex[:], er[:, :, None].to_broadcast([P, TG, K]), ALU.mult))
                    dve.wait_ge(p_done, ONE + g + 1)
                    for j in range(TG):
                        last = dve.tensor_tensor(hit[:, j, :, :], hot[:, j, :, :],
                                                 bank_p[:, None, j * E:(j + 1) * E].to_broadcast([P, K, E]), ALU.mult)
                    last.then_inc(pos_rdy, 1)
                    dve.wait_ge(pos_rdy, ONE + g + 1)
                    then(dve.tensor_reduce(pos[:], hit[:], AX.X, ALU.add))
                    then(dve.tensor_scalar(kept[:], pos[:], float(CAP), None, ALU.is_lt))
                    gates = k.gate[:, bass.ds(g * TG * K, TG * K)].rearrange("p (t q) -> p t q", t=TG)
                    dve.tensor_tensor(gates, dif[:], kept[:], ALU.mult)
                    then(dve.tensor_scalar(far[:], kept[:], -1.0, -float(FAR), ALU.add, ALU.mult))
                    then(dve.tensor_tensor(far[:], far[:], pos[:], ALU.add))
                    dve.wait_ge(tok_rdy, ONE + g)
                    dve.tensor_tensor(slot_i[:], far[:], base[:], ALU.add).then_inc(slot_rdy, 1)
                    dve.tensor_scalar(posc[:], pos[:], float(CAP - 1), None, ALU.min).then_inc(posc_rdy, 1)
                    dve.wait_ge(posc_rdy, ONE + g + 1)
                    dve.tensor_tensor(k.slot[:, bass.ds(g * TG * K, TG * K)].rearrange("p (t q) -> p t q", t=TG),
                                      posc[:], base[:], ALU.add).then_inc(hand_rdy, 1)
                    assert done[0] == STEPS, done[0]


def expert_stage(nc, k, dram):
    with ExitStack() as ctx:
        p = Parts(nc, ctx, "e_")
        wg = [p.sb(f"wg{i}", [P, DC, HID]) for i in range(2)]
        wu = [p.sb(f"wu{i}", [P, DC, HID]) for i in range(2)]
        wd = [p.sb(f"wd{i}", [P, HC, D]) for i in range(2)]
        tok = [p.sb(f"tok{i}", [P, ST], I32) for i in range(2)]
        xg = [p.sb(f"xg{i}", [P, ST, D]) for i in range(2)]
        xt = p.sb("xt", [P, DC, 512])
        sg = [p.sb(f"sg{i}", [P, 512]) for i in range(2)]
        ht = [p.sb(f"ht{i}", [P, HC, 512]) for i in range(2)]
        out = [p.sb(f"out{i}", [P, ST, D]) for i in range(2)]
        bank_t = [p.bank(f"t{i}") for i in range(2)]
        bank_g = [p.bank(f"g{i}") for i in range(2)]
        bank_u = [p.bank(f"u{i}") for i in range(2)]
        bank_d = [p.bank(f"d{i}") for i in range(2)]
        w_in = [p.sem(f"w_in{i}") for i in range(2)]
        tok_in = [p.sem(f"tok_in{i}") for i in range(2)]
        x_in = [p.sem(f"x_in{i}") for i in range(2)]
        t_done, xt_rdy, g_done, u_done = p.sem("t_done"), p.sem("xt"), p.sem("g_done"), p.sem("u_done")
        sg_rdy, h_rdy, d_done, out_rdy = p.sem("sg"), p.sem("h"), p.sem("d_done"), p.sem("out")
        stored = [p.sem(f"stored{i}") for i in range(2)]

        SETS = [(0, 4), (4, 4), (8, 2)]
        NS = len(SETS)
        PAIRS = ST // 2
        NE2 = E // 2
        gate_d = dram["eg"].rearrange("e (c p) n -> p e c n", p=P)
        up_d = dram["eu"].rearrange("e (c p) n -> p e c n", p=P)
        down_d = dram["ed"].rearrange("e (c p) n -> p e c n", p=P)
        tok_d = k.slot_tok.rearrange("(e p n) a -> p e (n a)", e=E, p=P)
        out_d = k.out_d.rearrange("(e p n) d -> p e (n d)", e=E, p=P)

        WS = 3
        down_before = [sum(n // 2 for _, n in SETS[:s]) for s in range(NS + 1)]

        def sets(i):
            return [(NS * a + s, a, first, n) for a in range(2) for s, (first, n) in enumerate(SETS)]

        with nc.Block() as block:
            @block.sync
            def _(sp):
                begin(sp, dma=(*w_in, *stored,))
                def load(e, a):
                    def one(d):
                        return d[:, bass.ds(e, 1), :, :].rearrange("p a c n -> p (a c) n")
                    for dst, src in ((wg, gate_d), (wu, up_d), (wd, down_d)):
                        sp.dma_start(dst[a][:], one(src)).then_inc(w_in[a], 16)

                def store(i, a):
                    sp.wait_ge(out_rdy, ONE + 2 * PAIRS * i + PAIRS * (a + 1) + 1)
                    sp.dma_start(out_d[:, bass.ds(2 * i + a, 1), :].rearrange("p a n -> p (a n)"),
                                 out[a][:].rearrange("p n d -> p (n d)")).then_inc(stored[a], 16)

                load(0, 0)
                load(1, 1)
                with sp.Fori(0, NE2 - 1) as i:
                    for a in range(2):
                        sp.wait_ge(d_done, ONE + 2 * PAIRS * i + PAIRS * (a + 1) + 1)
                        load(2 * i + 2 + a, a)
                        store(i, a)
                for a in range(2):
                    store(NE2 - 1, a)
                for a in range(2):
                    sp.wait_ge(stored[a], DMA + 16 * NE2)

            @block.gpsimd
            def _(pool):
                def gather(i, a, first):
                    if not first:
                        pool.wait_ge(t_done, ONE + DC * NS * (2 * i - 1 + a))
                    pool.dma_start(tok[a][:], tok_d[:, bass.ds(2 * i + a, 1), :].rearrange("p a n -> p (a n)"))\
                        .then_inc(tok_in[a], 16)
                    pool.wait_ge(tok_in[a], 16 * (i + 1))
                    apart(pool, k.past_pool)
                    for n in range(ST):
                        pool.indirect_dma_start(xg[a][:, n, :], None, k.x2_d,
                                                bass.IndirectOffsetOnAxis(ap=tok[a][:, n:n + 1], axis=0))\
                            .then_inc(x_in[a], 16)

                for a in range(2):
                    gather(0, a, True)
                with pool.Fori(1, NE2) as i:
                    for a in range(2):
                        gather(i, a, False)

            @block.tensor
            def _(pe):
                begin(pe, t_done, g_done, u_done, d_done)
                pe.sem_inc(d_done, 1)

                def turn(i, q, a, first, n):
                    if first == 0:
                        pe.wait_ge(x_in[a], 16 * ST * (i + 1))
                    pe.wait_ge(xt_rdy, ONE + DC * (2 * NS * i + q))
                    for c in range(DC):
                        for j in range(n):
                            last = pe.transpose(bank_t[c][:, j * P:(j + 1) * P],
                                                xg[a][:, first + j, c * P:(c + 1) * P], k.ident[:])
                        last.then_inc(t_done, 1)

                def up(i, q, a, first, n):
                    if first == 0:
                        pe.wait_ge(w_in[a], DMA + 16 * WS * (i + 1))
                    pe.wait_ge(xt_rdy, ONE + DC * (2 * NS * i + q + 1))
                    for m in range(HC):
                        job = HC * (2 * NS * i + q) + m
                        for w, bank, used, done in ((wg, bank_g, sg_rdy, g_done), (wu, bank_u, h_rdy, u_done)):
                            pe.wait_ge(used, ONE + job)
                            for c in range(DC):
                                last = pe.matmul(bank[m % 2][:, 0:n * P], w[a][:, c, m * P:(m + 1) * P],
                                                 xt[:, c, 0:n * P], start=(c == 0), stop=(c == DC - 1))
                            last.then_inc(done, 1)

                def down(i, q, a, first, n):
                    pe.wait_ge(h_rdy, ONE + HC * (2 * NS * i + q + 1) + 1)
                    for j in range(0, n, 2):
                        job = 2 * PAIRS * i + PAIRS * a + (first + j) // 2
                        pe.wait_ge(out_rdy, ONE + job)
                        for t in range(2):
                            for c in range(HC):
                                last = pe.matmul(bank_d[((first + j) // 2 + PAIRS * a) % 2][:, t * D:(t + 1) * D],
                                                 ht[q % 2][:, c, (j + t) * P:(j + t + 1) * P], wd[a][:, c, :],
                                                 start=(c == 0), stop=(c == HC - 1))
                        last.then_inc(d_done, 1)

                with pe.Fori(0, NE2) as i:
                    every = sets(i)
                    turn(i, *every[0])
                    for q, s in enumerate(every):
                        up(i, *s)
                        if q + 1 < len(every):
                            turn(i, *every[q + 1])
                        if q:
                            down(i, *every[q - 1])
                    down(i, *every[-1])

            @block.scalar
            def _(act):
                begin(act, xt_rdy, sg_rdy)
                act.sem_inc(sg_rdy, 1)

                def turned(i, q, a, first, n):
                    act.wait_ge(u_done, ONE + HC * (2 * NS * i + q))
                    for c in range(DC):
                        act.wait_ge(t_done, ONE + DC * (2 * NS * i + q) + c + 1)
                        act.activation(xt[:, c, 0:n * P], bank_t[c][:, 0:n * P], ACT.Copy).then_inc(xt_rdy, 1)

                def gate(i, q, a, first, n):
                    for m in range(HC):
                        job = HC * (2 * NS * i + q) + m
                        act.wait_ge(g_done, ONE + job + 1)
                        act.wait_ge(h_rdy, ONE + job)
                        act.activation(sg[m % 2][:, 0:n * P], bank_g[m % 2][:, 0:n * P], ACT.Silu).then_inc(sg_rdy, 1)

                with act.Fori(0, NE2) as i:
                    every = sets(i)
                    turned(i, *every[0])
                    for q, s in enumerate(every):
                        gate(i, *s)
                        if q + 1 < len(every):
                            turned(i, *every[q + 1])

            @block.vector
            def _(dve):
                begin(dve, h_rdy, out_rdy)
                dve.sem_inc(h_rdy, 1)
                dve.sem_inc(out_rdy, 1)

                def hidden(i, q, a, first, n):
                    before = PAIRS * ((q - 2) // NS) + down_before[(q - 2) % NS + 1]
                    dve.wait_ge(d_done, ONE + 2 * PAIRS * i + before + 1)
                    for m in range(HC):
                        job = HC * (2 * NS * i + q) + m
                        dve.wait_ge(sg_rdy, ONE + job + 2)
                        dve.wait_ge(u_done, ONE + job + 1)
                        dve.tensor_tensor(ht[q % 2][:, m, 0:n * P], sg[m % 2][:, 0:n * P], bank_u[m % 2][:, 0:n * P],
                                          ALU.mult).then_inc(h_rdy, 1)

                def copied(i, q, a, first, n):
                    if first == 0:
                        dve.wait_ge(stored[a], DMA + 16 * i)
                    for j in range(0, n, 2):
                        t = first + j
                        dve.wait_ge(d_done, ONE + 2 * PAIRS * i + PAIRS * a + t // 2 + 2)
                        dve.tensor_copy(out[a][:, t:t + 2, :],
                                        bank_d[(t // 2 + PAIRS * a) % 2][:].rearrange("p (t d) -> p t d", t=2))\
                           .then_inc(out_rdy, 1)

                with dve.Fori(0, NE2) as i:
                    every = sets(i)
                    for q, s in enumerate(every):
                        hidden(i, *s)
                        if q:
                            copied(i, *every[q - 1])
                    copied(i, *every[-1])


def combine_stage(nc, k, dram):
    with ExitStack() as ctx:
        p = Parts(nc, ctx, "f_")
        wg, wu, wd = p.sb("wg", [P, DC, HID]), p.sb("wu", [P, DC, HID]), p.sb("wd", [P, HC, D])
        idx = [p.sb(f"idx{i}", [P, TG, K], I32) for i in range(2)]
        row = [p.sb(f"row{i}", [P, TG, K, D]) for i in range(2)]
        res = [p.sb(f"res{i}", [P, TG, D]) for i in range(2)]
        xs, xt = p.sb("xs", [P, TG, D]), p.sb("xt", [P, DC, GW])
        sg, ht = [p.sb(f"sg{i}", [P, GW]) for i in range(2)], p.sb("ht", [P, HC, GW])
        stat, mv = p.sb("stat", [P, TG, 6]), p.sb("mv", [P, TG, 2])
        ve, rs = p.sb("ve", [P, TG]), p.sb("rs", [P, TG])
        bank_t = [p.bank(f"t{i}") for i in range(2)]
        bank_g = [p.bank(f"g{i}") for i in range(2)]
        bank_u = [p.bank(f"u{i}") for i in range(2)]
        bank_d = [p.bank(f"d{i}") for i in range(2)]
        w_in, xs_rdy, idx_rdy = p.sem("w_in"), p.sem("xs"), p.sem("idx")
        row_in = [p.sem(f"row_in{i}") for i in range(2)]
        t_done, xt_rdy, g_done, u_done = p.sem("t_done"), p.sem("xt"), p.sem("g_done"), p.sem("u_done")
        sg_rdy, h_rdy, d_done, sum_rdy = p.sem("sg"), p.sem("h"), p.sem("d_done"), p.sem("sum")
        add_rdy, stat_rdy, mv_rdy, ve_rdy = p.sem("add"), p.sem("stat"), p.sem("mv"), p.sem("ve")
        rs_rdy, res_rdy = p.sem("rs"), p.sem("res")
        stored = [p.sem(f"stored{i}") for i in range(2)]
        out_d = dram["out"].rearrange("b t d -> t b d")

        with nc.Block() as block:
            @block.sync
            def _(sp):
                begin(sp, dma=(w_in, *stored,))
                sp.dma_start(wg[:], dram["sg"].rearrange("(c p) n -> p c n", p=P)).then_inc(w_in, 16)
                sp.dma_start(wu[:], dram["su"].rearrange("(c p) n -> p c n", p=P)).then_inc(w_in, 16)
                sp.dma_start(wd[:], dram["sd"].rearrange("(c p) n -> p c n", p=P)).then_inc(w_in, 16)
                with sp.Fori(0, NG // 2) as i:
                    for a in range(2):
                        g = 2 * i + a
                        sp.wait_ge(res_rdy, ONE + g + 1)
                        sp.dma_start(out_d[:, bass.ds(g * TG, TG), :], res[a][:]).then_inc(stored[a], 16)
                for a in range(2):
                    sp.wait_ge(stored[a], DMA + 16 * (NG // 2))

            @block.gpsimd
            def _(pool):
                begin(pool, xs_rdy, idx_rdy, ve_rdy, rs_rdy)
                def fetch(g, i, a, first=False):
                    pool.wait_ge(t_done, ONE + DC * g)
                    pool.tensor_copy(xs[:], grouped(rows(k.x, g))).then_inc(xs_rdy, 1)
                    if not first:
                        pool.wait_ge(row_in[a], 16 * TG * K * i)
                    pool.tensor_copy(idx[a][:].rearrange("p t q -> p (t q)"),
                                     k.slot[:, bass.ds(g * TG * K, TG * K)]).then_inc(idx_rdy, 1)
                    pool.wait_ge(idx_rdy, ONE + g + 1)
                    apart(pool, k.past_pool)
                    for j in range(TG):
                        for q in range(K):
                            pool.indirect_dma_start(row[a][:, j, q, :], None, k.out_d,
                                                    bass.IndirectOffsetOnAxis(ap=idx[a][:, j, q:q + 1], axis=0))\
                                .then_inc(row_in[a], 16)

                def rstd(g):
                    pool.wait_ge(mv_rdy, ONE + g + 1)
                    apart(pool, k.past_pool)
                    pool.tensor_scalar(ve[:], mv[:, :, 1], EPS, None, ALU.add).then_inc(ve_rdy, 1)
                    pool.wait_ge(ve_rdy, ONE + g + 1)
                    pool.tensor_tensor(rs[:], ve[:], k.mhalf[:], ALU.pow).then_inc(rs_rdy, 1)

                fetch(0, 0, 0, True)
                fetch(1, 0, 1, True)
                rstd(0)
                with pool.Fori(1, NG // 2) as i:
                    fetch(2 * i, i, 0)
                    rstd(2 * i - 1)
                    fetch(2 * i + 1, i, 1)
                    rstd(2 * i)
                rstd(NG - 1)

            @block.tensor
            def _(pe):
                begin(pe, t_done, g_done, u_done, d_done)
                def turn(g):
                    pe.wait_ge(xs_rdy, ONE + g + 1)
                    pe.wait_ge(xt_rdy, ONE + DC * g)
                    for c in range(DC):
                        for j in range(TG):
                            last = pe.transpose(bank_t[c][:, j * P:(j + 1) * P], xs[:, j, c * P:(c + 1) * P], k.ident[:])
                        last.then_inc(t_done, 1)

                def up(g):
                    pe.wait_ge(xt_rdy, ONE + DC * (g + 1))
                    for m in range(HC):
                        job = HC * g + m
                        for w, bank, used, done in ((wg, bank_g, sg_rdy, g_done), (wu, bank_u, h_rdy, u_done)):
                            pe.wait_ge(used, ONE + job)
                            for c in range(DC):
                                last = pe.matmul(bank[m % 2][:], w[:, c, m * P:(m + 1) * P], xt[:, c, :],
                                                 start=(c == 0), stop=(c == DC - 1))
                            last.then_inc(done, 1)

                def down(g):
                    pe.wait_ge(h_rdy, ONE + HC * (g + 1) + 1)
                    pe.wait_ge(sum_rdy, ONE + 2 * g)
                    for h in range(2):
                        for t in range(2):
                            for c in range(HC):
                                last = pe.matmul(bank_d[h][:, t * D:(t + 1) * D],
                                                 ht[:, c, (2 * h + t) * T:(2 * h + t + 1) * T], wd[:, c, :],
                                                 start=(c == 0), stop=(c == HC - 1))
                        last.then_inc(d_done, 1)

                turn(0)
                pe.wait_ge(w_in, DMA + 48)
                with pe.Fori(0, NG - 1) as g:
                    up(g)
                    turn(g + 1)
                    down(g)
                up(NG - 1)
                down(NG - 1)

            @block.scalar
            def _(act):
                begin(act, xt_rdy, sg_rdy)
                act.sem_inc(sg_rdy, 1)

                def turned(g):
                    act.wait_ge(u_done, ONE + HC * g)
                    for c in range(DC):
                        act.wait_ge(t_done, ONE + DC * g + c + 1)
                        act.activation(xt[:, c, :], bank_t[c][:], ACT.Copy).then_inc(xt_rdy, 1)

                def gate(g):
                    for m in range(HC):
                        act.wait_ge(g_done, ONE + HC * g + m + 1)
                        act.wait_ge(h_rdy, ONE + HC * g + m)
                        act.activation(sg[m % 2][:], bank_g[m % 2][:], ACT.Silu).then_inc(sg_rdy, 1)

                turned(0)
                with act.Fori(0, NG - 1) as g:
                    gate(g)
                    turned(g + 1)
                gate(NG - 1)

            @block.vector
            def _(dve):
                begin(dve, h_rdy, sum_rdy, add_rdy, stat_rdy, mv_rdy, res_rdy)
                dve.sem_inc(h_rdy, 1)
                ADDS = TG * K

                with dve.Fori(0, NG // 2) as i:
                    for a in range(2):
                        g = 2 * i + a
                        dve.wait_ge(d_done, ONE + 2 * g)
                        for m in range(HC):
                            dve.wait_ge(sg_rdy, ONE + HC * g + m + 2)
                            dve.wait_ge(u_done, ONE + HC * g + m + 1)
                            dve.tensor_tensor(ht[:, m, :], sg[m % 2][:], bank_u[m % 2][:], ALU.mult).then_inc(h_rdy, 1)
                        dve.wait_ge(stored[a], DMA + 16 * i)
                        for h in range(2):
                            dve.wait_ge(d_done, ONE + 2 * g + h + 1)
                            dve.tensor_tensor(res[a][:, 2 * h:2 * h + 2, :],
                                              bank_d[h][:].rearrange("p (t d) -> p t d", t=2),
                                              grouped(rows(k.x, g, 2 * h, 2), 2), ALU.add).then_inc(sum_rdy, 1)
                        dve.wait_ge(sum_rdy, ONE + 2 * g + 2)
                        dve.wait_ge(row_in[a], 16 * TG * K * (i + 1))
                        for q in range(K):
                            for j in range(TG):
                                if q:
                                    dve.wait_ge(add_rdy, ONE + ADDS * g + TG * (q - 1) + j + 1)
                                dve.scalar_tensor_tensor(res[a][:, j, :], row[a][:, j, q, :],
                                                         k.gate[:, bass.ds(g * TG * K + j * K + q, 1)],
                                                         res[a][:, j, :], ALU.mult, ALU.add).then_inc(add_rdy, 1)
                        for j in range(TG):
                            dve.wait_ge(add_rdy, ONE + ADDS * g + TG * (K - 1) + j + 1)
                            apart(dve, k.past_dve)
                            dve.bn_stats(stat[:, j, :], res[a][:, j, :]).then_inc(stat_rdy, 1)
                        for j in range(TG):
                            dve.wait_ge(stat_rdy, ONE + TG * g + j + 1)
                            apart(dve, k.past_dve)
                            last = dve.bn_aggr(mv[:, j, :], stat[:, j, :])
                        last.then_inc(mv_rdy, 1)
                        dve.wait_ge(rs_rdy, ONE + g + 1)
                        for j in range(TG):
                            last = dve.tensor_scalar(res[a][:, j, :], res[a][:, j, :], mv[:, j, 0:1], rs[:, j:j + 1],
                                                     ALU.subtract, ALU.mult)
                        last.then_inc(res_rdy, 1)


class Kept:
    pass


def build(nc, dram):
    with ExitStack() as ctx:
        def sb(name, shape, dt=F32):
            return ctx.enter_context(nc.sbuf_tensor(name, shape, dt))

        k = Kept()
        k.x = sb("x", [P, B * D])
        k.ident, k.before, k.ones = sb("ident", [P, P]), sb("before", [P, P]), sb("ones", [P, P])
        k.mhalf = sb("mhalf", [P, TG])
        k.td, k.tf, k.gam, k.bet = (sb(n, [P, DC]) for n in ("td", "tf", "gam", "bet"))
        k.decay, k.keep = sb("decay", [P, DC, T]), sb("keep", [P, GW])
        k.wkv_in = sb("wkv_in", [P, DC, GW + 1])
        k.bout, k.ebias = sb("bout", [P, D]), sb("ebias", [P, E])
        k.cent, k.iota_e = sb("cent", [P, DC, G + E]), sb("iota_e", [P, E])
        k.tok, k.count = sb("tok", [P, TG], I32), sb("count", [P, E])
        k.gate, k.slot = sb("gate", [P, B * K]), sb("slot", [P, B * K], I32)
        k.past_dve, k.past_pool = (ctx.enter_context(nc.semaphore(n)) for n in ("past_dve", "past_pool"))
        k.x2_d = nc.dram_tensor("x2_rows", [B * T, D], F32).ap()
        k.out_d = nc.dram_tensor("expert_rows", [SLOTS, D], F32).ap()
        k.slot_tok = nc.dram_tensor("slot_token", [SLOTS, 1], I32).ap()
        setup_stage(nc, k, dram)
        mixer_stage(nc, k, dram)
        attention_stage(nc, k, dram)
        router_stage(nc, k, dram)
        expert_stage(nc, k, dram)
        combine_stage(nc, k, dram)


_AS_THEY_ARE = {
    "x": "x", "td": "L0_attn_time_decay", "tf": "L0_attn_time_first", "gam": "L0_attn_ln_gamma",
    "bet": "L0_attn_ln_beta", "wq": "L0_xattn_Wq", "wxk": "L0_xattn_Wk", "wxv": "L0_xattn_Wv",
    "wout": "L0_xattn_Wout", "bout": "L0_xattn_bout", "gcen": "L0_ffn_group_centroids",
    "ecen": "L0_ffn_expert_centroids", "ebias": "L0_ffn_bias", "eg": "L0_ffn_wg", "eu": "L0_ffn_wu",
    "ed": "L0_ffn_wd", "sg": "L0_ffn_sg", "su": "L0_ffn_su", "sd": "L0_ffn_sd",
}
_TRANSPOSED = {"wk": "L0_attn_Wk", "wv": "L0_attn_Wv", "wr": "L0_attn_Wr", "wo": "L0_attn_Wo"}


def kernel(**inputs):
    import numpy as np
    import concourse.bacc as bacc
    from concourse.bass_utils import run_bass_kernel_spmd

    arrays = {n: np.ascontiguousarray(inputs[key]) for n, key in _AS_THEY_ARE.items()}
    arrays.update({n: np.ascontiguousarray(np.transpose(inputs[key])) for n, key in _TRANSPOSED.items()})
    context = np.asarray(inputs["ctx_768"])
    arrays["ctx"] = np.ascontiguousarray(np.transpose(context, (2, 0, 1)).reshape(CD, B * T))

    nc = bacc.Bacc("TRN2", target_bir_lowering=False, num_devices=1)
    dram = {n: nc.dram_tensor(f"in_{n}", a.shape, mybir.dt.from_np(a.dtype), kind="ExternalInput").ap()
            for n, a in arrays.items()}
    dram["out"] = nc.dram_tensor("out_rows", (B, T, D), F32, kind="ExternalOutput").ap()
    build(nc, dram)
    result = run_bass_kernel_spmd(nc, [{f"in_{n}": a for n, a in arrays.items()}], core_ids=[0])
    return result.results[0]["out_rows"]
```

```python
from contextlib import ExitStack

import concourse.bass as bass
from concourse import mybir

F32 = mybir.dt.float32
F32R = mybir.dt.float32r
I32 = mybir.dt.int32
U32 = mybir.dt.uint32
ALU = mybir.AluOpType
ACT = mybir.ActivationFunctionType
AX = mybir.AxisListType

P = 128
B, T, D = 64, 128, 256
TG = 4
NG = B // TG
GW = TG * T
GX = TG * D
DC = D // P
CD, CC = 192, 96
HEADS, DH = 8, 64
INNER = HEADS * DH
IC = INNER // P
HID = 512
HC = HID // P
E, G, K = 32, 8, 4
EG = E // G
NTOP = G // 2
CAP = int(B * T / E * K * 1.25)
TI, RT = 4, 112
SETW = TI * RT
NSET = -(-CAP // SETW)
ES = NSET * SETW
SLOTS = E * ES
FAR = 4 * SLOTS
EPS = 1e-5
SCALE = DH ** -0.5
NEG = 1e9


def rows(x, g, j=0, n=TG):
    return x[:, bass.ds(g * GX + j * D, n * D)]


def grouped(ap, n=TG):
    return ap.rearrange("p (t d) -> p t d", t=n)


def apart(eng, past):
    eng.sem_inc(past, 1)


ONE = 1
DMA = 16


def begin(eng, *counts, dma=()):
    for c in counts:
        eng.sem_inc(c, ONE)
    for c in dma:
        eng.sem_inc(c, DMA)


class Parts:

    def __init__(self, nc, ctx, tag):
        self.nc, self.ctx, self.tag = nc, ctx, tag

    def sb(self, name, shape, dt=F32):
        return self.ctx.enter_context(self.nc.sbuf_tensor(self.tag + name, shape, dt))

    def bank(self, name):
        return self.ctx.enter_context(self.nc.psum_tensor(self.tag + name, [P, 512], F32))

    def sem(self, name):
        return self.ctx.enter_context(self.nc.semaphore(self.tag + name))


def setup_stage(nc, k, dram):
    with ExitStack() as ctx:
        p = Parts(nc, ctx, "c_")
        td, tf = p.sb("td", [P, DC]), p.sb("tf", [P, DC])
        zero, ones = p.sb("zero", [P, T]), p.sb("ones", [P, T])
        cen, sq = p.sb("cen", [G + E, D]), p.sb("sq", [G + E, D])
        nrm = p.sb("nrm", [G + E, 4])
        half = p.sb("half", [P, 1])
        tp = p.bank("tp")
        vec_in, cen_in = p.sem("vec_in"), p.sem("cen_in")
        fill, ident, sig, tri = p.sem("fill"), p.sem("ident"), p.sem("sig"), p.sem("tri")
        table, cent, root, cen_t = p.sem("table"), p.sem("cent"), p.sem("root"), p.sem("cen_t")
        iot, squared = p.sem("iot"), p.sem("squared")

        with nc.Block() as block:
            @block.sync
            def _(sp):
                with nc.allow_non_contiguous_dma(reason="short vectors"):
                    for dst, src in ((td, dram["td"]), (tf, dram["tf"]), (k.gam, dram["gam"]), (k.bet, dram["bet"])):
                        sp.dma_start(dst[:], src.rearrange("(c p) -> p c", p=P)).then_inc(vec_in, 16)
                sp.dma_start(cen[0:G, :], dram["gcen"]).then_inc(cen_in, 16)
                sp.dma_start(cen[G:G + E, :], dram["ecen"]).then_inc(cen_in, 16)
                sp.dma_start(k.ebias[:], dram["ebias"].rearrange("(a e) -> a e", a=1).to_broadcast([P, E])).then_inc(vec_in, 16)
                sp.dma_start(k.bout[:], dram["bout"].rearrange("(a e) -> a e", a=1).to_broadcast([P, D])).then_inc(vec_in, 16)
                sp.wait_ge(vec_in, 96)

            @block.gpsimd
            def _(pool):
                pool.memset(k.ident[:], 0.0).then_inc(fill, 1)
                pool.memset(k.before[:], 1.0).then_inc(fill, 1)
                pool.memset(k.ones[:], 1.0).then_inc(fill, 1)
                pool.memset(k.mhalf[:], -0.5).then_inc(fill, 1)
                pool.memset(half[:], 0.5).then_inc(fill, 1)
                pool.memset(k.keep[:], 1.0).then_inc(fill, 1)
                pool.wait_ge(fill, 6)
                pool.affine_select(out=k.ident[:], in_=k.ident[:], compare_op=ALU.not_equal, fill=1.0, base=0,
                                   pattern=[[-1, P]], channel_multiplier=1).then_inc(ident, 1)
                pool.affine_select(out=k.before[:], in_=k.before[:], compare_op=ALU.is_gt, fill=0.0, base=0,
                                   pattern=[[1, P]], channel_multiplier=-1).then_inc(tri, 1)
                first = k.keep[:].rearrange("p (b t) -> p b t", b=TG)[:, :, 0:1]
                pool.memset(first, 0.0).then_inc(tri, 1)
                pool.iota(k.iota_e[:], pattern=[[1, E]], base=0, channel_multiplier=0,
                          allow_small_or_imprecise_dtypes=True).then_inc(iot, 1)
                pool.iota(k.tok[:], pattern=[[T, TG]], base=0, channel_multiplier=1).then_inc(iot, 1)
                pool.wait_ge(cent, 1)
                pool.tensor_tensor(nrm[:, 1:2], nrm[:, 0:1], half[0:G + E, :], ALU.pow).then_inc(root, 1)

            @block.scalar
            def _(act):
                act.wait_ge(vec_in, 96)
                act.activation(k.td[:], td[:], ACT.Sigmoid).then_inc(sig, 1)
                act.activation(k.tf[:], tf[:], ACT.Sigmoid).then_inc(sig, 1)

            @block.vector
            def _(dve):
                dve.memset(zero[:], 0.0).then_inc(table, 1)
                dve.memset(ones[:], 1.0).then_inc(table, 1)
                dve.memset(k.count[:], 0.0).then_inc(table, 1)
                dve.memset(k.wkv_in[:], 0.0).then_inc(table, 1)
                dve.wait_ge(table, 2)
                dve.wait_ge(sig, 2)
                for c in range(DC):
                    dve.tensor_scalar(k.decay[:, c, :], ones[:], k.td[:, c:c + 1], None, ALU.mult).then_inc(table, 1)
                    dve.wait_ge(table, 5 + 3 * c)
                    dve.tensor_tensor_scan(k.decay[:, c, :], k.decay[:, c, :], zero[:], 1.0, ALU.mult, ALU.add).then_inc(table, 1)
                    dve.wait_ge(table, 6 + 3 * c)
                    dve.memset(k.decay[:, c, T - 1:T], 0.0).then_inc(table, 1)
                dve.wait_ge(cen_in, 32)
                dve.tensor_tensor(sq[:], cen[:], cen[:], ALU.mult).then_inc(squared, 1)
                dve.wait_ge(squared, 1)
                dve.tensor_reduce(nrm[:, 0:1], sq[:], AX.X, ALU.add).then_inc(cent, 1)
                dve.wait_ge(root, 1)
                dve.tensor_scalar(nrm[:, 2:3], nrm[:, 1:2], 1e-12, None, ALU.max).then_inc(cent, 1)
                dve.wait_ge(cent, 2)
                dve.reciprocal(nrm[:, 3:4], nrm[:, 2:3]).then_inc(cent, 1)
                dve.wait_ge(cent, 3)
                dve.tensor_scalar(cen[:], cen[:], nrm[:, 3:4], None, ALU.mult).then_inc(cent, 1)
                dve.wait_ge(cen_t, 1)
                dve.tensor_copy(k.cent[:], tp[:, 0:DC * (G + E)].rearrange("p (c e) -> p c e", c=DC)).then_inc(cent, 1)

            @block.tensor
            def _(pe):
                pe.wait_ge(ident, 1)
                pe.wait_ge(cent, 4)
                for c in range(DC):
                    last = pe.transpose(tp[:, c * (G + E):(c + 1) * (G + E)], cen[:, c * P:(c + 1) * P],
                                        k.ident[0:G + E, 0:G + E])
                last.then_inc(cen_t, 1)


def mixer_stage(nc, k, dram):
    with ExitStack() as ctx:
        p = Parts(nc, ctx, "m_")
        w = {n: p.sb("w" + n, [P, DC, D]) for n in "kvro"}
        xn, xnt = p.sb("xn", [P, TG, D]), p.sb("xnt", [P, DC, GW])
        sr, kv = p.sb("sr", [P, DC, GW]), p.sb("kv", [P, DC, GW])
        kc = p.sb("kc", [P, DC, GW])
        run, y = p.sb("run", [P, DC, GW]), p.sb("y", [P, DC, GW])
        stat, stat2 = p.sb("stat", [P, TG, 6]), p.sb("stat2", [P, TG, 6])
        mv, mv2 = p.sb("mv", [P, TG, 2]), p.sb("mv2", [P, TG, 2])
        ve, ve2 = p.sb("ve", [P, TG]), p.sb("ve2", [P, TG])
        rs, rs2 = p.sb("rs", [P, TG]), p.sb("rs2", [P, TG])
        bank_t, bank_o = p.bank("t"), p.bank("o")
        bank = [{n: p.bank(f"{n}{c}") for n in "kvr"} for c in range(DC)]
        w_in, x_in = p.sem("w_in"), p.sem("x_in")
        stat_rdy, mv_rdy, ve_rdy, rs_rdy = p.sem("stat"), p.sem("mv"), p.sem("ve"), p.sem("rs")
        xn_rdy, t_done, xnt_rdy = p.sem("xn"), p.sem("t_done"), p.sem("xnt")
        kvr_done, kv_rdy, sr_rdy = p.sem("kvr"), p.sem("kv"), p.sem("sr")
        w_rdy, run_rdy, wkv_rdy, y_rdy = p.sem("w"), p.sem("run"), p.sem("wkv"), p.sem("y")
        o_done, h_rdy, stat2_rdy, mv2_rdy = p.sem("o_done"), p.sem("h"), p.sem("stat2"), p.sem("mv2")
        ve2_rdy, rs2_rdy, x1_rdy, kc_rdy = p.sem("ve2"), p.sem("rs2"), p.sem("x1"), p.sem("kc")

        with nc.Block() as block:
            @block.sync
            def _(sp):
                begin(sp, dma=(x_in, w_in,))
                sp.dma_start(grouped(rows(k.x, 0)), dram["x"].rearrange("b t d -> t b d")[:, 0:TG, :]).then_inc(x_in, 16)
                for n in "kvro":
                    sp.dma_start(w[n][:], dram["w" + n].rearrange("(c p) n -> p c n", p=P)).then_inc(w_in, 16)
                with sp.Fori(1, NG) as g:
                    sp.wait_ge(x_in, DMA + 16 * g)
                    sp.dma_start(grouped(rows(k.x, g)),
                                 dram["x"].rearrange("b t d -> t b d")[:, bass.ds(g * TG, TG), :]).then_inc(x_in, 16)

            @block.tensor
            def _(pe):
                begin(pe, t_done, kvr_done, o_done)
                def turn(g, c):
                    if c == 0:
                        pe.wait_ge(xn_rdy, ONE + g + 1)
                    pe.wait_ge(xnt_rdy, ONE + DC * g + c)
                    for j in range(TG):
                        last = pe.transpose(bank_t[:, j * P:(j + 1) * P], xn[:, j, c * P:(c + 1) * P], k.ident[:])
                    last.then_inc(t_done, 1)

                def project(g):
                    pe.wait_ge(xnt_rdy, ONE + DC * (g + 1))
                    pe.wait_ge(kv_rdy, ONE + DC * g)
                    pe.wait_ge(sr_rdy, ONE + DC * g)
                    for c in range(DC):
                        for n in "kvr":
                            for q in range(DC):
                                last = pe.matmul(bank[c][n][:], w[n][:, q, c * P:(c + 1) * P], xnt[:, q, :],
                                                 start=(q == 0), stop=(q == DC - 1))
                            last.then_inc(kvr_done, 1)

                def mix(g, h):
                    pe.wait_ge(y_rdy, ONE + DC * (g + 1))
                    pe.wait_ge(h_rdy, ONE + 2 * g + h)
                    for j in range(2 * h, 2 * h + 2):
                        for q in range(DC):
                            last = pe.matmul(bank_o[:, (j % 2) * D:(j % 2 + 1) * D], y[:, q, j * T:(j + 1) * T],
                                             w["o"][:, q, :], start=(q == 0), stop=(q == DC - 1))
                    last.then_inc(o_done, 1)

                turn(0, 0)
                turn(0, 1)
                pe.wait_ge(w_in, DMA + 64)
                project(0)
                turn(1, 0)
                turn(1, 1)
                with pe.Fori(1, NG - 1) as g:
                    project(g)
                    turn(g + 1, 0)
                    mix(g - 1, 0)
                    turn(g + 1, 1)
                    mix(g - 1, 1)
                project(NG - 1)
                for g in (NG - 2, NG - 1):
                    mix(g, 0)
                    mix(g, 1)

            @block.scalar
            def _(act):
                begin(act, xnt_rdy, sr_rdy, kc_rdy)
                def norm_out(g):
                    for c in range(DC):
                        act.wait_ge(t_done, ONE + DC * g + c + 1)
                        act.wait_ge(kvr_done, ONE + 3 * DC * g)
                        act.activation(xnt[:, c, :], bank_t[:], ACT.Identity, bias=k.bet[:, c:c + 1],
                                       scale=k.gam[:, c:c + 1]).then_inc(xnt_rdy, 1)

                def gate(g):
                    for c in range(DC):
                        act.wait_ge(kvr_done, ONE + 3 * DC * g + 3 * c + 1)
                        act.wait_ge(kv_rdy, ONE + DC * g + c)
                        act.activation(kc[:, c, :], bank[c]["k"][:], ACT.Copy).then_inc(kc_rdy, 1)
                        act.wait_ge(kvr_done, ONE + 3 * DC * g + 3 * c + 3)
                        act.wait_ge(y_rdy, ONE + DC * g)
                        act.activation(sr[:, c, :], bank[c]["r"][:], ACT.Sigmoid).then_inc(sr_rdy, 1)

                norm_out(0)
                with act.Fori(0, NG - 1) as g:
                    gate(g)
                    norm_out(g + 1)
                gate(NG - 1)

            @block.gpsimd
            def _(pool):
                begin(pool, ve_rdy, rs_rdy, w_rdy, y_rdy, ve2_rdy, rs2_rdy)
                def rstd(g, mv_s, ve_s, rs_s, mv_t, ve_t, rs_t):
                    pool.wait_ge(mv_s, ONE + g + 1)
                    apart(pool, k.past_pool)
                    pool.tensor_scalar(ve_t[:], mv_t[:, :, 1], EPS, None, ALU.add).then_inc(ve_s, 1)
                    pool.wait_ge(ve_s, ONE + g + 1)
                    pool.tensor_tensor(rs_t[:], ve_t[:], k.mhalf[:], ALU.pow).then_inc(rs_s, 1)

                def decayed(g, c):
                    pool.wait_ge(kv_rdy, ONE + DC * g + c + 1)
                    pool.wait_ge(run_rdy, ONE + DC * g)
                    pool.tensor_tensor(k.wkv_in[:, c, 1:GW + 1].rearrange("p (b t) -> p b t", b=TG),
                                       kv[:, c, :].rearrange("p (b t) -> p b t", b=TG),
                                       k.decay[:, c, None, :].to_broadcast([P, TG, T]), ALU.mult).then_inc(w_rdy, 1)

                def gated(g, c):
                    pool.wait_ge(wkv_rdy, ONE + DC * g + c + 1)
                    pool.wait_ge(sr_rdy, ONE + DC * g + c + 1)
                    pool.wait_ge(o_done, ONE + 2 * g)
                    pool.tensor_tensor(y[:, c, :], run[:, c, :], sr[:, c, :], ALU.mult).then_inc(y_rdy, 1)

                def recur(g, more=True):
                    for c in range(DC):
                        decayed(g, c)
                    if more:
                        rstd(g + 1, mv_rdy, ve_rdy, rs_rdy, mv, ve, rs)
                    for c in range(DC):
                        gated(g, c)

                rstd(0, mv_rdy, ve_rdy, rs_rdy, mv, ve, rs)
                recur(0)
                with pool.Fori(1, NG - 1) as g:
                    recur(g)
                    rstd(g - 1, mv2_rdy, ve2_rdy, rs2_rdy, mv2, ve2, rs2)
                recur(NG - 1, False)
                for g in (NG - 2, NG - 1):
                    rstd(g, mv2_rdy, ve2_rdy, rs2_rdy, mv2, ve2, rs2)

            @block.vector
            def _(dve):
                begin(dve, stat_rdy, mv_rdy, xn_rdy, kv_rdy, run_rdy, wkv_rdy, h_rdy, stat2_rdy, mv2_rdy)
                def moments(g, st, mvt, st_s, mv_s):
                    apart(dve, k.past_dve)
                    for j in range(TG):
                        dve.bn_stats(st[:, j, :], rows(k.x, g, j, 1)).then_inc(st_s, 1)
                    for j in range(TG):
                        dve.wait_ge(st_s, ONE + TG * g + j + 1)
                        apart(dve, k.past_dve)
                        last = dve.bn_aggr(mvt[:, j, :], st[:, j, :])
                    last.then_inc(mv_s, 1)

                def moments_in(g):
                    dve.wait_ge(x_in, DMA + 16 * (g + 1))
                    moments(g, stat, mv, stat_rdy, mv_rdy)

                def norm_in(g):
                    dve.wait_ge(rs_rdy, ONE + g + 1)
                    dve.wait_ge(t_done, ONE + DC * g)
                    for j in range(TG):
                        last = dve.tensor_scalar(xn[:, j, :], rows(k.x, g, j, 1), mv[:, j, 0:1], rs[:, j:j + 1],
                                                 ALU.subtract, ALU.mult)
                    last.then_inc(xn_rdy, 1)

                def recur(g, more=True):
                    for c in range(DC):
                        dve.wait_ge(kvr_done, ONE + 3 * DC * g + 3 * c + 2)
                        dve.wait_ge(w_rdy, ONE + DC * g)
                        dve.wait_ge(kc_rdy, ONE + DC * g + c + 1)
                        dve.tensor_tensor(kv[:, c, :], kc[:, c, :], bank[c]["v"][:], ALU.mult).then_inc(kv_rdy, 1)
                    if more:
                        moments_in(g + 1)
                    for c in range(DC):
                        dve.wait_ge(w_rdy, ONE + DC * g + c + 1)
                        dve.wait_ge(y_rdy, ONE + DC * g)
                        dve.tensor_tensor_scan(run[:, c, :], k.keep[:], k.wkv_in[:, c, 0:GW], 0.0,
                                               ALU.mult, ALU.add).then_inc(run_rdy, 1)
                        dve.wait_ge(run_rdy, ONE + DC * g + c + 1)
                        dve.scalar_tensor_tensor(run[:, c, :], kv[:, c, :], k.tf[:, c:c + 1], run[:, c, :],
                                                 ALU.mult, ALU.add).then_inc(wkv_rdy, 1)

                def norm_out(g):
                    for h in range(2):
                        dve.wait_ge(o_done, ONE + 2 * g + h + 1)
                        dve.tensor_tensor(rows(k.x, g, 2 * h, 2), bank_o[:], rows(k.x, g, 2 * h, 2), ALU.add)\
                           .then_inc(h_rdy, 1)
                    dve.wait_ge(h_rdy, ONE + 2 * (g + 1))
                    moments(g, stat2, mv2, stat2_rdy, mv2_rdy)
                    dve.wait_ge(rs2_rdy, ONE + g + 1)
                    for j in range(TG):
                        last = dve.tensor_scalar(rows(k.x, g, j, 1), rows(k.x, g, j, 1), mv2[:, j, 0:1],
                                                 rs2[:, j:j + 1], ALU.subtract, ALU.mult)
                    last.then_inc(x1_rdy, 1)

                moments_in(0)
                norm_in(0)
                recur(0)
                norm_in(1)
                with dve.Fori(1, NG - 1) as g:
                    recur(g)
                    norm_in(g + 1)
                    norm_out(g - 1)
                recur(NG - 1, False)
                norm_out(NG - 2)
                norm_out(NG - 1)

def attention_stage(nc, k, dram):
    with ExitStack() as ctx:
        p = Parts(nc, ctx, "a_")
        wq, wk, wv = p.sb("wq", [P, DC, INNER]), p.sb("wk", [CC, 2, INNER]), p.sb("wv", [CC, 2, INNER])
        wo = p.sb("wo", [P, IC, D])
        xs, xt = p.sb("xs", [P, TG, D]), p.sb("xt", [P, DC, GW])
        ct = [p.sb(f"ct{i}", [CC, 2, GW]) for i in range(2)]
        qt = [p.sb(f"qt{i}", [P, IC, GW]) for i in range(2)]
        kt = [p.sb(f"kt{i}", [P, IC, GW]) for i in range(2)]
        vv = [p.sb(f"vv{i}", [P, TG, INNER]) for i in range(2)]
        prob, prob_t = p.sb("prob", [P, HEADS, T]), p.sb("prob_t", [P, HEADS, T])
        ot = p.sb("ot", [P, IC, T])
        top, nbias = p.sb("top", [P, HEADS]), p.sb("nbias", [P, HEADS])
        den, rden = p.sb("den", [P, HEADS]), p.sb("rden", [P, HEADS])
        stat, mv = p.sb("stat", [P, TG, 6]), p.sb("mv", [P, TG, 2])
        ve, rs = p.sb("ve", [P, TG]), p.sb("rs", [P, TG])
        zero = p.sb("zero", [P, D])
        rxs, rxt = p.sb("rxs", [P, TG, D]), p.sb("rxt", [P, DC, GW])
        sqr = p.sb("sqr", [P, TG, D])
        ssq, nrm, rn = p.sb("ssq", [P, TG]), p.sb("nrm", [P, TG]), p.sb("rn", [P, TG])
        r_half = p.sb("half", [P, TG])
        sc = p.sb("sc", [P, TG, G + E])
        gtop, gidx, gsel = p.sb("gtop", [P, TG, 8]), p.sb("gidx", [P, TG, 8], U32), p.sb("gsel", [P, TG, NTOP])
        geq, gmask, gpen = p.sb("geq", [P, TG, G, NTOP]), p.sb("gmask", [P, TG, G]), p.sb("gpen", [P, TG, G])
        es = p.sb("es", [P, TG, E])
        etop, eidx, esel = p.sb("etop", [P, TG, 8]), p.sb("eidx", [P, TG, 8], U32), p.sb("esel", [P, TG, K])
        dif, ex = p.sb("dif", [P, TG, K]), p.sb("ex", [P, TG, K])
        esum, er = p.sb("esum", [P, TG]), p.sb("er", [P, TG])
        hot, hit = p.sb("hot", [P, TG, K, E]), p.sb("hit", [P, TG, K, E])
        mask, sofar = p.sb("mask", [P, TG, E]), p.sb("sofar", [P, TG, E])
        pos, kept, posc = p.sb("pos", [P, TG, K]), p.sb("kept", [P, TG, K]), p.sb("posc", [P, TG, K])
        base = p.sb("base", [P, TG, K])
        far, slot_i = p.sb("far", [P, TG, K]), p.sb("slot_i", [P, TG, K], I32)
        blank = p.sb("blank", [RT, (SLOTS + SETW) // RT], I32)
        zero_rdy, filled = p.sem("zero_rdy"), p.sem("filled")
        bank_a = [p.bank(f"a{i}") for i in range(2)]
        bank_s = [p.bank(f"s{i}") for i in range(2)]
        bank_t = [p.bank(f"t{i}") for i in range(2)]
        bank_v, bank_o = p.bank("v"), p.bank("o")
        w_in, wo_in = p.sem("w_in"), p.sem("wo_in")
        c_in = [p.sem(f"c_in{i}") for i in range(2)]
        a_done, a_out = p.sem("a_done"), p.sem("a_out")
        s_done, top_rdy, nb_rdy, e_rdy = p.sem("s_done"), p.sem("top"), p.sem("nb"), p.sem("e")
        rden_rdy, n_rdy, t_done, t_out = p.sem("rden"), p.sem("n"), p.sem("t_done"), p.sem("t_out")
        v_done, ot_rdy, o_done, h_rdy = p.sem("v_done"), p.sem("ot"), p.sem("o_done"), p.sem("h")
        xb_rdy, stat_rdy, mv_rdy, ve_rdy = p.sem("xb"), p.sem("stat"), p.sem("mv"), p.sem("ve")
        rs_rdy, x2_rdy, x2_out, xs_rdy = p.sem("rs"), p.sem("x2"), p.sem("x2_out"), p.sem("xs")

        rxs_rdy, ssq_rdy, nrm_rdy, ex_rdy = p.sem("rxs"), p.sem("ssq"), p.sem("nrm"), p.sem("ex")
        step, mask_rdy, slot_rdy, dif_rdy = p.sem("step"), p.sem("mask"), p.sem("slot"), p.sem("dif")
        posc_rdy, hand_rdy, scattered, tok_rdy = p.sem("posc"), p.sem("hand"), p.sem("scattered"), p.sem("tok")
        blank_rdy, blanked, half_rdy = p.sem("blank_rdy"), p.sem("blanked"), p.sem("half_rdy")
        CHOSEN, STEPS = 20, 28

        A = [[("t", 0), ("t", 1), ("q", 0), ("q", 1)], [("q", 2), ("q", 3), ("k", 0)],
             [("k", 1), ("k", 2), ("k", 3)], [("v", m) for m in range(TG)]]
        R = [[], [("rt", 0), ("rt", 1)], [("rs", 0)], [("rp", 0)]]
        BOTH = [A[0], A[1] + R[1], R[2] + A[2], A[3] + R[3]]
        assert IC == 4 and TG == 4
        N_A, N_R = sum(map(len, A)), sum(map(len, R))
        NJ = N_A + N_R
        assert N_A % 2 == 0 and N_R % 2 == 0

        def jobs(h):
            if isinstance(h, int):
                return A if h < 2 else R if h >= NG else BOTH
            return BOTH

        def before(h):
            if isinstance(h, int):
                return sum(len(part) for i in range(h) for part in jobs(i))
            return h * NJ - 2 * N_R

        def numbered(h, q):
            first = sum(map(len, jobs(h)[:q]))
            return [(first + i, kind, m) for i, (kind, m) in enumerate(jobs(h)[q])]

        def upto(h, kind, m):
            return [job for part in jobs(h) for job in part].index((kind, m)) + 1

        ctx_d = dram["ctx"].rearrange("(c p) n -> p c n", p=CC)

        def groups(eng, slot, part):
            for q in range(4):
                part(0, 0, q)
            for b in range(TG):
                slot(0, 0, b, lambda b=b: part(1, 1, b), b == 0)
            with eng.Fori(0, (NG - 2) // 2) as i:
                for par in (1, 0):
                    g = 2 * i + (1 if par else 2)
                    for b in range(TG):
                        slot(g, par, b, lambda g=g, par=par, b=b: part(g + 1, 1 - par, b), False)
            for b in range(TG):
                slot(NG - 1, 1, b, lambda b=b: part(NG, 0, b), False)

        with nc.Block() as block:
            @block.sync
            def _(sp):
                begin(sp, dma=(w_in, wo_in, *c_in, x2_out, filled, blanked))
                sp.dma_start(wq[:], dram["wq"].rearrange("(c p) n -> p c n", p=P)).then_inc(w_in, 16)
                sp.dma_start(wk[:], dram["wxk"].rearrange("(c p) n -> p c n", p=CC)).then_inc(w_in, 16)
                sp.dma_start(ct[0][:], ctx_d[:, :, 0:GW]).then_inc(c_in[0], 16)
                sp.dma_start(wv[:], dram["wxv"].rearrange("(c p) n -> p c n", p=CC)).then_inc(w_in, 16)
                sp.dma_start(wo[:], dram["wout"].rearrange("(c p) n -> p c n", p=P)).then_inc(wo_in, 16)
                sp.dma_start(ct[1][:], ctx_d[:, :, GW:2 * GW]).then_inc(c_in[1], 16)

                FILL = SLOTS // NG
                sp.wait_ge(blank_rdy, 1)
                sp.dma_start(k.slot_tok.rearrange("(p n) a -> p (n a)", p=RT), blank[:]).then_inc(blanked, 16)
                sp.wait_ge(zero_rdy, 1)

                def store(g):
                    sp.dma_start(k.out_d[bass.ds(g * FILL, FILL), :].rearrange("(p n) d -> p n d", p=P),
                                 zero[:, None, :].to_broadcast([P, FILL // P, D])).then_inc(filled, 16)
                    sp.wait_ge(x2_rdy, ONE + g + 1)
                    sp.dma_start(k.x2_d[bass.ds(g * GW, GW), :].rearrange("(b t) d -> t b d", b=TG),
                                 grouped(rows(k.x, g))).then_inc(x2_out, 16)

                def turnover(i):
                    for par in range(2):
                        g = 2 * i + par
                        sp.wait_ge(a_done, ONE + before(g + 1))
                        sp.dma_start(ct[par][:], ctx_d[:, :, bass.ds((g + 2) * GW, GW)]).then_inc(c_in[par], 16)
                        store(g)

                turnover(0)
                with sp.Fori(1, (NG - 2) // 2) as i:
                    turnover(i)
                store(NG - 2)
                store(NG - 1)
                sp.wait_ge(x2_out, DMA + 16 * NG)
                sp.wait_ge(filled, DMA + 16 * NG)
                sp.wait_ge(blanked, DMA + 16)

            @block.tensor
            def _(pe):
                begin(pe, a_done, s_done, t_done, v_done, o_done)
                def part(g, par, q):
                    for n, kind, m in numbered(g, q):
                        out = bank_a[n % 2]
                        pe.wait_ge(a_out, ONE + before(g) + n)
                        if kind == "t":
                            pe.wait_ge(xs_rdy, ONE + g + 1)
                            for j in range(TG):
                                last = pe.transpose(out[:, j * P:(j + 1) * P], xs[:, j, m * P:(m + 1) * P], k.ident[:])
                        elif kind == "q":
                            pe.wait_ge(a_out, ONE + before(g) + upto(g, "t", 1) + 1)
                            for c in range(DC):
                                last = pe.matmul(out[:], wq[:, c, m * P:(m + 1) * P], xt[:, c, :],
                                                 start=(c == 0), stop=(c == DC - 1))
                        elif kind == "k":
                            if m == 0:
                                ctx_landed(pe, g, par)
                            for c in range(2):
                                last = pe.matmul(out[:], wk[:, c, m * P:(m + 1) * P], ct[par][:, c, :],
                                                 start=(c == 0), stop=(c == 1))
                        elif kind == "rt":
                            pe.wait_ge(rxs_rdy, ONE + g - 2 + 1)
                            for j in range(TG):
                                last = pe.transpose(out[:, j * P:(j + 1) * P], rxs[:, j, m * P:(m + 1) * P], k.ident[:])
                        elif kind == "rs":
                            pe.wait_ge(a_out, ONE + before(g) + upto(g, "rt", 1) + 1)
                            for j in range(TG):
                                for c in range(DC):
                                    last = pe.matmul(out[:, j * (G + E):(j + 1) * (G + E)], rxt[:, c, j * T:(j + 1) * T],
                                                     k.cent[:, c, :], start=(c == 0), stop=(c == DC - 1))
                        elif kind == "rp":
                            pe.wait_ge(mask_rdy, ONE + g - 2 + 1)
                            pe.matmul(out[:, 0:TG * E], k.before[:], mask[:].rearrange("p t e -> p (t e)"),
                                      start=True, stop=False)
                            last = pe.matmul(out[:, 0:TG * E], k.ones[:], sofar[:].rearrange("p t e -> p (t e)"),
                                             start=False, stop=True)
                        else:
                            for c in range(2):
                                last = pe.matmul(out[:], ct[par][:, c, m * T:(m + 1) * T], wv[:, c, :],
                                                 start=(c == 0), stop=(c == 1))
                        last.then_inc(a_done, 1)

                def ctx_landed(pe, g, par):
                    pe.wait_ge(c_in[par], DMA + 8 * (g - par) + 16)

                def out_rows(s):
                    pe.wait_ge(ot_rdy, ONE + s + 1)
                    pe.wait_ge(h_rdy, ONE + s)
                    for m in range(IC):
                        last = pe.matmul(bank_o[:, 0:D], ot[:, m, :], wo[:, m, :], start=(m == 0), stop=(m == IC - 1))
                    last.then_inc(o_done, 1)

                def slot(g, par, b, fill, first):
                    s = g * TG + b
                    pe.wait_ge(a_out, ONE + before(g + 1) + 1)
                    pe.wait_ge(e_rdy, ONE + s)
                    for m in range(IC):
                        for r in range(2):
                            last = pe.matmul(bank_s[r][:, m * T:(m + 1) * T],
                                             qt[par][r * DH:(r + 1) * DH, m, b * T:(b + 1) * T],
                                             kt[par][r * DH:(r + 1) * DH, m, b * T:(b + 1) * T],
                                             start=True, stop=True)
                    last.then_inc(s_done, 1)
                    fill()
                    pe.wait_ge(t_out, ONE + 2 * s)
                    for r in range(2):
                        pe.wait_ge(n_rdy, ONE + 2 * s + r + 1)
                        for m in range(IC):
                            last = pe.transpose(bank_t[r][:, m * T:(m + 1) * T], prob[:, r * IC + m, :], k.ident[:])
                        last.then_inc(t_done, 1)
                    if not first:
                        out_rows(s - 1)
                    pe.wait_ge(t_out, ONE + 2 * s + 2)
                    pe.wait_ge(ot_rdy, ONE + s)
                    for m in range(IC):
                        for r in range(2):
                            h = 2 * m + r
                            last = pe.matmul(bank_v[r * DH:(r + 1) * DH, m * T:(m + 1) * T],
                                             vv[par][:, b, h * DH:(h + 1) * DH], prob_t[:, r * IC + m, :],
                                             start=True, stop=True)
                    last.then_inc(v_done, 1)

                pe.wait_ge(w_in, DMA + 48)
                pe.wait_ge(wo_in, DMA + 16)
                groups(pe, slot, part)
                out_rows(B - 1)
                for q in range(4):
                    part(NG + 1, 0, q)

            @block.scalar
            def _(act):
                begin(act, e_rdy, t_out, ssq_rdy, ex_rdy)
                def squares(r):
                    act.wait_ge(rxs_rdy, ONE + r + 1)
                    act.wait_ge(nrm_rdy, ONE + r)
                    for j in range(TG):
                        last = act.activation(sqr[:, j, :], rxs[:, j, :], ACT.Square, accum_out=ssq[:, j:j + 1])
                    last.then_inc(ssq_rdy, 1)

                def gate_exp(r):
                    act.wait_ge(dif_rdy, ONE + r + 1)
                    act.activation(ex[:], dif[:], ACT.Exp).then_inc(ex_rdy, 1)

                def slot(g, par, b, fill, first):
                    s = g * TG + b
                    routes = not isinstance(g, int) or g >= 1
                    if b == 3 and routes:
                        gate_exp(g - 1)
                    act.wait_ge(nb_rdy, ONE + s + 1)
                    act.wait_ge(t_done, ONE + 2 * s)
                    act.wait_ge(rden_rdy, ONE + s)
                    for r in range(2):
                        for m in range(IC):
                            h = r * IC + m
                            last = act.activation(prob[:, h, :], bank_s[r][:, m * T:(m + 1) * T], ACT.Exp,
                                                  bias=nbias[:, h:h + 1], scale=SCALE, accum_out=den[:, h:h + 1])
                    last.then_inc(e_rdy, 1)
                    act.wait_ge(v_done, ONE + s)
                    for r in range(2):
                        act.wait_ge(t_done, ONE + 2 * s + r + 1)
                        act.activation(prob_t[:, r * IC:(r + 1) * IC, :],
                                       bank_t[r][:].rearrange("p (m t) -> p m t", m=IC), ACT.Copy).then_inc(t_out, 1)
                    if b == 1 and routes:
                        squares(g - 1)

                groups(act, slot, lambda g, par, q: None)
                squares(NG - 1)
                gate_exp(NG - 1)

            @block.gpsimd
            def _(pool):
                pool.memset(zero[:], 0.0).then_inc(zero_rdy, 1)
                begin(pool, xs_rdy, xb_rdy, ve_rdy, rs_rdy, rxs_rdy, nrm_rdy, tok_rdy)
                pool.memset(blank[:], 0).then_inc(blank_rdy, 1)
                pool.memset(r_half[:], 0.5).then_inc(half_rdy, 1)
                pool.wait_ge(half_rdy, 1)
                def stage(g):
                    pool.tensor_copy(xs[:], grouped(rows(k.x, g))).then_inc(xs_rdy, 1)
                    pool.tensor_tensor(grouped(rows(k.x, g)), grouped(rows(k.x, g)),
                                       k.bout[:, None, :].to_broadcast([P, TG, D]), ALU.add).then_inc(xb_rdy, 1)

                def rstd(g):
                    pool.wait_ge(mv_rdy, ONE + g + 1)
                    apart(pool, k.past_pool)
                    pool.tensor_scalar(ve[:], mv[:, :, 1], EPS, None, ALU.add).then_inc(ve_rdy, 1)
                    pool.wait_ge(ve_rdy, ONE + g + 1)
                    pool.tensor_tensor(rs[:], ve[:], k.mhalf[:], ALU.pow).then_inc(rs_rdy, 1)

                def norms(r, first=False):
                    pool.wait_ge(x2_rdy, ONE + r + 1)
                    if not first:
                        pool.wait_ge(a_done, ONE + before(r + 1) + upto(r + 1, "rt", 1))
                    pool.tensor_copy(rxs[:], grouped(rows(k.x, r))).then_inc(rxs_rdy, 1)
                    pool.wait_ge(ssq_rdy, ONE + r + 1)
                    pool.wait_ge(step, ONE + STEPS * r)
                    pool.tensor_tensor(nrm[:], ssq[:], r_half[:], ALU.pow).then_inc(nrm_rdy, 1)

                def scatter(r):
                    pool.wait_ge(slot_rdy, ONE + r + 1)
                    pool.wait_ge(tok_rdy, ONE + r)
                    pool.wait_ge(blanked, DMA + 16)
                    apart(pool, k.past_pool)
                    for j in range(TG):
                        for q in range(K):
                            pool.indirect_dma_start(
                                k.slot_tok, bass.IndirectOffsetOnAxis(ap=slot_i[:, j, q:q + 1], axis=0),
                                k.tok[:, j:j + 1], None, bounds_check=SLOTS - 1, oob_is_err=False)\
                                .then_inc(scattered, 16)
                    pool.wait_ge(scattered, 16 * TG * K * (r + 1))
                    apart(pool, k.past_pool)
                    pool.tensor_scalar(k.tok[:], k.tok[:], float(GW), None, ALU.add).then_inc(tok_rdy, 1)

                def around(g, scatters=True):
                    pool.wait_ge(a_done, ONE + before(g + 1) + 2)
                    stage(g + 2)
                    if scatters:
                        scatter(g - 2)
                    rstd(g)
                    norms(g, isinstance(g, int) and g == 0)

                stage(0)
                pool.wait_ge(a_done, ONE + 2)
                stage(1)
                around(0, False)
                around(1, False)
                with pool.Fori(2, NG - 2) as g:
                    around(g)
                for g in (NG - 2, NG - 1):
                    scatter(g - 2)
                    rstd(g)
                    norms(g)
                scatter(NG - 2)
                scatter(NG - 1)

            @block.vector
            def _(dve):
                begin(dve, a_out, top_rdy, nb_rdy, rden_rdy, n_rdy, h_rdy, stat_rdy, mv_rdy, x2_rdy, ot_rdy,
                      step, mask_rdy, slot_rdy, posc_rdy, dif_rdy)
                dve.sem_inc(a_out, 1)

                class Steps:
                    def __init__(self, r, done):
                        self.r, self.done = r, done

                    def __call__(self, ins):
                        self.done += 1
                        ins.then_inc(step, 1)
                        dve.wait_ge(step, ONE + STEPS * self.r + self.done)

                def inverse_norms(r):
                    then = Steps(r, 0)
                    dve.wait_ge(nrm_rdy, ONE + r + 1)
                    then(dve.tensor_scalar(rn[:], nrm[:], 1e-12, None, ALU.max))
                    then(dve.reciprocal(rn[:], rn[:]))
                    assert then.done == 2

                def choose(r):
                    then = Steps(r, 2)
                    h = r + 2
                    dve.wait_ge(a_out, ONE + 1 + before(h) + upto(h, "rs", 0))
                    io_g = k.iota_e[:, None, 0:G, None]
                    apart(dve, k.past_dve)
                    for j in range(TG):
                        last = dve.max(gtop[:, j, :], sc[:, j, 0:G])
                    then(last)
                    apart(dve, k.past_dve)
                    for j in range(TG):
                        last = dve.max_index(gidx[:, j, :], gtop[:, j, :], sc[:, j, 0:G])
                    then(last)
                    then(dve.tensor_copy(gsel[:], gidx[:, :, 0:NTOP]))
                    then(dve.tensor_tensor(geq[:], io_g.to_broadcast([P, TG, G, NTOP]),
                                           gsel[:, :, None, :].to_broadcast([P, TG, G, NTOP]), ALU.is_equal))
                    then(dve.tensor_reduce(gmask[:], geq[:], AX.X, ALU.add))
                    then(dve.tensor_scalar(gpen[:], gmask[:], -1.0, NEG, ALU.add, ALU.mult))
                    then(dve.tensor_tensor(es[:], sc[:, :, G:], k.ebias[:, None, :].to_broadcast([P, TG, E]), ALU.add))
                    for j in range(TG):
                        last = dve.tensor_tensor(es[:, j, :].rearrange("p (g e) -> p g e", g=G),
                                                 es[:, j, :].rearrange("p (g e) -> p g e", g=G),
                                                 gmask[:, j, :, None].to_broadcast([P, G, EG]), ALU.mult)
                    then(last)
                    for j in range(TG):
                        last = dve.tensor_tensor(es[:, j, :].rearrange("p (g e) -> p g e", g=G),
                                                 es[:, j, :].rearrange("p (g e) -> p g e", g=G),
                                                 gpen[:, j, :, None].to_broadcast([P, G, EG]), ALU.add)
                    then(last)
                    apart(dve, k.past_dve)
                    for j in range(TG):
                        last = dve.max(etop[:, j, :], es[:, j, :])
                    then(last)
                    dve.wait_ge(ex_rdy, ONE + r)
                    dve.tensor_tensor(dif[:], etop[:, :, 0:K], etop[:, :, 0:1].to_broadcast([P, TG, K]),
                                      ALU.subtract).then_inc(dif_rdy, 1)
                    for j in range(TG):
                        last = dve.max_index(eidx[:, j, :], etop[:, j, :], es[:, j, :])
                    then(last)
                    then(dve.tensor_copy(esel[:], eidx[:, :, 0:K]))
                    for j in range(TG):
                        last = dve.tensor_tensor(hot[:, j, :, :], k.iota_e[:, None, :].to_broadcast([P, K, E]),
                                                 esel[:, j, :, None].to_broadcast([P, K, E]), ALU.is_equal)
                    then(last)
                    then(dve.tensor_reduce(mask[:], hot[:].rearrange("p t q e -> p t e q"), AX.X, ALU.add))
                    then(dve.tensor_copy(sofar[:, 0, :], k.count[:]))
                    for j in range(1, TG):
                        then(dve.tensor_tensor(sofar[:, j, :], sofar[:, j - 1, :], mask[:, j - 1, :], ALU.add))
                    dve.tensor_tensor(k.count[:], sofar[:, TG - 1, :], mask[:, TG - 1, :], ALU.add)\
                       .then_inc(mask_rdy, 1)
                    assert then.done == CHOSEN, then.done

                def place(r):
                    then = Steps(r, CHOSEN)
                    h = r + 2
                    dve.wait_ge(a_out, ONE + 1 + before(h) + upto(h, "rp", 0))
                    then(dve.tensor_scalar(base[:], esel[:], float(ES), None, ALU.mult))
                    dve.wait_ge(ex_rdy, ONE + r + 1)
                    then(dve.tensor_reduce(esum[:], ex[:], AX.X, ALU.add))
                    then(dve.reciprocal(er[:], esum[:]))
                    then(dve.tensor_tensor(dif[:], ex[:], er[:, :, None].to_broadcast([P, TG, K]), ALU.mult))
                    then(dve.tensor_reduce(pos[:], hit[:], AX.X, ALU.add))
                    then(dve.tensor_scalar(kept[:], pos[:], float(CAP), None, ALU.is_lt))
                    gates = k.gate[:, bass.ds(r * TG * K, TG * K)].rearrange("p (t q) -> p t q", t=TG)
                    dve.tensor_tensor(gates, dif[:], kept[:], ALU.mult)
                    then(dve.tensor_scalar(far[:], kept[:], -1.0, -float(FAR), ALU.add, ALU.mult))
                    then(dve.tensor_tensor(far[:], far[:], pos[:], ALU.add))
                    dve.wait_ge(tok_rdy, ONE + r)
                    dve.tensor_tensor(slot_i[:], far[:], base[:], ALU.add).then_inc(slot_rdy, 1)
                    dve.tensor_scalar(posc[:], pos[:], float(CAP - 1), None, ALU.min).then_inc(posc_rdy, 1)
                    dve.wait_ge(posc_rdy, ONE + r + 1)
                    dve.tensor_tensor(k.slot[:, bass.ds(r * TG * K, TG * K)].rearrange("p (t q) -> p t q", t=TG),
                                      posc[:], base[:], ALU.add).then_inc(hand_rdy, 1)
                    assert then.done == STEPS, then.done

                def part(g, par, q):
                    for n, kind, m in numbered(g, q):
                        if kind == "rs":
                            inverse_norms(g - 2)
                        dve.wait_ge(a_done, ONE + before(g) + n + 1)
                        bank = bank_a[n % 2]
                        if kind == "rs":
                            dve.tensor_tensor(sc[:], bank[:, 0:TG * (G + E)].rearrange("p (t e) -> p t e", t=TG),
                                              rn[:, :, None].to_broadcast([P, TG, G + E]), ALU.mult).then_inc(a_out, 1)
                        elif kind == "rp":
                            for j in range(TG):
                                last = dve.tensor_tensor(hit[:, j, :, :], hot[:, j, :, :],
                                                         bank[:, None, j * E:(j + 1) * E].to_broadcast([P, K, E]),
                                                         ALU.mult)
                            last.then_inc(a_out, 1)
                        else:
                            out = {"t": xt, "q": qt[par], "k": kt[par], "v": vv[par], "rt": rxt}[kind]
                            dve.tensor_copy(out[:, m, :], bank[:]).then_inc(a_out, 1)

                def finish(g, b):
                    s = g * TG + b
                    dve.wait_ge(o_done, ONE + s + 1)
                    dve.wait_ge(xb_rdy, ONE + g + 1)
                    row = k.x[:, bass.ds(s * D, D)]
                    dve.tensor_tensor(row, bank_o[:, 0:D], row, ALU.add).then_inc(h_rdy, 1)
                    dve.wait_ge(h_rdy, ONE + s + 1)
                    apart(dve, k.past_dve)
                    dve.bn_stats(stat[:, b, :], row).then_inc(stat_rdy, 1)
                    dve.wait_ge(stat_rdy, ONE + s + 1)
                    apart(dve, k.past_dve)
                    last = dve.bn_aggr(mv[:, b, :], stat[:, b, :])
                    if b == TG - 1:
                        last.then_inc(mv_rdy, 1)

                def normed(g):
                    dve.wait_ge(rs_rdy, ONE + g + 1)
                    for j in range(TG):
                        last = dve.tensor_scalar(rows(k.x, g, j, 1), rows(k.x, g, j, 1), mv[:, j, 0:1],
                                                 rs[:, j:j + 1], ALU.subtract, ALU.mult)
                    last.then_inc(x2_rdy, 1)

                def slot(g, par, b, fill, first):
                    s = g * TG + b
                    dve.wait_ge(s_done, ONE + s + 1)
                    for r in range(2):
                        last = dve.tensor_reduce(top[:, r * IC:(r + 1) * IC],
                                                 bank_s[r][:].rearrange("p (m t) -> p m t", m=IC), AX.X, ALU.max)
                    last.then_inc(top_rdy, 1)
                    dve.wait_ge(top_rdy, ONE + s + 1)
                    dve.wait_ge(e_rdy, ONE + s)
                    dve.tensor_scalar(nbias[:], top[:], -SCALE, None, ALU.mult).then_inc(nb_rdy, 1)
                    if b == 0:
                        dve.wait_ge(v_done, ONE + s)
                    fill()
                    dve.wait_ge(e_rdy, ONE + s + 1)
                    dve.reciprocal(rden[:], den[:]).then_inc(rden_rdy, 1)
                    dve.wait_ge(rden_rdy, ONE + s + 1)
                    for r in range(2):
                        part_ = prob[:, r * IC:(r + 1) * IC, :]
                        dve.tensor_tensor(part_, part_, rden[:, r * IC:(r + 1) * IC, None].to_broadcast([P, IC, T]),
                                          ALU.mult).then_inc(n_rdy, 1)
                    if not first:
                        finish(g - 1, TG - 1) if b == 0 else finish(g, b - 1)
                        if b == 0:
                            normed(g - 1)
                    if not isinstance(g, int) or g >= 1:
                        if b == 2:
                            choose(g - 1)
                        if b == 3:
                            place(g - 1)
                    dve.wait_ge(v_done, ONE + s + 1)
                    dve.tensor_copy(ot[:], bank_v[:].rearrange("p (m t) -> p m t", m=IC)).then_inc(ot_rdy, 1)

                groups(dve, slot, part)
                finish(NG - 1, TG - 1)
                normed(NG - 1)
                part(NG + 1, 0, 1)
                part(NG + 1, 0, 2)
                choose(NG - 1)
                part(NG + 1, 0, 3)
                place(NG - 1)


def plan_stage(nc, k):
    with ExitStack() as ctx:
        p = Parts(nc, ctx, "p_")
        taken, n_items, more = p.sb("taken", [P, E]), p.sb("n_items", [P, E]), p.sb("more", [P, E])
        ones, upto, whole = p.sb("ones", [P, E]), p.sb("upto", [P, E]), p.sb("whole", [P, E])
        item, col, col_i = p.sb("item", [P, 1]), p.sb("col", [P, 4]), p.sb("col_i", [P, 4], I32)
        bank = p.bank("n")
        item_rdy, tot, step, listed, plan_in = (p.sem(n) for n in ("item", "tot", "step", "listed", "plan_in"))

        with nc.Block() as block:
            @block.tensor
            def _(pe):
                pe.matmul(bank[:, 0:E], k.ones[:], k.count[:], start=True, stop=True).then_inc(tot, 1)

            @block.gpsimd
            def _(pool):
                pool.iota(item[:], pattern=[[0, 1]], base=0, channel_multiplier=1,
                          allow_small_or_imprecise_dtypes=True).then_inc(item_rdy, 1)

            @block.vector
            def _(dve):
                done = [0]

                def then(ins):
                    done[0] += 1
                    ins.then_inc(step, 1)
                    dve.wait_ge(step, done[0])

                dve.wait_ge(tot, 1)
                then(dve.tensor_scalar(taken[:], bank[:, 0:E], float(CAP), None, ALU.min))
                then(dve.tensor_scalar(n_items[:], taken[:], 0.0, None, ALU.is_gt))
                for s in range(1, NSET):
                    then(dve.tensor_scalar(more[:], taken[:], float(s * SETW), None, ALU.is_gt))
                    then(dve.tensor_tensor(n_items[:], n_items[:], more[:], ALU.add))
                then(dve.memset(ones[:], 1.0))
                then(dve.tensor_tensor_scan(upto[:], ones[:], n_items[:], 0.0, ALU.mult, ALU.add))
                dve.wait_ge(item_rdy, 1)
                then(dve.tensor_scalar(whole[:], upto[:], item[:, 0:1], None, ALU.is_le))
                then(dve.tensor_reduce(col[:, 0:1], whole[:], AX.X, ALU.add))
                then(dve.tensor_tensor(more[:], n_items[:], whole[:], ALU.mult))
                then(dve.tensor_reduce(col[:, 1:2], more[:], AX.X, ALU.add))
                then(dve.tensor_tensor(col[:, 2:3], item[:], col[:, 1:2], ALU.subtract))
                then(dve.tensor_scalar(col[:, 2:3], col[:, 2:3], float(SETW), None, ALU.mult))
                then(dve.tensor_scalar(col[:, 3:4], col[:, 0:1], float(ES), None, ALU.mult))
                then(dve.tensor_tensor(col[:, 3:4], col[:, 3:4], col[:, 2:3], ALU.add))
                then(dve.tensor_scalar(col_i[:, 0:1], col[:, 3:4], float(SLOTS), None, ALU.min))
                then(dve.tensor_scalar(col_i[:, 1:2], col[:, 0:1], float(E - 1), None, ALU.min))
                then(dve.tensor_copy(col_i[:, 2:3], upto[:, E - 1:E]))
                dve.tensor_copy(col_i[:, 3:4], upto[:, E - 1:E]).then_inc(listed, 1)

            @block.sync
            def _(sp):
                sp.wait_ge(listed, 1)
                sp.dma_start(k.plan_d, col_i[:]).then_inc(plan_in, 16)
                sp.wait_ge(plan_in, 16)
                sp.dma_start(k.plan[:], k.plan_d.rearrange("w f -> (w f)").rearrange("(a n) -> a n", a=1))\
                    .then_inc(plan_in, 16)
                sp.wait_ge(plan_in, 32)


def split_product(pe, out, chunks):
    last = None
    for n, ((lh, ll), (rh, rl)) in enumerate(chunks):
        for t, (a, b) in enumerate(((lh, rh), (lh, rl), (ll, rh))):
            last = pe.matmul(out, a, b, start=(n == 0 and t == 0), stop=(n == len(chunks) - 1 and t == 2))
    return last


def expert_stage(nc, k, dram):
    with ExitStack() as ctx:
        p = Parts(nc, ctx, "e_")
        raw_g, raw_u, raw_d = p.sb("raw_g", [P, DC, HID]), p.sb("raw_u", [P, DC, HID]), p.sb("raw_d", [P, HC, D])
        wg = [[p.sb(f"wg{i}{h}", [P, DC, HID], F32R) for h in "hl"] for i in range(2)]
        wu = [[p.sb(f"wu{i}{h}", [P, DC, HID], F32R) for h in "hl"] for i in range(2)]
        wd = [[p.sb(f"wd{i}{h}", [P, HC, D], F32R) for h in "hl"] for i in range(2)]
        tok = [p.sb(f"tok{i}", [RT, TI], I32) for i in range(2)]
        xg = [p.sb(f"xg{i}", [RT, TI, D]) for i in range(2)]
        xt = [p.sb(f"xt{h}", [P, DC, SETW], F32R) for h in "hl"]
        sg = [p.sb(f"sg{i}", [P, SETW]) for i in range(2)]
        hid = [p.sb(f"hid{i}", [P, SETW]) for i in range(2)]
        ht = [[p.sb(f"ht{i}{h}", [P, HC, SETW], F32R) for h in "hl"] for i in range(2)]
        out = [p.sb(f"out{i}", [RT, TI, D]) for i in range(2)]
        bank_t = [p.bank(f"t{i}") for i in range(2)]
        bank_g = [p.bank(f"g{i}") for i in range(2)]
        bank_u = [p.bank(f"u{i}") for i in range(2)]
        bank_d = [p.bank(f"d{i}") for i in range(2)]
        g_in, u_in, d_in = p.sem("g_in"), p.sem("u_in"), p.sem("d_in")
        tok_in = [p.sem(f"tok_in{i}") for i in range(2)]
        x_in = [p.sem(f"x_in{i}") for i in range(2)]
        stored = [p.sem(f"stored{i}") for i in range(2)]
        t_done, xh_rdy, xl_rdy = p.sem("t_done"), p.sem("xh"), p.sem("xl")
        g_done, u_done, d_done = p.sem("g_done"), p.sem("u_done"), p.sem("d_done")
        sg_rdy, hid_rdy, hh_rdy, hl_rdy = p.sem("sg"), p.sem("hid"), p.sem("hh"), p.sem("hl")
        wh_rdy, wl_rdy, out_rdy = p.sem("wh"), p.sem("wl"), p.sem("out")
        dh_rdy, dl_rdy = p.sem("dh"), p.sem("dl")

        ROUNDS = E * NSET // 2
        NP = TI // 2
        gate_d = dram["eg"].rearrange("e (c p) n -> p e c n", p=P)
        up_d = dram["eu"].rearrange("e (c p) n -> p e c n", p=P)
        down_d = dram["ed"].rearrange("e (c p) n -> p e c n", p=P)
        PIECES = [(raw_g, wg, 0), (raw_g, wg, 1), (raw_u, wu, 0), (raw_u, wu, 1)]
        assert len(PIECES) == HC == 4 and DC == 2

        def items_of(eng):
            return eng.value_load(k.plan[0:1, 2:3], min_val=1, max_val=E * NSET)

        def rounds(eng, first, again, skipped):
            n = items_of(eng)
            first()
            with eng.Fori(1, ROUNDS) as i:
                with eng.If(i * 2 < n):
                    again(i)
                with eng.Else():
                    for c, by, beyond in skipped:
                        eng.wait_ge(c, beyond + by * i)
                        eng.sem_inc(c, by)

        with nc.Block() as block:
            @block.sync
            def _(sp):
                begin(sp, dma=(g_in, u_in, d_in, *stored))

                def load(w):
                    e = sp.value_load(k.plan[0:1, bass.ds(w * 4 + 1, 1)], min_val=0, max_val=E - 1)

                    def one(d):
                        return d[:, bass.ds(e, 1), :, :].rearrange("p a c n -> p (a c) n")
                    later = not isinstance(w, int) or w > 0
                    if later:
                        sp.wait_ge(wl_rdy, ONE + HC * w - 2)
                    sp.dma_start(raw_g[:], one(gate_d)).then_inc(g_in, 16)
                    if later:
                        sp.wait_ge(wl_rdy, ONE + HC * w)
                    sp.dma_start(raw_u[:], one(up_d)).then_inc(u_in, 16)
                    if later:
                        sp.wait_ge(dl_rdy, ONE + HC * w)
                    sp.dma_start(raw_d[:], one(down_d)).then_inc(d_in, 16)

                def store(w, a):
                    start = sp.value_load(k.plan[0:1, bass.ds(w * 4, 1)], min_val=0, max_val=SLOTS)
                    sp.wait_ge(out_rdy, ONE + NP * (w + 1))
                    sp.dma_start(k.out_d[bass.ds(start, SETW), :].rearrange("(p n) d -> p n d", n=TI), out[a][:])\
                        .then_inc(stored[a], 16)

                def first():
                    load(0)
                    load(1)
                    load(2)
                    store(0, 0)

                def again(i):
                    load(2 * i + 1)
                    store(2 * i - 1, 1)
                    load(2 * i + 2)
                    store(2 * i, 0)

                rounds(sp, first, again, [(stored[0], 16, DMA), (stored[1], 16, DMA - 16)])
                n = items_of(sp)
                last = (n + 1) // 2 * 2 - 1
                start = sp.value_load(k.plan[0:1, bass.ds(last * 4, 1)], min_val=0, max_val=SLOTS)
                sp.wait_ge(d_in, DMA + 16 * (last + 2))
                sp.wait_ge(out_rdy, ONE + NP * 2 * ROUNDS)
                sp.dma_start(k.out_d[bass.ds(start, SETW), :].rearrange("(p n) d -> p n d", n=TI), out[1][:])\
                    .then_inc(stored[1], 16)
                for a in range(2):
                    sp.wait_ge(stored[a], DMA + 16 * ROUNDS)

            @block.gpsimd
            def _(pool):
                begin(pool, dl_rdy)

                def gather(w, a, i):
                    start = pool.value_load(k.plan[0:1, bass.ds(w * 4, 1)], min_val=0, max_val=SLOTS)
                    if not isinstance(i, int) or i:
                        pool.wait_ge(t_done, ONE + DC * (w - 1))
                    pool.dma_start(tok[a][:], k.slot_tok[bass.ds(start, SETW), :].rearrange("(p n) a -> p (n a)", n=TI))\
                        .then_inc(tok_in[a], 16)
                    pool.wait_ge(tok_in[a], 16 * (i + 1))
                    apart(pool, k.past_pool)
                    for n in range(TI):
                        pool.indirect_dma_start(xg[a][:, n, :], None, k.x2_d,
                                                bass.IndirectOffsetOnAxis(ap=tok[a][:, n:n + 1], axis=0))\
                            .then_inc(x_in[a], 16)

                def down_low(w, par):
                    if not isinstance(w, int) or w >= 2:
                        pool.wait_ge(d_done, ONE + NP * (w - 1))
                    for m in range(HC):
                        pool.wait_ge(dh_rdy, ONE + HC * w + m + 1)
                        pool.tensor_tensor(wd[par][1][:, m, :], raw_d[:, m, :], wd[par][0][:, m, :].bitcast(F32),
                                           ALU.subtract).then_inc(dl_rdy, 1)

                def first():
                    gather(0, 0, 0)
                    gather(1, 1, 0)
                    down_low(0, 0)
                    gather(2, 0, 1)
                    down_low(1, 1)

                def again(i):
                    gather(2 * i + 1, 1, i)
                    down_low(2 * i, 0)
                    gather(2 * i + 2, 0, i + 1)
                    down_low(2 * i + 1, 1)

                rounds(pool, first, again, [(dl_rdy, 2 * HC, ONE)])

            @block.tensor
            def _(pe):
                begin(pe, t_done, g_done, u_done, d_done)

                def turn(w, a, i):
                    pe.wait_ge(x_in[a], 16 * TI * (i + 1))
                    if not isinstance(w, int) or w:
                        pe.wait_ge(xl_rdy, ONE + DC * w)
                    for c in range(DC):
                        for n in range(TI):
                            last = pe.transpose(bank_t[c][:, n * RT:(n + 1) * RT],
                                                xg[a][:, n, c * P:(c + 1) * P], k.ident[0:RT, 0:RT])
                        last.then_inc(t_done, 1)

                def up(w, a):
                    pe.wait_ge(xl_rdy, ONE + DC * (w + 1))
                    pe.wait_ge(wl_rdy, ONE + HC * (w + 1))
                    for m in range(HC):
                        job = HC * w + m
                        for wt, bank, used, done in ((wg, bank_g, sg_rdy, g_done), (wu, bank_u, hid_rdy, u_done)):
                            if not isinstance(job, int) or job >= 2:
                                pe.wait_ge(used, ONE + job - 1)
                            cols = slice(m * P, (m + 1) * P)
                            split_product(pe, bank[m % 2][:, 0:SETW],
                                          [((wt[a][0][:, c, cols], wt[a][1][:, c, cols]),
                                            (xt[0][:, c, :], xt[1][:, c, :])) for c in range(DC)]).then_inc(done, 1)

                def down(w, a):
                    pe.wait_ge(hl_rdy, ONE + HC * (w + 1))
                    pe.wait_ge(dl_rdy, ONE + HC * (w + 1))
                    for h in range(NP):
                        if not isinstance(w, int) or w:
                            pe.wait_ge(out_rdy, ONE + NP * (w - 1) + h + 1)
                        for t in (2 * h, 2 * h + 1):
                            rows_ = slice(t * RT, (t + 1) * RT)
                            last = split_product(pe, bank_d[h][0:RT, (t % 2) * D:(t % 2 + 1) * D],
                                                 [((ht[a][0][:, c, rows_], ht[a][1][:, c, rows_]),
                                                   (wd[a][0][:, c, :], wd[a][1][:, c, :])) for c in range(HC)])
                        last.then_inc(d_done, 1)

                def first():
                    turn(0, 0, 0)
                    up(0, 0)
                    turn(1, 1, 0)
                    up(1, 1)
                    turn(2, 0, 1)
                    down(0, 0)

                def again(i):
                    up(2 * i, 0)
                    turn(2 * i + 1, 1, i)
                    down(2 * i - 1, 1)
                    up(2 * i + 1, 1)
                    turn(2 * i + 2, 0, i + 1)
                    down(2 * i, 0)

                rounds(pe, first, again, [(t_done, 2 * DC, ONE + DC), (g_done, 2 * HC, ONE), (u_done, 2 * HC, ONE),
                                          (d_done, 2 * NP, ONE - NP)])
                down(2 * ROUNDS - 1, 1)

            @block.scalar
            def _(act):
                begin(act, xh_rdy, sg_rdy, hh_rdy, wh_rdy, dh_rdy)

                def weights_high(w, par, m):
                    raw, high, c = PIECES[m]
                    if m in (0, 2):
                        act.wait_ge(g_in if m == 0 else u_in, DMA + 16 * (w + 1))
                        if not isinstance(w, int) or w >= 2:
                            act.wait_ge(u_done, ONE + HC * (w - 1))
                    act.activation(high[par][0][:, c, :], raw[:, c, :], ACT.Copy).then_inc(wh_rdy, 1)

                def down_high(w, par, m):
                    if m == 0:
                        act.wait_ge(d_in, DMA + 16 * (w + 1))
                        if not isinstance(w, int) or w >= 2:
                            act.wait_ge(d_done, ONE + NP * (w - 1))
                    act.activation(wd[par][0][:, m, :], raw_d[:, m, :], ACT.Copy).then_inc(dh_rdy, 1)

                def turned(w):
                    if not isinstance(w, int) or w:
                        act.wait_ge(u_done, ONE + HC * w)
                    for c in range(DC):
                        act.wait_ge(t_done, ONE + DC * w + c + 1)
                        act.activation(xt[0][:, c, :], bank_t[c][:, 0:SETW], ACT.Copy).then_inc(xh_rdy, 1)

                def hidden_high(w, a, m):
                    act.wait_ge(hid_rdy, ONE + HC * w + m + 1)
                    if m == 0 and (not isinstance(w, int) or w >= 2):
                        act.wait_ge(d_done, ONE + NP * (w - 1))
                    act.activation(ht[a][0][:, m, :], hid[m % 2][:], ACT.Copy).then_inc(hh_rdy, 1)

                def item(w, a):
                    for m in range(HC):
                        job = HC * w + m
                        act.wait_ge(g_done, ONE + job + 1)
                        if not isinstance(job, int) or job >= 2:
                            act.wait_ge(hid_rdy, ONE + job - 1)
                        act.activation(sg[m % 2][:], bank_g[m % 2][:, 0:SETW], ACT.Silu).then_inc(sg_rdy, 1)
                        weights_high(w + 1, 1 - a, m)
                        down_high(w, a, m)
                        if m:
                            hidden_high(w, a, m - 1)
                    hidden_high(w, a, HC - 1)
                    turned(w + 1)

                def first():
                    for m in range(HC):
                        weights_high(0, 0, m)
                    turned(0)
                    item(0, 0)
                    item(1, 1)

                def again(i):
                    item(2 * i, 0)
                    item(2 * i + 1, 1)

                rounds(act, first, again, [(xh_rdy, 2 * DC, ONE + DC), (sg_rdy, 2 * HC, ONE), (hh_rdy, 2 * HC, ONE),
                                           (wh_rdy, 2 * HC, ONE + HC), (dh_rdy, 2 * HC, ONE)])

            @block.vector
            def _(dve):
                begin(dve, xl_rdy, hid_rdy, hl_rdy, wl_rdy, out_rdy)

                def weights_low(w, par, m):
                    raw, parts, c = PIECES[m]
                    dve.wait_ge(wh_rdy, ONE + HC * w + m + 1)
                    dve.tensor_tensor(parts[par][1][:, c, :], raw[:, c, :], parts[par][0][:, c, :].bitcast(F32),
                                      ALU.subtract).then_inc(wl_rdy, 1)

                def turned(w):
                    for c in range(DC):
                        dve.wait_ge(xh_rdy, ONE + DC * w + c + 1)
                        dve.tensor_tensor(xt[1][:, c, :], bank_t[c][:, 0:SETW], xt[0][:, c, :].bitcast(F32),
                                          ALU.subtract).then_inc(xl_rdy, 1)

                def hidden_low(w, a, m):
                    dve.wait_ge(hh_rdy, ONE + HC * w + m + 1)
                    dve.tensor_tensor(ht[a][1][:, m, :], hid[m % 2][:], ht[a][0][:, m, :].bitcast(F32),
                                      ALU.subtract).then_inc(hl_rdy, 1)

                def item(w, a):
                    for m in range(HC):
                        job = HC * w + m
                        dve.wait_ge(sg_rdy, ONE + job + 1)
                        dve.wait_ge(u_done, ONE + job + 1)
                        if not isinstance(job, int) or job >= 2:
                            dve.wait_ge(hl_rdy, ONE + job - 1)
                        dve.tensor_tensor(hid[m % 2][:], sg[m % 2][:], bank_u[m % 2][:, 0:SETW], ALU.mult)\
                           .then_inc(hid_rdy, 1)
                        weights_low(w + 1, 1 - a, m)
                        if m:
                            hidden_low(w, a, m - 1)
                    hidden_low(w, a, HC - 1)
                    turned(w + 1)

                def copied(w, a, i):
                    if not isinstance(i, int) or i:
                        dve.wait_ge(stored[a], DMA + 16 * i)
                    for h in range(NP):
                        dve.wait_ge(d_done, ONE + NP * w + h + 1)
                        dve.tensor_copy(out[a][:, 2 * h:2 * h + 2, :],
                                        bank_d[h][0:RT, :].rearrange("p (t d) -> p t d", t=2)).then_inc(out_rdy, 1)

                def first():
                    for m in range(HC):
                        weights_low(0, 0, m)
                    turned(0)
                    item(0, 0)
                    item(1, 1)
                    copied(0, 0, 0)

                def again(i):
                    item(2 * i, 0)
                    copied(2 * i - 1, 1, i - 1)
                    item(2 * i + 1, 1)
                    copied(2 * i, 0, i)

                rounds(dve, first, again, [(xl_rdy, 2 * DC, ONE + DC), (hid_rdy, 2 * HC, ONE), (hl_rdy, 2 * HC, ONE),
                                           (wl_rdy, 2 * HC, ONE + HC), (out_rdy, 2 * NP, ONE - NP)])
                dve.wait_ge(d_done, ONE + NP * 2 * ROUNDS)
                for h in range(NP):
                    dve.tensor_copy(out[1][:, 2 * h:2 * h + 2, :],
                                    bank_d[h][0:RT, :].rearrange("p (t d) -> p t d", t=2)).then_inc(out_rdy, 1)


def combine_stage(nc, k, dram):
    with ExitStack() as ctx:
        p = Parts(nc, ctx, "f_")
        wg, wu, wd = p.sb("wg", [P, DC, HID]), p.sb("wu", [P, DC, HID]), p.sb("wd", [P, HC, D])
        idx = [p.sb(f"idx{i}", [P, TG, K], I32) for i in range(2)]
        row = [p.sb(f"row{i}", [P, TG, K, D]) for i in range(2)]
        res = [p.sb(f"res{i}", [P, TG, D]) for i in range(2)]
        xs, xt = p.sb("xs", [P, TG, D]), p.sb("xt", [P, DC, GW])
        sg, ht = [p.sb(f"sg{i}", [P, GW]) for i in range(2)], p.sb("ht", [P, HC, GW])
        stat, mv = p.sb("stat", [P, TG, 6]), p.sb("mv", [P, TG, 2])
        ve, rs = p.sb("ve", [P, TG]), p.sb("rs", [P, TG])
        bank_t = [p.bank(f"t{i}") for i in range(2)]
        bank_g = [p.bank(f"g{i}") for i in range(2)]
        bank_u = [p.bank(f"u{i}") for i in range(2)]
        bank_d = [p.bank(f"d{i}") for i in range(2)]
        w_in, xs_rdy, idx_rdy = p.sem("w_in"), p.sem("xs"), p.sem("idx")
        row_in = [p.sem(f"row_in{i}") for i in range(2)]
        t_done, xt_rdy, g_done, u_done = p.sem("t_done"), p.sem("xt"), p.sem("g_done"), p.sem("u_done")
        sg_rdy, h_rdy, d_done, sum_rdy = p.sem("sg"), p.sem("h"), p.sem("d_done"), p.sem("sum")
        add_rdy, stat_rdy, mv_rdy, ve_rdy = p.sem("add"), p.sem("stat"), p.sem("mv"), p.sem("ve")
        rs_rdy, res_rdy = p.sem("rs"), p.sem("res")
        stored = [p.sem(f"stored{i}") for i in range(2)]
        out_d = dram["out"].rearrange("b t d -> t b d")

        with nc.Block() as block:
            @block.sync
            def _(sp):
                begin(sp, dma=(w_in, *stored,))
                sp.dma_start(wg[:], dram["sg"].rearrange("(c p) n -> p c n", p=P)).then_inc(w_in, 16)
                sp.dma_start(wu[:], dram["su"].rearrange("(c p) n -> p c n", p=P)).then_inc(w_in, 16)
                sp.dma_start(wd[:], dram["sd"].rearrange("(c p) n -> p c n", p=P)).then_inc(w_in, 16)
                with sp.Fori(0, NG // 2) as i:
                    for a in range(2):
                        g = 2 * i + a
                        sp.wait_ge(res_rdy, ONE + g + 1)
                        sp.dma_start(out_d[:, bass.ds(g * TG, TG), :], res[a][:]).then_inc(stored[a], 16)
                for a in range(2):
                    sp.wait_ge(stored[a], DMA + 16 * (NG // 2))

            @block.gpsimd
            def _(pool):
                begin(pool, xs_rdy, idx_rdy, ve_rdy, rs_rdy)
                def fetch(g, i, a, first=False):
                    pool.wait_ge(t_done, ONE + DC * g)
                    pool.tensor_copy(xs[:], grouped(rows(k.x, g))).then_inc(xs_rdy, 1)
                    if not first:
                        pool.wait_ge(row_in[a], 16 * TG * K * i)
                    pool.tensor_copy(idx[a][:].rearrange("p t q -> p (t q)"),
                                     k.slot[:, bass.ds(g * TG * K, TG * K)]).then_inc(idx_rdy, 1)
                    pool.wait_ge(idx_rdy, ONE + g + 1)
                    apart(pool, k.past_pool)
                    for j in range(TG):
                        for q in range(K):
                            pool.indirect_dma_start(row[a][:, j, q, :], None, k.out_d[0:SLOTS, :],
                                                    bass.IndirectOffsetOnAxis(ap=idx[a][:, j, q:q + 1], axis=0))\
                                .then_inc(row_in[a], 16)

                def rstd(g):
                    pool.wait_ge(mv_rdy, ONE + g + 1)
                    apart(pool, k.past_pool)
                    pool.tensor_scalar(ve[:], mv[:, :, 1], EPS, None, ALU.add).then_inc(ve_rdy, 1)
                    pool.wait_ge(ve_rdy, ONE + g + 1)
                    pool.tensor_tensor(rs[:], ve[:], k.mhalf[:], ALU.pow).then_inc(rs_rdy, 1)

                fetch(0, 0, 0, True)
                fetch(1, 0, 1, True)
                rstd(0)
                with pool.Fori(1, NG // 2) as i:
                    fetch(2 * i, i, 0)
                    rstd(2 * i - 1)
                    fetch(2 * i + 1, i, 1)
                    rstd(2 * i)
                rstd(NG - 1)

            @block.tensor
            def _(pe):
                begin(pe, t_done, g_done, u_done, d_done)
                def turn(g):
                    pe.wait_ge(xs_rdy, ONE + g + 1)
                    pe.wait_ge(xt_rdy, ONE + DC * g)
                    for c in range(DC):
                        for j in range(TG):
                            last = pe.transpose(bank_t[c][:, j * P:(j + 1) * P], xs[:, j, c * P:(c + 1) * P], k.ident[:])
                        last.then_inc(t_done, 1)

                def up(g):
                    pe.wait_ge(xt_rdy, ONE + DC * (g + 1))
                    for m in range(HC):
                        job = HC * g + m
                        for w, bank, used, done in ((wg, bank_g, sg_rdy, g_done), (wu, bank_u, h_rdy, u_done)):
                            pe.wait_ge(used, ONE + job)
                            for c in range(DC):
                                last = pe.matmul(bank[m % 2][:], w[:, c, m * P:(m + 1) * P], xt[:, c, :],
                                                 start=(c == 0), stop=(c == DC - 1))
                            last.then_inc(done, 1)

                def down(g):
                    pe.wait_ge(h_rdy, ONE + HC * (g + 1) + 1)
                    pe.wait_ge(sum_rdy, ONE + 2 * g)
                    for h in range(2):
                        for t in range(2):
                            for c in range(HC):
                                last = pe.matmul(bank_d[h][:, t * D:(t + 1) * D],
                                                 ht[:, c, (2 * h + t) * T:(2 * h + t + 1) * T], wd[:, c, :],
                                                 start=(c == 0), stop=(c == HC - 1))
                        last.then_inc(d_done, 1)

                turn(0)
                pe.wait_ge(w_in, DMA + 48)
                with pe.Fori(0, NG - 1) as g:
                    up(g)
                    turn(g + 1)
                    down(g)
                up(NG - 1)
                down(NG - 1)

            @block.scalar
            def _(act):
                begin(act, xt_rdy, sg_rdy)
                act.sem_inc(sg_rdy, 1)

                def turned(g):
                    act.wait_ge(u_done, ONE + HC * g)
                    for c in range(DC):
                        act.wait_ge(t_done, ONE + DC * g + c + 1)
                        act.activation(xt[:, c, :], bank_t[c][:], ACT.Copy).then_inc(xt_rdy, 1)

                def gate(g):
                    for m in range(HC):
                        act.wait_ge(g_done, ONE + HC * g + m + 1)
                        act.wait_ge(h_rdy, ONE + HC * g + m)
                        act.activation(sg[m % 2][:], bank_g[m % 2][:], ACT.Silu).then_inc(sg_rdy, 1)

                turned(0)
                with act.Fori(0, NG - 1) as g:
                    gate(g)
                    turned(g + 1)
                gate(NG - 1)

            @block.vector
            def _(dve):
                begin(dve, h_rdy, sum_rdy, add_rdy, stat_rdy, mv_rdy, res_rdy)
                dve.sem_inc(h_rdy, 1)
                ADDS = TG * K

                with dve.Fori(0, NG // 2) as i:
                    for a in range(2):
                        g = 2 * i + a
                        dve.wait_ge(d_done, ONE + 2 * g)
                        for m in range(HC):
                            dve.wait_ge(sg_rdy, ONE + HC * g + m + 2)
                            dve.wait_ge(u_done, ONE + HC * g + m + 1)
                            dve.tensor_tensor(ht[:, m, :], sg[m % 2][:], bank_u[m % 2][:], ALU.mult).then_inc(h_rdy, 1)
                        dve.wait_ge(stored[a], DMA + 16 * i)
                        for h in range(2):
                            dve.wait_ge(d_done, ONE + 2 * g + h + 1)
                            dve.tensor_tensor(res[a][:, 2 * h:2 * h + 2, :],
                                              bank_d[h][:].rearrange("p (t d) -> p t d", t=2),
                                              grouped(rows(k.x, g, 2 * h, 2), 2), ALU.add).then_inc(sum_rdy, 1)
                        dve.wait_ge(sum_rdy, ONE + 2 * g + 2)
                        dve.wait_ge(row_in[a], 16 * TG * K * (i + 1))
                        for q in range(K):
                            for j in range(TG):
                                if q:
                                    dve.wait_ge(add_rdy, ONE + ADDS * g + TG * (q - 1) + j + 1)
                                dve.scalar_tensor_tensor(res[a][:, j, :], row[a][:, j, q, :],
                                                         k.gate[:, bass.ds(g * TG * K + j * K + q, 1)],
                                                         res[a][:, j, :], ALU.mult, ALU.add).then_inc(add_rdy, 1)
                        for j in range(TG):
                            dve.wait_ge(add_rdy, ONE + ADDS * g + TG * (K - 1) + j + 1)
                            apart(dve, k.past_dve)
                            dve.bn_stats(stat[:, j, :], res[a][:, j, :]).then_inc(stat_rdy, 1)
                        for j in range(TG):
                            dve.wait_ge(stat_rdy, ONE + TG * g + j + 1)
                            apart(dve, k.past_dve)
                            last = dve.bn_aggr(mv[:, j, :], stat[:, j, :])
                        last.then_inc(mv_rdy, 1)
                        dve.wait_ge(rs_rdy, ONE + g + 1)
                        for j in range(TG):
                            last = dve.tensor_scalar(res[a][:, j, :], res[a][:, j, :], mv[:, j, 0:1], rs[:, j:j + 1],
                                                     ALU.subtract, ALU.mult)
                        last.then_inc(res_rdy, 1)


class Kept:
    pass


def build(nc, dram):
    with ExitStack() as ctx:
        def sb(name, shape, dt=F32):
            return ctx.enter_context(nc.sbuf_tensor(name, shape, dt))

        k = Kept()
        k.x = sb("x", [P, B * D])
        k.ident, k.before, k.ones = sb("ident", [P, P]), sb("before", [P, P]), sb("ones", [P, P])
        k.mhalf = sb("mhalf", [P, TG])
        k.td, k.tf, k.gam, k.bet = (sb(n, [P, DC]) for n in ("td", "tf", "gam", "bet"))
        k.decay, k.keep = sb("decay", [P, DC, T]), sb("keep", [P, GW])
        k.wkv_in = sb("wkv_in", [P, DC, GW + 1])
        k.bout, k.ebias = sb("bout", [P, D]), sb("ebias", [P, E])
        k.cent, k.iota_e = sb("cent", [P, DC, G + E]), sb("iota_e", [P, E])
        k.tok, k.count = sb("tok", [P, TG], I32), sb("count", [P, E])
        k.gate, k.slot = sb("gate", [P, B * K]), sb("slot", [P, B * K], I32)
        k.past_dve, k.past_pool = (ctx.enter_context(nc.semaphore(n)) for n in ("past_dve", "past_pool"))
        k.x2_d = nc.dram_tensor("x2_rows", [B * T, D], F32).ap()
        k.out_d = nc.dram_tensor("expert_rows", [SLOTS + SETW, D], F32).ap()
        k.plan = sb("plan", [1, 4 * P], I32)
        k.plan_d = nc.dram_tensor("item_list", [P, 4], I32).ap()
        k.slot_tok = nc.dram_tensor("slot_token", [SLOTS + SETW, 1], I32).ap()
        setup_stage(nc, k, dram)
        mixer_stage(nc, k, dram)
        attention_stage(nc, k, dram)
        plan_stage(nc, k)
        expert_stage(nc, k, dram)
        combine_stage(nc, k, dram)


_AS_THEY_ARE = {
    "x": "x", "td": "L0_attn_time_decay", "tf": "L0_attn_time_first", "gam": "L0_attn_ln_gamma",
    "bet": "L0_attn_ln_beta", "wq": "L0_xattn_Wq", "wxk": "L0_xattn_Wk", "wxv": "L0_xattn_Wv",
    "wout": "L0_xattn_Wout", "bout": "L0_xattn_bout", "gcen": "L0_ffn_group_centroids",
    "ecen": "L0_ffn_expert_centroids", "ebias": "L0_ffn_bias", "eg": "L0_ffn_wg", "eu": "L0_ffn_wu",
    "ed": "L0_ffn_wd", "sg": "L0_ffn_sg", "su": "L0_ffn_su", "sd": "L0_ffn_sd",
}
_TRANSPOSED = {"wk": "L0_attn_Wk", "wv": "L0_attn_Wv", "wr": "L0_attn_Wr", "wo": "L0_attn_Wo"}


def kernel(**inputs):
    import numpy as np
    import concourse.bacc as bacc
    from concourse.bass_utils import run_bass_kernel_spmd

    arrays = {n: np.ascontiguousarray(inputs[key]) for n, key in _AS_THEY_ARE.items()}
    arrays.update({n: np.ascontiguousarray(np.transpose(inputs[key])) for n, key in _TRANSPOSED.items()})
    context = np.asarray(inputs["ctx_768"])
    arrays["ctx"] = np.ascontiguousarray(np.transpose(context, (2, 0, 1)).reshape(CD, B * T))

    nc = bacc.Bacc("TRN2", target_bir_lowering=False, num_devices=1)
    dram = {n: nc.dram_tensor(f"in_{n}", a.shape, mybir.dt.from_np(a.dtype), kind="ExternalInput").ap()
            for n, a in arrays.items()}
    dram["out"] = nc.dram_tensor("out_rows", (B, T, D), F32, kind="ExternalOutput").ap()
    build(nc, dram)
    result = run_bass_kernel_spmd(nc, [{f"in_{n}": a for n, a in arrays.items()}], core_ids=[0])
    return result.results[0]["out_rows"]
```

```python
from contextlib import ExitStack

import concourse.bass as bass
from concourse import mybir

F32 = mybir.dt.float32
F32R = mybir.dt.float32r
I32 = mybir.dt.int32
U32 = mybir.dt.uint32
ALU = mybir.AluOpType
ACT = mybir.ActivationFunctionType
AX = mybir.AxisListType

P = 128
B, T, D = 64, 128, 256
TG = 4
NG = B // TG
GW = TG * T
GX = TG * D
DC = D // P
CD, CC = 192, 96
HEADS, DH = 8, 64
INNER = HEADS * DH
IC = INNER // P
HID = 512
HC = HID // P
E, G, K = 32, 8, 4
EG = E // G
NTOP = G // 2
CAP = int(B * T / E * K * 1.25)
TI, RT = 4, 112
SETW = TI * RT
NSET = -(-CAP // SETW)
ES = NSET * SETW
SLOTS = E * ES
FAR = 4 * SLOTS
EPS = 1e-5
SCALE = DH ** -0.5
NEG = 1e9


def rows(x, g, j=0, n=TG):
    return x[:, bass.ds(g * GX + j * D, n * D)]


def grouped(ap, n=TG):
    return ap.rearrange("p (t d) -> p t d", t=n)


def apart(eng, past):
    eng.sem_inc(past, 1)


ONE = 1
DMA = 16


def begin(eng, *counts, dma=()):
    for c in counts:
        eng.sem_inc(c, ONE)
    for c in dma:
        eng.sem_inc(c, DMA)


class Parts:

    def __init__(self, nc, ctx, tag):
        self.nc, self.ctx, self.tag = nc, ctx, tag

    def sb(self, name, shape, dt=F32):
        return self.ctx.enter_context(self.nc.sbuf_tensor(self.tag + name, shape, dt))

    def bank(self, name):
        return self.ctx.enter_context(self.nc.psum_tensor(self.tag + name, [P, 512], F32))

    def sem(self, name):
        return self.ctx.enter_context(self.nc.semaphore(self.tag + name))


def setup_stage(nc, k, dram):
    with ExitStack() as ctx:
        p = Parts(nc, ctx, "c_")
        td, tf = p.sb("td", [P, DC]), p.sb("tf", [P, DC])
        zero, ones = p.sb("zero", [P, T]), p.sb("ones", [P, T])
        cen, sq = p.sb("cen", [G + E, D]), p.sb("sq", [G + E, D])
        nrm = p.sb("nrm", [G + E, 4])
        half = p.sb("half", [P, 1])
        tp = p.bank("tp")
        vec_in, cen_in = p.sem("vec_in"), p.sem("cen_in")
        fill, ident, sig, tri = p.sem("fill"), p.sem("ident"), p.sem("sig"), p.sem("tri")
        table, cent, root, cen_t = p.sem("table"), p.sem("cent"), p.sem("root"), p.sem("cen_t")
        iot, squared = p.sem("iot"), p.sem("squared")

        with nc.Block() as block:
            @block.sync
            def _(sp):
                with nc.allow_non_contiguous_dma(reason="short vectors"):
                    for dst, src in ((td, dram["td"]), (tf, dram["tf"]), (k.gam, dram["gam"]), (k.bet, dram["bet"])):
                        sp.dma_start(dst[:], src.rearrange("(c p) -> p c", p=P)).then_inc(vec_in, 16)
                sp.dma_start(cen[0:G, :], dram["gcen"]).then_inc(cen_in, 16)
                sp.dma_start(cen[G:G + E, :], dram["ecen"]).then_inc(cen_in, 16)
                sp.dma_start(k.ebias[:], dram["ebias"].rearrange("(a e) -> a e", a=1).to_broadcast([P, E])).then_inc(vec_in, 16)
                sp.dma_start(k.bout[:], dram["bout"].rearrange("(a e) -> a e", a=1).to_broadcast([P, D])).then_inc(vec_in, 16)
                sp.wait_ge(vec_in, 96)

            @block.gpsimd
            def _(pool):
                pool.memset(k.ident[:], 0.0).then_inc(fill, 1)
                pool.memset(k.before[:], 1.0).then_inc(fill, 1)
                pool.memset(k.ones[:], 1.0).then_inc(fill, 1)
                pool.memset(k.mhalf[:], -0.5).then_inc(fill, 1)
                pool.memset(half[:], 0.5).then_inc(fill, 1)
                pool.memset(k.keep[:], 1.0).then_inc(fill, 1)
                pool.wait_ge(fill, 6)
                pool.affine_select(out=k.ident[:], in_=k.ident[:], compare_op=ALU.not_equal, fill=1.0, base=0,
                                   pattern=[[-1, P]], channel_multiplier=1).then_inc(ident, 1)
                pool.affine_select(out=k.before[:], in_=k.before[:], compare_op=ALU.is_gt, fill=0.0, base=0,
                                   pattern=[[1, P]], channel_multiplier=-1).then_inc(tri, 1)
                first = k.keep[:].rearrange("p (b t) -> p b t", b=TG)[:, :, 0:1]
                pool.memset(first, 0.0).then_inc(tri, 1)
                pool.iota(k.iota_e[:], pattern=[[1, E]], base=0, channel_multiplier=0,
                          allow_small_or_imprecise_dtypes=True).then_inc(iot, 1)
                pool.iota(k.tok[:], pattern=[[T, TG]], base=0, channel_multiplier=1).then_inc(iot, 1)
                pool.wait_ge(cent, 1)
                pool.tensor_tensor(nrm[:, 1:2], nrm[:, 0:1], half[0:G + E, :], ALU.pow).then_inc(root, 1)

            @block.scalar
            def _(act):
                act.wait_ge(vec_in, 96)
                act.activation(k.td[:], td[:], ACT.Sigmoid).then_inc(sig, 1)
                act.activation(k.tf[:], tf[:], ACT.Sigmoid).then_inc(sig, 1)

            @block.vector
            def _(dve):
                dve.memset(zero[:], 0.0).then_inc(table, 1)
                dve.memset(ones[:], 1.0).then_inc(table, 1)
                dve.memset(k.count[:], 0.0).then_inc(table, 1)
                dve.memset(k.wkv_in[:], 0.0).then_inc(table, 1)
                dve.wait_ge(table, 2)
                dve.wait_ge(sig, 2)
                for c in range(DC):
                    dve.tensor_scalar(k.decay[:, c, :], ones[:], k.td[:, c:c + 1], None, ALU.mult).then_inc(table, 1)
                    dve.wait_ge(table, 5 + 3 * c)
                    dve.tensor_tensor_scan(k.decay[:, c, :], k.decay[:, c, :], zero[:], 1.0, ALU.mult, ALU.add).then_inc(table, 1)
                    dve.wait_ge(table, 6 + 3 * c)
                    dve.memset(k.decay[:, c, T - 1:T], 0.0).then_inc(table, 1)
                dve.wait_ge(cen_in, 32)
                dve.tensor_tensor(sq[:], cen[:], cen[:], ALU.mult).then_inc(squared, 1)
                dve.wait_ge(squared, 1)
                dve.tensor_reduce(nrm[:, 0:1], sq[:], AX.X, ALU.add).then_inc(cent, 1)
                dve.wait_ge(root, 1)
                dve.tensor_scalar(nrm[:, 2:3], nrm[:, 1:2], 1e-12, None, ALU.max).then_inc(cent, 1)
                dve.wait_ge(cent, 2)
                dve.reciprocal(nrm[:, 3:4], nrm[:, 2:3]).then_inc(cent, 1)
                dve.wait_ge(cent, 3)
                dve.tensor_scalar(cen[:], cen[:], nrm[:, 3:4], None, ALU.mult).then_inc(cent, 1)
                dve.wait_ge(cen_t, 1)
                dve.tensor_copy(k.cent[:], tp[:, 0:DC * (G + E)].rearrange("p (c e) -> p c e", c=DC)).then_inc(cent, 1)

            @block.tensor
            def _(pe):
                pe.wait_ge(ident, 1)
                pe.wait_ge(cent, 4)
                for c in range(DC):
                    last = pe.transpose(tp[:, c * (G + E):(c + 1) * (G + E)], cen[:, c * P:(c + 1) * P],
                                        k.ident[0:G + E, 0:G + E])
                last.then_inc(cen_t, 1)


def mixer_stage(nc, k, dram):
    with ExitStack() as ctx:
        p = Parts(nc, ctx, "m_")
        w = {n: p.sb("w" + n, [P, DC, D]) for n in "kvro"}
        xn, xnt = p.sb("xn", [P, TG, D]), p.sb("xnt", [P, DC, GW])
        sr, kv = p.sb("sr", [P, DC, GW]), p.sb("kv", [P, DC, GW])
        kc = p.sb("kc", [P, DC, GW])
        run, y = p.sb("run", [P, DC, GW]), p.sb("y", [P, DC, GW])
        stat, stat2 = p.sb("stat", [P, TG, 6]), p.sb("stat2", [P, TG, 6])
        mv, mv2 = p.sb("mv", [P, TG, 2]), p.sb("mv2", [P, TG, 2])
        ve, ve2 = p.sb("ve", [P, TG]), p.sb("ve2", [P, TG])
        rs, rs2 = p.sb("rs", [P, TG]), p.sb("rs2", [P, TG])
        bank_t, bank_o = p.bank("t"), p.bank("o")
        bank = [{n: p.bank(f"{n}{c}") for n in "kvr"} for c in range(DC)]
        w_in, x_in = p.sem("w_in"), p.sem("x_in")
        stat_rdy, mv_rdy, ve_rdy, rs_rdy = p.sem("stat"), p.sem("mv"), p.sem("ve"), p.sem("rs")
        xn_rdy, t_done, xnt_rdy = p.sem("xn"), p.sem("t_done"), p.sem("xnt")
        kvr_done, kv_rdy, sr_rdy = p.sem("kvr"), p.sem("kv"), p.sem("sr")
        w_rdy, run_rdy, wkv_rdy, y_rdy = p.sem("w"), p.sem("run"), p.sem("wkv"), p.sem("y")
        o_done, h_rdy, stat2_rdy, mv2_rdy = p.sem("o_done"), p.sem("h"), p.sem("stat2"), p.sem("mv2")
        ve2_rdy, rs2_rdy, x1_rdy, kc_rdy = p.sem("ve2"), p.sem("rs2"), p.sem("x1"), p.sem("kc")

        with nc.Block() as block:
            @block.sync
            def _(sp):
                begin(sp, dma=(x_in, w_in,))
                sp.dma_start(grouped(rows(k.x, 0)), dram["x"].rearrange("b t d -> t b d")[:, 0:TG, :]).then_inc(x_in, 16)
                for n in "kvro":
                    sp.dma_start(w[n][:], dram["w" + n].rearrange("(c p) n -> p c n", p=P)).then_inc(w_in, 16)
                with sp.Fori(1, NG) as g:
                    sp.wait_ge(x_in, DMA + 16 * g)
                    sp.dma_start(grouped(rows(k.x, g)),
                                 dram["x"].rearrange("b t d -> t b d")[:, bass.ds(g * TG, TG), :]).then_inc(x_in, 16)

            @block.tensor
            def _(pe):
                begin(pe, t_done, kvr_done, o_done)
                def turn(g, c):
                    if c == 0:
                        pe.wait_ge(xn_rdy, ONE + g + 1)
                    pe.wait_ge(xnt_rdy, ONE + DC * g + c)
                    for j in range(TG):
                        last = pe.transpose(bank_t[:, j * P:(j + 1) * P], xn[:, j, c * P:(c + 1) * P], k.ident[:])
                    last.then_inc(t_done, 1)

                def project(g):
                    pe.wait_ge(xnt_rdy, ONE + DC * (g + 1))
                    pe.wait_ge(kv_rdy, ONE + DC * g)
                    pe.wait_ge(sr_rdy, ONE + DC * g)
                    for c in range(DC):
                        for n in "kvr":
                            for q in range(DC):
                                last = pe.matmul(bank[c][n][:], w[n][:, q, c * P:(c + 1) * P], xnt[:, q, :],
                                                 start=(q == 0), stop=(q == DC - 1))
                            last.then_inc(kvr_done, 1)

                def mix(g, h):
                    pe.wait_ge(y_rdy, ONE + DC * (g + 1))
                    pe.wait_ge(h_rdy, ONE + 2 * g + h)
                    for j in range(2 * h, 2 * h + 2):
                        for q in range(DC):
                            last = pe.matmul(bank_o[:, (j % 2) * D:(j % 2 + 1) * D], y[:, q, j * T:(j + 1) * T],
                                             w["o"][:, q, :], start=(q == 0), stop=(q == DC - 1))
                    last.then_inc(o_done, 1)

                turn(0, 0)
                turn(0, 1)
                pe.wait_ge(w_in, DMA + 64)
                project(0)
                turn(1, 0)
                turn(1, 1)
                with pe.Fori(1, NG - 1) as g:
                    project(g)
                    turn(g + 1, 0)
                    mix(g - 1, 0)
                    turn(g + 1, 1)
                    mix(g - 1, 1)
                project(NG - 1)
                for g in (NG - 2, NG - 1):
                    mix(g, 0)
                    mix(g, 1)

            @block.scalar
            def _(act):
                begin(act, xnt_rdy, sr_rdy, kc_rdy)
                def norm_out(g):
                    for c in range(DC):
                        act.wait_ge(t_done, ONE + DC * g + c + 1)
                        act.wait_ge(kvr_done, ONE + 3 * DC * g)
                        act.activation(xnt[:, c, :], bank_t[:], ACT.Identity, bias=k.bet[:, c:c + 1],
                                       scale=k.gam[:, c:c + 1]).then_inc(xnt_rdy, 1)

                def gate(g):
                    for c in range(DC):
                        act.wait_ge(kvr_done, ONE + 3 * DC * g + 3 * c + 1)
                        act.wait_ge(kv_rdy, ONE + DC * g + c)
                        act.activation(kc[:, c, :], bank[c]["k"][:], ACT.Copy).then_inc(kc_rdy, 1)
                        act.wait_ge(kvr_done, ONE + 3 * DC * g + 3 * c + 3)
                        act.wait_ge(y_rdy, ONE + DC * g)
                        act.activation(sr[:, c, :], bank[c]["r"][:], ACT.Sigmoid).then_inc(sr_rdy, 1)

                norm_out(0)
                with act.Fori(0, NG - 1) as g:
                    gate(g)
                    norm_out(g + 1)
                gate(NG - 1)

            @block.gpsimd
            def _(pool):
                begin(pool, ve_rdy, rs_rdy, w_rdy, y_rdy, ve2_rdy, rs2_rdy)
                def rstd(g, mv_s, ve_s, rs_s, mv_t, ve_t, rs_t):
                    pool.wait_ge(mv_s, ONE + g + 1)
                    apart(pool, k.past_pool)
                    pool.tensor_scalar(ve_t[:], mv_t[:, :, 1], EPS, None, ALU.add).then_inc(ve_s, 1)
                    pool.wait_ge(ve_s, ONE + g + 1)
                    pool.tensor_tensor(rs_t[:], ve_t[:], k.mhalf[:], ALU.pow).then_inc(rs_s, 1)

                def decayed(g, c):
                    pool.wait_ge(kv_rdy, ONE + DC * g + c + 1)
                    pool.wait_ge(run_rdy, ONE + DC * g)
                    pool.tensor_tensor(k.wkv_in[:, c, 1:GW + 1].rearrange("p (b t) -> p b t", b=TG),
                                       kv[:, c, :].rearrange("p (b t) -> p b t", b=TG),
                                       k.decay[:, c, None, :].to_broadcast([P, TG, T]), ALU.mult).then_inc(w_rdy, 1)

                def gated(g, c):
                    pool.wait_ge(wkv_rdy, ONE + DC * g + c + 1)
                    pool.wait_ge(sr_rdy, ONE + DC * g + c + 1)
                    pool.wait_ge(o_done, ONE + 2 * g)
                    pool.tensor_tensor(y[:, c, :], run[:, c, :], sr[:, c, :], ALU.mult).then_inc(y_rdy, 1)

                def recur(g, more=True):
                    if more:
                        rstd(g + 1, mv_rdy, ve_rdy, rs_rdy, mv, ve, rs)
                    for c in range(DC):
                        decayed(g, c)
                    for c in range(DC):
                        gated(g, c)

                rstd(0, mv_rdy, ve_rdy, rs_rdy, mv, ve, rs)
                recur(0)
                with pool.Fori(1, NG - 1) as g:
                    recur(g)
                    rstd(g - 1, mv2_rdy, ve2_rdy, rs2_rdy, mv2, ve2, rs2)
                recur(NG - 1, False)
                for g in (NG - 2, NG - 1):
                    rstd(g, mv2_rdy, ve2_rdy, rs2_rdy, mv2, ve2, rs2)

            @block.vector
            def _(dve):
                begin(dve, stat_rdy, mv_rdy, xn_rdy, kv_rdy, run_rdy, wkv_rdy, h_rdy, stat2_rdy, mv2_rdy)
                def moments(g, st, mvt, st_s, mv_s):
                    apart(dve, k.past_dve)
                    for j in range(TG):
                        dve.bn_stats(st[:, j, :], rows(k.x, g, j, 1)).then_inc(st_s, 1)
                    for j in range(TG):
                        dve.wait_ge(st_s, ONE + TG * g + j + 1)
                        apart(dve, k.past_dve)
                        last = dve.bn_aggr(mvt[:, j, :], st[:, j, :])
                    last.then_inc(mv_s, 1)

                def moments_in(g):
                    dve.wait_ge(x_in, DMA + 16 * (g + 1))
                    moments(g, stat, mv, stat_rdy, mv_rdy)

                def norm_in(g):
                    dve.wait_ge(rs_rdy, ONE + g + 1)
                    dve.wait_ge(t_done, ONE + DC * g)
                    for j in range(TG):
                        last = dve.tensor_scalar(xn[:, j, :], rows(k.x, g, j, 1), mv[:, j, 0:1], rs[:, j:j + 1],
                                                 ALU.subtract, ALU.mult)
                    last.then_inc(xn_rdy, 1)

                def keyed(g, c):
                    dve.wait_ge(kvr_done, ONE + 3 * DC * g + 3 * c + 2)
                    dve.wait_ge(w_rdy, ONE + DC * g)
                    dve.wait_ge(kc_rdy, ONE + DC * g + c + 1)
                    dve.tensor_tensor(kv[:, c, :], kc[:, c, :], bank[c]["v"][:], ALU.mult).then_inc(kv_rdy, 1)

                def summed(g, c):
                    dve.wait_ge(w_rdy, ONE + DC * g + c + 1)
                    dve.wait_ge(y_rdy, ONE + DC * g)
                    dve.tensor_tensor_scan(run[:, c, :], k.keep[:], k.wkv_in[:, c, 0:GW], 0.0,
                                           ALU.mult, ALU.add).then_inc(run_rdy, 1)
                    dve.wait_ge(run_rdy, ONE + DC * g + c + 1)
                    dve.scalar_tensor_tensor(run[:, c, :], kv[:, c, :], k.tf[:, c:c + 1], run[:, c, :],
                                             ALU.mult, ALU.add).then_inc(wkv_rdy, 1)

                def residual(g, h):
                    dve.wait_ge(o_done, ONE + 2 * g + h + 1)
                    dve.tensor_tensor(rows(k.x, g, 2 * h, 2), bank_o[:], rows(k.x, g, 2 * h, 2), ALU.add)\
                       .then_inc(h_rdy, 1)

                def norm_out(g):
                    dve.wait_ge(h_rdy, ONE + 2 * (g + 1))
                    moments(g, stat2, mv2, stat2_rdy, mv2_rdy)
                    dve.wait_ge(rs2_rdy, ONE + g + 1)
                    for j in range(TG):
                        last = dve.tensor_scalar(rows(k.x, g, j, 1), rows(k.x, g, j, 1), mv2[:, j, 0:1],
                                                 rs2[:, j:j + 1], ALU.subtract, ALU.mult)
                    last.then_inc(x1_rdy, 1)

                def group(g, first=False, final=False):
                    if not final:
                        moments_in(g + 1)
                    for c in range(DC):
                        keyed(g, c)
                    if not final:
                        norm_in(g + 1)
                    for c in range(DC):
                        summed(g, c)
                        if not first and not final:
                            residual(g - 1, c)
                    if not first and not final:
                        norm_out(g - 1)

                moments_in(0)
                norm_in(0)
                group(0, first=True)
                with dve.Fori(1, NG - 1) as g:
                    group(g)
                group(NG - 1, final=True)
                for g in (NG - 2, NG - 1):
                    for h in range(2):
                        residual(g, h)
                    norm_out(g)


class Plan:

    def __init__(self, k, p):
        self.k = k
        self.taken, self.n_items, self.more = (p.sb(n, [P, E]) for n in ("taken", "n_items", "more"))
        self.ones, self.upto, self.whole = (p.sb(n, [P, E]) for n in ("p_ones", "upto", "whole"))
        self.item, self.col, self.col_i = p.sb("item", [P, 1]), p.sb("col", [P, 4]), p.sb("col_i", [P, 4], I32)
        self.item_rdy, self.total, self.step, self.listed, self.plan_in = \
            (p.sem(n) for n in ("item_rdy", "total", "plan_step", "listed", "plan_in"))

    def totals(self, pe, bank):
        pe.matmul(bank[:, 0:E], self.k.ones[:], self.k.count[:], start=True, stop=True).then_inc(self.total, 1)

    def numbers(self, pool):
        pool.iota(self.item[:], pattern=[[0, 1]], base=0, channel_multiplier=1,
                  allow_small_or_imprecise_dtypes=True).then_inc(self.item_rdy, 1)

    def make(self, dve, bank):
        taken, n_items, more, ones = self.taken, self.n_items, self.more, self.ones
        upto, whole, item, col, col_i = self.upto, self.whole, self.item, self.col, self.col_i
        done = [0]

        def then(ins):
            done[0] += 1
            ins.then_inc(self.step, 1)
            dve.wait_ge(self.step, done[0])

        dve.wait_ge(self.total, 1)
        then(dve.tensor_scalar(taken[:], bank[:, 0:E], float(CAP), None, ALU.min))
        then(dve.tensor_scalar(n_items[:], taken[:], 0.0, None, ALU.is_gt))
        for s in range(1, NSET):
            then(dve.tensor_scalar(more[:], taken[:], float(s * SETW), None, ALU.is_gt))
            then(dve.tensor_tensor(n_items[:], n_items[:], more[:], ALU.add))
        then(dve.memset(ones[:], 1.0))
        then(dve.tensor_tensor_scan(upto[:], ones[:], n_items[:], 0.0, ALU.mult, ALU.add))
        dve.wait_ge(self.item_rdy, 1)
        then(dve.tensor_scalar(whole[:], upto[:], item[:, 0:1], None, ALU.is_le))
        then(dve.tensor_reduce(col[:, 0:1], whole[:], AX.X, ALU.add))
        then(dve.tensor_tensor(more[:], n_items[:], whole[:], ALU.mult))
        then(dve.tensor_reduce(col[:, 1:2], more[:], AX.X, ALU.add))
        then(dve.tensor_tensor(col[:, 2:3], item[:], col[:, 1:2], ALU.subtract))
        then(dve.tensor_scalar(col[:, 2:3], col[:, 2:3], float(SETW), None, ALU.mult))
        then(dve.tensor_scalar(col[:, 3:4], col[:, 0:1], float(ES), None, ALU.mult))
        then(dve.tensor_tensor(col[:, 3:4], col[:, 3:4], col[:, 2:3], ALU.add))
        then(dve.tensor_scalar(col_i[:, 0:1], col[:, 3:4], float(SLOTS), None, ALU.min))
        then(dve.tensor_scalar(col_i[:, 1:2], col[:, 0:1], float(E - 1), None, ALU.min))
        then(dve.tensor_copy(col_i[:, 2:3], upto[:, E - 1:E]))
        dve.tensor_copy(col_i[:, 3:4], upto[:, E - 1:E]).then_inc(self.listed, 1)

    def deliver(self, sp):
        k = self.k
        sp.wait_ge(self.listed, 1)
        sp.dma_start(k.plan_d, self.col_i[:]).then_inc(self.plan_in, 16)
        sp.wait_ge(self.plan_in, 16)
        sp.dma_start(k.plan[:], k.plan_d.rearrange("w f -> (w f)").rearrange("(a n) -> a n", a=1))\
          .then_inc(self.plan_in, 16)
        sp.wait_ge(self.plan_in, 32)


def attention_stage(nc, k, dram):
    with ExitStack() as ctx:
        p = Parts(nc, ctx, "a_")
        wq, wk, wv = p.sb("wq", [P, DC, INNER]), p.sb("wk", [CC, 2, INNER]), p.sb("wv", [CC, 2, INNER])
        wo = p.sb("wo", [P, IC, D])
        xs, xt = p.sb("xs", [P, TG, D]), p.sb("xt", [P, DC, GW])
        ct = [p.sb(f"ct{i}", [CC, 2, GW]) for i in range(2)]
        qt = [p.sb(f"qt{i}", [P, IC, GW]) for i in range(2)]
        kt = [p.sb(f"kt{i}", [P, IC, GW]) for i in range(2)]
        vv = [p.sb(f"vv{i}", [P, TG, INNER]) for i in range(2)]
        prob, prob_t = p.sb("prob", [P, HEADS, T]), p.sb("prob_t", [P, HEADS, T])
        ot = p.sb("ot", [P, IC, T])
        top, nbias = p.sb("top", [P, HEADS]), p.sb("nbias", [P, HEADS])
        den, rden = p.sb("den", [P, HEADS]), p.sb("rden", [P, HEADS])
        stat, mv = p.sb("stat", [P, TG, 6]), p.sb("mv", [P, TG, 2])
        ve, rs = p.sb("ve", [P, TG]), p.sb("rs", [P, TG])
        zero = p.sb("zero", [P, D])
        rxs, rxt = p.sb("rxs", [P, TG, D]), p.sb("rxt", [P, DC, GW])
        sqr = p.sb("sqr", [P, TG, D])
        ssq, nrm, rn = p.sb("ssq", [P, TG]), p.sb("nrm", [P, TG]), p.sb("rn", [P, TG])
        r_half = p.sb("half", [P, TG])
        sc = p.sb("sc", [P, TG, G + E])
        gtop, gidx, gsel = p.sb("gtop", [P, TG, 8]), p.sb("gidx", [P, TG, 8], U32), p.sb("gsel", [P, TG, NTOP])
        geq, gmask, gpen = p.sb("geq", [P, TG, G, NTOP]), p.sb("gmask", [P, TG, G]), p.sb("gpen", [P, TG, G])
        es = p.sb("es", [P, TG, E])
        etop, eidx, esel = p.sb("etop", [P, TG, 8]), p.sb("eidx", [P, TG, 8], U32), p.sb("esel", [P, TG, K])
        dif, ex = p.sb("dif", [P, TG, K]), p.sb("ex", [P, TG, K])
        esum, er = p.sb("esum", [P, TG]), p.sb("er", [P, TG])
        hot, hit = p.sb("hot", [P, TG, K, E]), p.sb("hit", [P, TG, K, E])
        mask, sofar = p.sb("mask", [P, TG, E]), p.sb("sofar", [P, TG, E])
        pos, kept, posc = p.sb("pos", [P, TG, K]), p.sb("kept", [P, TG, K]), p.sb("posc", [P, TG, K])
        base = p.sb("base", [P, TG, K])
        far, slot_i = p.sb("far", [P, TG, K]), p.sb("slot_i", [P, TG, K], I32)
        blank = p.sb("blank", [RT, (SLOTS + SETW) // RT], I32)
        zero_rdy, filled = p.sem("zero_rdy"), p.sem("filled")
        bank_a = [p.bank(f"a{i}") for i in range(2)]
        bank_s = [p.bank(f"s{i}") for i in range(2)]
        bank_t = [p.bank(f"t{i}") for i in range(2)]
        bank_v, bank_o = p.bank("v"), p.bank("o")
        w_in, wo_in = p.sem("w_in"), p.sem("wo_in")
        c_in = [p.sem(f"c_in{i}") for i in range(2)]
        a_done, a_out = p.sem("a_done"), p.sem("a_out")
        s_done, top_rdy, nb_rdy, e_rdy = p.sem("s_done"), p.sem("top"), p.sem("nb"), p.sem("e")
        rden_rdy, n_rdy, t_done, t_out = p.sem("rden"), p.sem("n"), p.sem("t_done"), p.sem("t_out")
        v_done, ot_rdy, o_done, h_rdy = p.sem("v_done"), p.sem("ot"), p.sem("o_done"), p.sem("h")
        xb_rdy, stat_rdy, mv_rdy, ve_rdy = p.sem("xb"), p.sem("stat"), p.sem("mv"), p.sem("ve")
        rs_rdy, x2_rdy, x2_out, xs_rdy = p.sem("rs"), p.sem("x2"), p.sem("x2_out"), p.sem("xs")

        rxs_rdy, ssq_rdy, nrm_rdy, ex_rdy = p.sem("rxs"), p.sem("ssq"), p.sem("nrm"), p.sem("ex")
        step, mask_rdy, slot_rdy, dif_rdy = p.sem("step"), p.sem("mask"), p.sem("slot"), p.sem("dif")
        posc_rdy, hand_rdy, scattered, tok_rdy = p.sem("posc"), p.sem("hand"), p.sem("scattered"), p.sem("tok")
        COUNTED = K + TG
        blank_rdy, blanked, half_rdy = p.sem("blank_rdy"), p.sem("blanked"), p.sem("half_rdy")
        INVERTED, GROUPED, CHOSEN, STEPS = 2, 11, 15, 23

        plan = Plan(k, p)

        A = [[("t", 0), ("t", 1), ("q", 0), ("q", 1)], [("q", 2), ("q", 3), ("k", 0)],
             [("k", 1), ("k", 2), ("k", 3)], [("v", m) for m in range(TG)]]
        R = [[], [("rt", 0), ("rt", 1)], [("rs", 0)], []]
        RP = [[], [("rp", 0)], [], []]
        assert IC == 4 and TG == 4

        def parts(*kinds):
            return [sum(q, []) for q in zip(*kinds)]

        def jobs(h):
            if isinstance(h, int):
                return parts(*[A] * (h < NG), *[RP] * (h >= 3), *[R] * (2 <= h < NG + 2))
            return ALL

        ALL = parts(A, RP, R)
        NJ = sum(map(len, ALL))

        def before(h):
            if isinstance(h, int):
                return sum(len(part) for i in range(h) for part in jobs(i))
            return h * NJ - (3 * NJ - before(3))

        def bank_of(h, n):
            assert NJ % 2 == 0
            return bank_a[(before(h if isinstance(h, int) else 3) + n) % 2]

        def numbered(h, q):
            first = sum(map(len, jobs(h)[:q]))
            return [(first + i, kind, m) for i, (kind, m) in enumerate(jobs(h)[q])]

        def upto(h, kind, m):
            return [job for part in jobs(h) for job in part].index((kind, m)) + 1

        ctx_d = dram["ctx"].rearrange("(c p) n -> p c n", p=CC)

        def groups(eng, slot, part):
            for q in range(4):
                part(0, 0, q)
            for b in range(TG):
                slot(0, 0, b, lambda b=b: part(1, 1, b), b == 0)
            def two(i):
                for par in (1, 0):
                    g = 2 * i + (1 if par else 2)
                    for b in range(TG):
                        slot(g, par, b, lambda g=g, par=par, b=b: part(g + 1, 1 - par, b), False)

            two(0)
            with eng.Fori(1, (NG - 2) // 2) as i:
                two(i)
            for b in range(TG):
                slot(NG - 1, 1, b, lambda b=b: part(NG, 0, b), False)

        with nc.Block() as block:
            @block.sync
            def _(sp):
                begin(sp, dma=(w_in, wo_in, *c_in, x2_out, filled, blanked))
                sp.dma_start(wq[:], dram["wq"].rearrange("(c p) n -> p c n", p=P)).then_inc(w_in, 16)
                sp.dma_start(wk[:], dram["wxk"].rearrange("(c p) n -> p c n", p=CC)).then_inc(w_in, 16)
                sp.dma_start(ct[0][:], ctx_d[:, :, 0:GW]).then_inc(c_in[0], 16)
                sp.dma_start(wv[:], dram["wxv"].rearrange("(c p) n -> p c n", p=CC)).then_inc(w_in, 16)
                sp.dma_start(wo[:], dram["wout"].rearrange("(c p) n -> p c n", p=P)).then_inc(wo_in, 16)
                sp.dma_start(ct[1][:], ctx_d[:, :, GW:2 * GW]).then_inc(c_in[1], 16)

                FILL = SLOTS // NG
                sp.wait_ge(blank_rdy, 1)
                sp.dma_start(k.slot_tok.rearrange("(p n) a -> p (n a)", p=RT), blank[:]).then_inc(blanked, 16)
                sp.wait_ge(zero_rdy, 1)

                def store(g):
                    sp.dma_start(k.out_d[bass.ds(g * FILL, FILL), :].rearrange("(p n) d -> p n d", p=P),
                                 zero[:, None, :].to_broadcast([P, FILL // P, D])).then_inc(filled, 16)
                    sp.wait_ge(x2_rdy, ONE + g + 1)
                    sp.dma_start(k.x2_d[bass.ds(g * GW, GW), :].rearrange("(b t) d -> t b d", b=TG),
                                 grouped(rows(k.x, g))).then_inc(x2_out, 16)

                def turnover(i):
                    for par in range(2):
                        g = 2 * i + par
                        sp.wait_ge(a_done, ONE + before(g + 1))
                        sp.dma_start(ct[par][:], ctx_d[:, :, bass.ds((g + 2) * GW, GW)]).then_inc(c_in[par], 16)
                        store(g)

                turnover(0)
                with sp.Fori(1, (NG - 2) // 2) as i:
                    turnover(i)
                store(NG - 2)
                store(NG - 1)
                plan.deliver(sp)
                sp.wait_ge(x2_out, DMA + 16 * NG)
                sp.wait_ge(filled, DMA + 16 * NG)
                sp.wait_ge(blanked, DMA + 16)

            @block.tensor
            def _(pe):
                begin(pe, a_done, s_done, t_done, v_done, o_done)
                def part(g, par, q):
                    for n, kind, m in numbered(g, q):
                        out = bank_of(g, n)
                        pe.wait_ge(a_out, ONE + before(g) + n)
                        if kind == "t":
                            pe.wait_ge(xs_rdy, ONE + g + 1)
                            for j in range(TG):
                                last = pe.transpose(out[:, j * P:(j + 1) * P], xs[:, j, m * P:(m + 1) * P], k.ident[:])
                        elif kind == "q":
                            pe.wait_ge(a_out, ONE + before(g) + upto(g, "t", 1) + 1)
                            for c in range(DC):
                                last = pe.matmul(out[:], wq[:, c, m * P:(m + 1) * P], xt[:, c, :],
                                                 start=(c == 0), stop=(c == DC - 1))
                        elif kind == "k":
                            if m == 0:
                                ctx_landed(pe, g, par)
                            for c in range(2):
                                last = pe.matmul(out[:], wk[:, c, m * P:(m + 1) * P], ct[par][:, c, :],
                                                 start=(c == 0), stop=(c == 1))
                        elif kind == "rt":
                            pe.wait_ge(rxs_rdy, ONE + g - 2 + 1)
                            for j in range(TG):
                                last = pe.transpose(out[:, j * P:(j + 1) * P], rxs[:, j, m * P:(m + 1) * P], k.ident[:])
                        elif kind == "rs":
                            pe.wait_ge(a_out, ONE + before(g) + upto(g, "rt", 1) + 1)
                            for j in range(TG):
                                for c in range(DC):
                                    last = pe.matmul(out[:, j * (G + E):(j + 1) * (G + E)], rxt[:, c, j * T:(j + 1) * T],
                                                     k.cent[:, c, :], start=(c == 0), stop=(c == DC - 1))
                        elif kind == "rp":
                            pe.wait_ge(mask_rdy, ONE + COUNTED * (g - 3 + 1))
                            pe.matmul(out[:, 0:TG * E], k.before[:], mask[:].rearrange("p t e -> p (t e)"),
                                      start=True, stop=False)
                            last = pe.matmul(out[:, 0:TG * E], k.ones[:], sofar[:].rearrange("p t e -> p (t e)"),
                                             start=False, stop=True)
                        else:
                            for c in range(2):
                                last = pe.matmul(out[:], ct[par][:, c, m * T:(m + 1) * T], wv[:, c, :],
                                                 start=(c == 0), stop=(c == 1))
                        last.then_inc(a_done, 1)

                def ctx_landed(pe, g, par):
                    pe.wait_ge(c_in[par], DMA + 8 * (g - par) + 16)

                def out_rows(s):
                    pe.wait_ge(ot_rdy, ONE + s + 1)
                    pe.wait_ge(h_rdy, ONE + s)
                    for m in range(IC):
                        last = pe.matmul(bank_o[:, 0:D], ot[:, m, :], wo[:, m, :], start=(m == 0), stop=(m == IC - 1))
                    last.then_inc(o_done, 1)

                def slot(g, par, b, fill, first):
                    s = g * TG + b
                    pe.wait_ge(a_out, ONE + before(g + 1) + 1)
                    pe.wait_ge(e_rdy, ONE + s)
                    for m in range(IC):
                        for r in range(2):
                            last = pe.matmul(bank_s[r][:, m * T:(m + 1) * T],
                                             qt[par][r * DH:(r + 1) * DH, m, b * T:(b + 1) * T],
                                             kt[par][r * DH:(r + 1) * DH, m, b * T:(b + 1) * T],
                                             start=True, stop=True)
                    last.then_inc(s_done, 1)
                    fill()
                    pe.wait_ge(t_out, ONE + 2 * s)
                    for r in range(2):
                        pe.wait_ge(n_rdy, ONE + 2 * s + r + 1)
                        for m in range(IC):
                            last = pe.transpose(bank_t[r][:, m * T:(m + 1) * T], prob[:, r * IC + m, :], k.ident[:])
                        last.then_inc(t_done, 1)
                    if not first:
                        out_rows(s - 1)
                    pe.wait_ge(t_out, ONE + 2 * s + 2)
                    pe.wait_ge(ot_rdy, ONE + s)
                    for m in range(IC):
                        for r in range(2):
                            h = 2 * m + r
                            last = pe.matmul(bank_v[r * DH:(r + 1) * DH, m * T:(m + 1) * T],
                                             vv[par][:, b, h * DH:(h + 1) * DH], prob_t[:, r * IC + m, :],
                                             start=True, stop=True)
                    last.then_inc(v_done, 1)

                pe.wait_ge(w_in, DMA + 48)
                pe.wait_ge(wo_in, DMA + 16)
                groups(pe, slot, part)
                out_rows(B - 1)
                for h in (NG + 1, NG + 2):
                    for q in range(4):
                        part(h, 0, q)
                plan.totals(pe, bank_v)

            @block.scalar
            def _(act):
                begin(act, e_rdy, t_out, ssq_rdy, ex_rdy)
                def squares(r):
                    act.wait_ge(rxs_rdy, ONE + r + 1)
                    act.wait_ge(nrm_rdy, ONE + r)
                    for j in range(TG):
                        last = act.activation(sqr[:, j, :], rxs[:, j, :], ACT.Square, accum_out=ssq[:, j:j + 1])
                    last.then_inc(ssq_rdy, 1)

                def gate_exp(r):
                    act.wait_ge(dif_rdy, ONE + r + 1)
                    act.activation(ex[:], dif[:], ACT.Exp).then_inc(ex_rdy, 1)

                def slot(g, par, b, fill, first):
                    s = g * TG + b
                    if b == 0 and (not isinstance(g, int) or g >= 2):
                        gate_exp(g - 2)
                    act.wait_ge(nb_rdy, ONE + s + 1)
                    act.wait_ge(t_done, ONE + 2 * s)
                    act.wait_ge(rden_rdy, ONE + s)
                    for r in range(2):
                        for m in range(IC):
                            h = r * IC + m
                            last = act.activation(prob[:, h, :], bank_s[r][:, m * T:(m + 1) * T], ACT.Exp,
                                                  bias=nbias[:, h:h + 1], scale=SCALE, accum_out=den[:, h:h + 1])
                    last.then_inc(e_rdy, 1)
                    act.wait_ge(v_done, ONE + s)
                    for r in range(2):
                        act.wait_ge(t_done, ONE + 2 * s + r + 1)
                        act.activation(prob_t[:, r * IC:(r + 1) * IC, :],
                                       bank_t[r][:].rearrange("p (m t) -> p m t", m=IC), ACT.Copy).then_inc(t_out, 1)
                    if b == 1 and (not isinstance(g, int) or g >= 1):
                        squares(g - 1)

                groups(act, slot, lambda g, par, q: None)
                gate_exp(NG - 2)
                squares(NG - 1)
                gate_exp(NG - 1)

            @block.gpsimd
            def _(pool):
                pool.memset(zero[:], 0.0).then_inc(zero_rdy, 1)
                begin(pool, xs_rdy, xb_rdy, ve_rdy, rs_rdy, rxs_rdy, nrm_rdy, tok_rdy, mask_rdy)
                pool.memset(blank[:], 0).then_inc(blank_rdy, 1)
                pool.memset(r_half[:], 0.5).then_inc(half_rdy, 1)
                plan.numbers(pool)
                pool.wait_ge(half_rdy, 1)
                def stage(g):
                    pool.tensor_copy(xs[:], grouped(rows(k.x, g))).then_inc(xs_rdy, 1)
                    pool.tensor_tensor(grouped(rows(k.x, g)), grouped(rows(k.x, g)),
                                       k.bout[:, None, :].to_broadcast([P, TG, D]), ALU.add).then_inc(xb_rdy, 1)

                def rstd(g):
                    pool.wait_ge(mv_rdy, ONE + g + 1)
                    apart(pool, k.past_pool)
                    pool.tensor_scalar(ve[:], mv[:, :, 1], EPS, None, ALU.add).then_inc(ve_rdy, 1)
                    pool.wait_ge(ve_rdy, ONE + g + 1)
                    pool.tensor_tensor(rs[:], ve[:], k.mhalf[:], ALU.pow).then_inc(rs_rdy, 1)

                def norms(r, first=False):
                    pool.wait_ge(x2_rdy, ONE + r + 1)
                    if not first:
                        pool.wait_ge(a_done, ONE + before(r + 1) + upto(r + 1, "rt", 1))
                    pool.tensor_copy(rxs[:], grouped(rows(k.x, r))).then_inc(rxs_rdy, 1)
                    pool.wait_ge(ssq_rdy, ONE + r + 1)
                    if not first:
                        pool.wait_ge(step, ONE + STEPS * (r - 1) + INVERTED)
                    pool.tensor_tensor(nrm[:], ssq[:], r_half[:], ALU.pow).then_inc(nrm_rdy, 1)

                def counted(r):
                    pool.wait_ge(step, ONE + STEPS * r + CHOSEN)
                    steps = [(pool.tensor_tensor, mask[:], hot[:, :, 0, :], hot[:, :, 1, :], ALU.add)]
                    steps += [(pool.tensor_tensor, mask[:], mask[:], hot[:, :, q, :], ALU.add) for q in range(2, K)]
                    steps += [(pool.tensor_copy, sofar[:, 0, :], k.count[:])]
                    steps += [(pool.tensor_tensor, sofar[:, j, :], sofar[:, j - 1, :], mask[:, j - 1, :], ALU.add)
                              for j in range(1, TG)]
                    steps += [(pool.tensor_tensor, k.count[:], sofar[:, TG - 1, :], mask[:, TG - 1, :], ALU.add)]
                    assert len(steps) == COUNTED
                    for n, (do, *operands) in enumerate(steps):
                        if do == pool.tensor_copy:
                            apart(pool, k.past_pool)
                        do(*operands).then_inc(mask_rdy, 1)
                        pool.wait_ge(mask_rdy, ONE + COUNTED * r + n + 1)
                    apart(pool, k.past_pool)

                def scatter(r):
                    pool.wait_ge(slot_rdy, ONE + r + 1)
                    pool.wait_ge(tok_rdy, ONE + r)
                    pool.wait_ge(blanked, DMA + 16)
                    apart(pool, k.past_pool)
                    for j in range(TG):
                        for q in range(K):
                            pool.indirect_dma_start(
                                k.slot_tok, bass.IndirectOffsetOnAxis(ap=slot_i[:, j, q:q + 1], axis=0),
                                k.tok[:, j:j + 1], None, bounds_check=SLOTS - 1, oob_is_err=False)\
                                .then_inc(scattered, 16)
                    pool.wait_ge(scattered, 16 * TG * K * (r + 1))
                    apart(pool, k.past_pool)
                    pool.tensor_scalar(k.tok[:], k.tok[:], float(GW), None, ALU.add).then_inc(tok_rdy, 1)

                def around(g, scatters=True):
                    pool.wait_ge(a_done, ONE + before(g + 1) + 2)
                    stage(g + 2)
                    if scatters:
                        scatter(g - 2)
                    if not isinstance(g, int) or g:
                        counted(g - 1)
                    rstd(g)
                    norms(g, isinstance(g, int) and g == 0)

                stage(0)
                pool.wait_ge(a_done, ONE + 2)
                stage(1)
                around(0, False)
                around(1, False)
                with pool.Fori(2, NG - 2) as g:
                    around(g)
                for g in (NG - 2, NG - 1):
                    scatter(g - 2)
                    counted(g - 1)
                    rstd(g)
                    norms(g)
                counted(NG - 1)
                scatter(NG - 2)
                scatter(NG - 1)

            @block.vector
            def _(dve):
                begin(dve, a_out, top_rdy, nb_rdy, rden_rdy, n_rdy, h_rdy, stat_rdy, mv_rdy, x2_rdy, ot_rdy,
                      step, slot_rdy, posc_rdy, dif_rdy)
                dve.sem_inc(a_out, 1)

                class Steps:
                    def __init__(self, r, done):
                        self.r, self.done = r, done

                    def __call__(self, ins):
                        self.done += 1
                        ins.then_inc(step, 1)
                        dve.wait_ge(step, ONE + STEPS * self.r + self.done)

                def inverse_norms(r):
                    then = Steps(r, 0)
                    dve.wait_ge(nrm_rdy, ONE + r + 1)
                    then(dve.tensor_scalar(rn[:], nrm[:], 1e-12, None, ALU.max))
                    then(dve.reciprocal(rn[:], rn[:]))
                    assert then.done == INVERTED

                def choose_groups(r):
                    then = Steps(r, INVERTED)
                    h = r + 2
                    dve.wait_ge(a_out, ONE + 1 + before(h) + upto(h, "rs", 0))
                    io_g = k.iota_e[:, None, 0:G, None]
                    apart(dve, k.past_dve)
                    for j in range(TG):
                        last = dve.max(gtop[:, j, :], sc[:, j, 0:G])
                    then(last)
                    apart(dve, k.past_dve)
                    for j in range(TG):
                        last = dve.max_index(gidx[:, j, :], gtop[:, j, :], sc[:, j, 0:G])
                    then(last)
                    then(dve.tensor_copy(gsel[:], gidx[:, :, 0:NTOP]))
                    then(dve.tensor_tensor(geq[:], io_g.to_broadcast([P, TG, G, NTOP]),
                                           gsel[:, :, None, :].to_broadcast([P, TG, G, NTOP]), ALU.is_equal))
                    then(dve.tensor_reduce(gmask[:], geq[:], AX.X, ALU.add))
                    then(dve.tensor_scalar(gpen[:], gmask[:], -1.0, NEG, ALU.add, ALU.mult))
                    then(dve.tensor_tensor(es[:], sc[:, :, G:], k.ebias[:, None, :].to_broadcast([P, TG, E]), ALU.add))
                    for j in range(TG):
                        last = dve.tensor_tensor(es[:, j, :].rearrange("p (g e) -> p g e", g=G),
                                                 es[:, j, :].rearrange("p (g e) -> p g e", g=G),
                                                 gmask[:, j, :, None].to_broadcast([P, G, EG]), ALU.mult)
                    then(last)
                    for j in range(TG):
                        last = dve.tensor_tensor(es[:, j, :].rearrange("p (g e) -> p g e", g=G),
                                                 es[:, j, :].rearrange("p (g e) -> p g e", g=G),
                                                 gpen[:, j, :, None].to_broadcast([P, G, EG]), ALU.add)
                    then(last)
                    assert then.done == GROUPED, then.done

                def choose_experts(r):
                    then = Steps(r, GROUPED)
                    apart(dve, k.past_dve)
                    for j in range(TG):
                        last = dve.max(etop[:, j, :], es[:, j, :])
                    then(last)
                    dve.wait_ge(ex_rdy, ONE + r)
                    dve.tensor_tensor(dif[:], etop[:, :, 0:K], etop[:, :, 0:1].to_broadcast([P, TG, K]),
                                      ALU.subtract).then_inc(dif_rdy, 1)
                    for j in range(TG):
                        last = dve.max_index(eidx[:, j, :], etop[:, j, :], es[:, j, :])
                    then(last)
                    then(dve.tensor_copy(esel[:], eidx[:, :, 0:K]))
                    for j in range(TG):
                        last = dve.tensor_tensor(hot[:, j, :, :], k.iota_e[:, None, :].to_broadcast([P, K, E]),
                                                 esel[:, j, :, None].to_broadcast([P, K, E]), ALU.is_equal)
                    then(last)
                    assert then.done == CHOSEN, then.done

                def place(r):
                    then = Steps(r, CHOSEN)
                    h = r + 3
                    dve.wait_ge(a_out, ONE + 1 + before(h) + upto(h, "rp", 0))
                    then(dve.tensor_scalar(base[:], esel[:], float(ES), None, ALU.mult))
                    dve.wait_ge(ex_rdy, ONE + r + 1)
                    then(dve.tensor_reduce(esum[:], ex[:], AX.X, ALU.add))
                    then(dve.reciprocal(er[:], esum[:]))
                    then(dve.tensor_tensor(dif[:], ex[:], er[:, :, None].to_broadcast([P, TG, K]), ALU.mult))
                    then(dve.tensor_reduce(pos[:], hit[:], AX.X, ALU.add))
                    then(dve.tensor_scalar(kept[:], pos[:], float(CAP), None, ALU.is_lt))
                    gates = k.gate[:, bass.ds(r * TG * K, TG * K)].rearrange("p (t q) -> p t q", t=TG)
                    dve.tensor_tensor(gates, dif[:], kept[:], ALU.mult)
                    then(dve.tensor_scalar(far[:], kept[:], -1.0, -float(FAR), ALU.add, ALU.mult))
                    then(dve.tensor_tensor(far[:], far[:], pos[:], ALU.add))
                    dve.wait_ge(tok_rdy, ONE + r)
                    dve.tensor_tensor(slot_i[:], far[:], base[:], ALU.add).then_inc(slot_rdy, 1)
                    dve.tensor_scalar(posc[:], pos[:], float(CAP - 1), None, ALU.min).then_inc(posc_rdy, 1)
                    dve.wait_ge(posc_rdy, ONE + r + 1)
                    dve.tensor_tensor(k.slot[:, bass.ds(r * TG * K, TG * K)].rearrange("p (t q) -> p t q", t=TG),
                                      posc[:], base[:], ALU.add).then_inc(hand_rdy, 1)
                    assert then.done == STEPS, then.done

                def part(g, par, q):
                    for n, kind, m in numbered(g, q):
                        if kind == "rs":
                            inverse_norms(g - 2)
                        dve.wait_ge(a_done, ONE + before(g) + n + 1)
                        bank = bank_of(g, n)
                        if kind == "rs":
                            dve.tensor_tensor(sc[:], bank[:, 0:TG * (G + E)].rearrange("p (t e) -> p t e", t=TG),
                                              rn[:, :, None].to_broadcast([P, TG, G + E]), ALU.mult).then_inc(a_out, 1)
                        elif kind == "rp":
                            for j in range(TG):
                                last = dve.tensor_tensor(hit[:, j, :, :], hot[:, j, :, :],
                                                         bank[:, None, j * E:(j + 1) * E].to_broadcast([P, K, E]),
                                                         ALU.mult)
                            last.then_inc(a_out, 1)
                        else:
                            out = {"t": xt, "q": qt[par], "k": kt[par], "v": vv[par], "rt": rxt}[kind]
                            dve.tensor_copy(out[:, m, :], bank[:]).then_inc(a_out, 1)

                def finish(g, b):
                    s = g * TG + b
                    dve.wait_ge(o_done, ONE + s + 1)
                    dve.wait_ge(xb_rdy, ONE + g + 1)
                    row = k.x[:, bass.ds(s * D, D)]
                    dve.tensor_tensor(row, bank_o[:, 0:D], row, ALU.add).then_inc(h_rdy, 1)
                    dve.wait_ge(h_rdy, ONE + s + 1)
                    apart(dve, k.past_dve)
                    dve.bn_stats(stat[:, b, :], row).then_inc(stat_rdy, 1)
                    dve.wait_ge(stat_rdy, ONE + s + 1)
                    apart(dve, k.past_dve)
                    last = dve.bn_aggr(mv[:, b, :], stat[:, b, :])
                    if b == TG - 1:
                        last.then_inc(mv_rdy, 1)

                def normed(g):
                    dve.wait_ge(rs_rdy, ONE + g + 1)
                    for j in range(TG):
                        last = dve.tensor_scalar(rows(k.x, g, j, 1), rows(k.x, g, j, 1), mv[:, j, 0:1],
                                                 rs[:, j:j + 1], ALU.subtract, ALU.mult)
                    last.then_inc(x2_rdy, 1)

                def slot(g, par, b, fill, first):
                    s = g * TG + b
                    dve.wait_ge(s_done, ONE + s + 1)
                    for r in range(2):
                        last = dve.tensor_reduce(top[:, r * IC:(r + 1) * IC],
                                                 bank_s[r][:].rearrange("p (m t) -> p m t", m=IC), AX.X, ALU.max)
                    last.then_inc(top_rdy, 1)
                    dve.wait_ge(top_rdy, ONE + s + 1)
                    dve.wait_ge(e_rdy, ONE + s)
                    dve.tensor_scalar(nbias[:], top[:], -SCALE, None, ALU.mult).then_inc(nb_rdy, 1)
                    if b == 0:
                        dve.wait_ge(v_done, ONE + s)
                    fill()
                    dve.wait_ge(e_rdy, ONE + s + 1)
                    dve.reciprocal(rden[:], den[:]).then_inc(rden_rdy, 1)
                    dve.wait_ge(rden_rdy, ONE + s + 1)
                    for r in range(2):
                        part_ = prob[:, r * IC:(r + 1) * IC, :]
                        dve.tensor_tensor(part_, part_, rden[:, r * IC:(r + 1) * IC, None].to_broadcast([P, IC, T]),
                                          ALU.mult).then_inc(n_rdy, 1)
                    if not first:
                        finish(g - 1, TG - 1) if b == 0 else finish(g, b - 1)
                        if b == 0:
                            normed(g - 1)
                    if b == 1 and (not isinstance(g, int) or g >= 2):
                        place(g - 2)
                    if b >= 2 and (not isinstance(g, int) or g >= 1):
                        (choose_groups if b == 2 else choose_experts)(g - 1)
                    dve.wait_ge(v_done, ONE + s + 1)
                    dve.tensor_copy(ot[:], bank_v[:].rearrange("p (m t) -> p m t", m=IC)).then_inc(ot_rdy, 1)

                groups(dve, slot, part)
                finish(NG - 1, TG - 1)
                normed(NG - 1)
                part(NG + 1, 0, 1)
                place(NG - 2)
                part(NG + 1, 0, 2)
                choose_groups(NG - 1)
                choose_experts(NG - 1)
                part(NG + 2, 0, 1)
                place(NG - 1)
                plan.make(dve, bank_v)


def split_product(pe, out, chunks):
    last = None
    for n, ((lh, ll), (rh, rl)) in enumerate(chunks):
        for t, (a, b) in enumerate(((lh, rh), (lh, rl), (ll, rh))):
            last = pe.matmul(out, a, b, start=(n == 0 and t == 0), stop=(n == len(chunks) - 1 and t == 2))
    return last


def expert_stage(nc, k, dram):
    with ExitStack() as ctx:
        p = Parts(nc, ctx, "e_")
        raw_g, raw_u, raw_d = p.sb("raw_g", [P, DC, HID]), p.sb("raw_u", [P, DC, HID]), p.sb("raw_d", [P, HC, D])
        wg = [[p.sb(f"wg{i}{h}", [P, DC, HID], F32R) for h in "hl"] for i in range(2)]
        wu = [[p.sb(f"wu{i}{h}", [P, DC, HID], F32R) for h in "hl"] for i in range(2)]
        wd = [[p.sb(f"wd{i}{h}", [P, HC, D], F32R) for h in "hl"] for i in range(2)]
        tok = [p.sb(f"tok{i}", [RT, TI], I32) for i in range(2)]
        xg = [p.sb(f"xg{i}", [RT, TI, D]) for i in range(2)]
        xt = [p.sb(f"xt{h}", [P, DC, SETW], F32R) for h in "hl"]
        sg = [p.sb(f"sg{i}", [P, SETW]) for i in range(2)]
        hid = [p.sb(f"hid{i}", [P, SETW]) for i in range(2)]
        ht = [[p.sb(f"ht{i}{h}", [P, HC, SETW], F32R) for h in "hl"] for i in range(2)]
        out = [p.sb(f"out{i}", [RT, TI, D]) for i in range(2)]
        bank_t = [p.bank(f"t{i}") for i in range(2)]
        bank_g = [p.bank(f"g{i}") for i in range(2)]
        bank_u = [p.bank(f"u{i}") for i in range(2)]
        bank_d = [p.bank(f"d{i}") for i in range(2)]
        g_in, u_in, d_in = p.sem("g_in"), p.sem("u_in"), p.sem("d_in")
        tok_in = [p.sem(f"tok_in{i}") for i in range(2)]
        x_in = [p.sem(f"x_in{i}") for i in range(2)]
        stored = [p.sem(f"stored{i}") for i in range(2)]
        t_done, xh_rdy, xl_rdy = p.sem("t_done"), p.sem("xh"), p.sem("xl")
        g_done, u_done, d_done = p.sem("g_done"), p.sem("u_done"), p.sem("d_done")
        sg_rdy, hid_rdy, hh_rdy, hl_rdy = p.sem("sg"), p.sem("hid"), p.sem("hh"), p.sem("hl")
        wh_rdy, wl_rdy, out_rdy = p.sem("wh"), p.sem("wl"), p.sem("out")
        dh_rdy, dl_rdy = p.sem("dh"), p.sem("dl")

        ROUNDS = E * NSET // 2
        NP = TI // 2
        OUT = ONE + NP
        gate_d = dram["eg"].rearrange("e (c p) n -> p e c n", p=P)
        up_d = dram["eu"].rearrange("e (c p) n -> p e c n", p=P)
        down_d = dram["ed"].rearrange("e (c p) n -> p e c n", p=P)
        PIECES = [(raw_g, wg, 0), (raw_g, wg, 1), (raw_u, wu, 0), (raw_u, wu, 1)]
        assert len(PIECES) == HC == 4 and DC == 2

        def items_of(eng):
            return eng.value_load(k.plan[0:1, 2:3], min_val=1, max_val=E * NSET)

        def rounds(eng, first, again):
            n = items_of(eng)
            first()
            with eng.Fori(1, ROUNDS) as i:
                with eng.If(i * 2 < n):
                    again(i)
            n = items_of(eng)
            used = (n + 1) // 2
            return used, used * 2 - 1

        with nc.Block() as block:
            @block.sync
            def _(sp):
                begin(sp, dma=(g_in, u_in, d_in, *stored))

                def load(w):
                    e = sp.value_load(k.plan[0:1, bass.ds(w * 4 + 1, 1)], min_val=0, max_val=E - 1)

                    def one(d):
                        return d[:, bass.ds(e, 1), :, :].rearrange("p a c n -> p (a c) n")
                    later = not isinstance(w, int) or w > 0
                    if later:
                        sp.wait_ge(wl_rdy, ONE + HC * w - 2)
                    sp.dma_start(raw_g[:], one(gate_d)).then_inc(g_in, 16)
                    if later:
                        sp.wait_ge(wl_rdy, ONE + HC * w)
                    sp.dma_start(raw_u[:], one(up_d)).then_inc(u_in, 16)
                    if later:
                        sp.wait_ge(dl_rdy, ONE + HC * w)
                    sp.dma_start(raw_d[:], one(down_d)).then_inc(d_in, 16)

                def store(w, a):
                    start = sp.value_load(k.plan[0:1, bass.ds(w * 4, 1)], min_val=0, max_val=SLOTS)
                    sp.wait_ge(out_rdy, OUT + NP * (w + 1))
                    sp.dma_start(k.out_d[bass.ds(start, SETW), :].rearrange("(p n) d -> p n d", n=TI), out[a][:])\
                        .then_inc(stored[a], 16)

                def first():
                    load(0)
                    load(1)
                    load(2)
                    store(0, 0)

                def again(i):
                    load(2 * i + 1)
                    store(2 * i - 1, 1)
                    load(2 * i + 2)
                    store(2 * i, 0)

                used, last = rounds(sp, first, again)
                start = sp.value_load(k.plan[0:1, bass.ds(last * 4, 1)], min_val=0, max_val=SLOTS)
                sp.wait_ge(d_in, DMA + 16 * (last + 2))
                sp.wait_ge(out_rdy, OUT + NP * (last + 1))
                sp.dma_start(k.out_d[bass.ds(start, SETW), :].rearrange("(p n) d -> p n d", n=TI), out[1][:])\
                    .then_inc(stored[1], 16)
                for a in range(2):
                    sp.wait_ge(stored[a], DMA + 16 * used)
                apart(sp, k.past_sp)

            @block.gpsimd
            def _(pool):
                begin(pool, dl_rdy)

                def gather(w, a, i):
                    start = pool.value_load(k.plan[0:1, bass.ds(w * 4, 1)], min_val=0, max_val=SLOTS)
                    if not isinstance(i, int) or i:
                        pool.wait_ge(t_done, ONE + DC * (w - 1))
                    pool.dma_start(tok[a][:], k.slot_tok[bass.ds(start, SETW), :].rearrange("(p n) a -> p (n a)", n=TI))\
                        .then_inc(tok_in[a], 16)
                    pool.wait_ge(tok_in[a], 16 * (i + 1))
                    apart(pool, k.past_pool)
                    for n in range(TI):
                        pool.indirect_dma_start(xg[a][:, n, :], None, k.x2_d,
                                                bass.IndirectOffsetOnAxis(ap=tok[a][:, n:n + 1], axis=0))\
                            .then_inc(x_in[a], 16)

                def down_low(w, par):
                    if not isinstance(w, int) or w >= 2:
                        pool.wait_ge(d_done, ONE + NP * (w - 1))
                    for m in range(HC):
                        pool.wait_ge(dh_rdy, ONE + HC * w + m + 1)
                        pool.tensor_tensor(wd[par][1][:, m, :], raw_d[:, m, :], wd[par][0][:, m, :].bitcast(F32),
                                           ALU.subtract).then_inc(dl_rdy, 1)

                def first():
                    gather(0, 0, 0)
                    gather(1, 1, 0)
                    down_low(0, 0)
                    gather(2, 0, 1)
                    down_low(1, 1)

                def again(i):
                    gather(2 * i + 1, 1, i)
                    down_low(2 * i, 0)
                    gather(2 * i + 2, 0, i + 1)
                    down_low(2 * i + 1, 1)

                rounds(pool, first, again)

            @block.tensor
            def _(pe):
                begin(pe, t_done, g_done, u_done, d_done)

                def turn(w, a, i):
                    pe.wait_ge(x_in[a], 16 * TI * (i + 1))
                    if not isinstance(w, int) or w:
                        pe.wait_ge(xl_rdy, ONE + DC * w)
                    for c in range(DC):
                        for n in range(TI):
                            last = pe.transpose(bank_t[c][:, n * RT:(n + 1) * RT],
                                                xg[a][:, n, c * P:(c + 1) * P], k.ident[0:RT, 0:RT])
                        last.then_inc(t_done, 1)

                def up(w, a):
                    pe.wait_ge(xl_rdy, ONE + DC * (w + 1))
                    pe.wait_ge(wl_rdy, ONE + HC * (w + 1))
                    for m in range(HC):
                        job = HC * w + m
                        for wt, bank, used, done in ((wg, bank_g, sg_rdy, g_done), (wu, bank_u, hid_rdy, u_done)):
                            if not isinstance(job, int) or job >= 2:
                                pe.wait_ge(used, ONE + job - 1)
                            cols = slice(m * P, (m + 1) * P)
                            split_product(pe, bank[m % 2][:, 0:SETW],
                                          [((wt[a][0][:, c, cols], wt[a][1][:, c, cols]),
                                            (xt[0][:, c, :], xt[1][:, c, :])) for c in range(DC)]).then_inc(done, 1)

                def down(w, a):
                    pe.wait_ge(hl_rdy, ONE + HC * (w + 1))
                    pe.wait_ge(dl_rdy, ONE + HC * (w + 1))
                    for h in range(NP):
                        if not isinstance(w, int) or w:
                            pe.wait_ge(out_rdy, OUT + NP * (w - 1) + h + 1)
                        for t in (2 * h, 2 * h + 1):
                            rows_ = slice(t * RT, (t + 1) * RT)
                            last = split_product(pe, bank_d[h][0:RT, (t % 2) * D:(t % 2 + 1) * D],
                                                 [((ht[a][0][:, c, rows_], ht[a][1][:, c, rows_]),
                                                   (wd[a][0][:, c, :], wd[a][1][:, c, :])) for c in range(HC)])
                        last.then_inc(d_done, 1)

                def first():
                    turn(0, 0, 0)
                    up(0, 0)
                    turn(1, 1, 0)
                    up(1, 1)
                    turn(2, 0, 1)
                    down(0, 0)

                def again(i):
                    up(2 * i, 0)
                    turn(2 * i + 1, 1, i)
                    down(2 * i - 1, 1)
                    up(2 * i + 1, 1)
                    turn(2 * i + 2, 0, i + 1)
                    down(2 * i, 0)

                used, last = rounds(pe, first, again)
                down(last, 1)

            @block.scalar
            def _(act):
                begin(act, xh_rdy, sg_rdy, hh_rdy, wh_rdy, dh_rdy)

                def weights_high(w, par, m):
                    raw, high, c = PIECES[m]
                    if m in (0, 2):
                        act.wait_ge(g_in if m == 0 else u_in, DMA + 16 * (w + 1))
                        if not isinstance(w, int) or w >= 2:
                            act.wait_ge(u_done, ONE + HC * (w - 1))
                    act.activation(high[par][0][:, c, :], raw[:, c, :], ACT.Copy).then_inc(wh_rdy, 1)

                def down_high(w, par, m):
                    if m == 0:
                        act.wait_ge(d_in, DMA + 16 * (w + 1))
                        if not isinstance(w, int) or w >= 2:
                            act.wait_ge(d_done, ONE + NP * (w - 1))
                    act.activation(wd[par][0][:, m, :], raw_d[:, m, :], ACT.Copy).then_inc(dh_rdy, 1)

                def turned(w):
                    if not isinstance(w, int) or w:
                        act.wait_ge(u_done, ONE + HC * w)
                    for c in range(DC):
                        act.wait_ge(t_done, ONE + DC * w + c + 1)
                        act.activation(xt[0][:, c, :], bank_t[c][:, 0:SETW], ACT.Copy).then_inc(xh_rdy, 1)

                def hidden_high(w, a, m):
                    act.wait_ge(hid_rdy, ONE + HC * w + m + 1)
                    if m == 0 and (not isinstance(w, int) or w >= 2):
                        act.wait_ge(d_done, ONE + NP * (w - 1))
                    act.activation(ht[a][0][:, m, :], hid[m % 2][:], ACT.Copy).then_inc(hh_rdy, 1)

                def item(w, a):
                    for m in range(HC):
                        job = HC * w + m
                        act.wait_ge(g_done, ONE + job + 1)
                        if not isinstance(job, int) or job >= 2:
                            act.wait_ge(hid_rdy, ONE + job - 1)
                        act.activation(sg[m % 2][:], bank_g[m % 2][:, 0:SETW], ACT.Silu).then_inc(sg_rdy, 1)
                        weights_high(w + 1, 1 - a, m)
                        down_high(w, a, m)
                        if m:
                            hidden_high(w, a, m - 1)
                    hidden_high(w, a, HC - 1)
                    turned(w + 1)

                def first():
                    for m in range(HC):
                        weights_high(0, 0, m)
                    turned(0)
                    item(0, 0)
                    item(1, 1)

                def again(i):
                    item(2 * i, 0)
                    item(2 * i + 1, 1)

                rounds(act, first, again)

            @block.vector
            def _(dve):
                begin(dve, xl_rdy, hid_rdy, hl_rdy, wl_rdy, out_rdy)
                dve.sem_inc(out_rdy, NP)

                def weights_low(w, par, m):
                    raw, parts, c = PIECES[m]
                    dve.wait_ge(wh_rdy, ONE + HC * w + m + 1)
                    dve.tensor_tensor(parts[par][1][:, c, :], raw[:, c, :], parts[par][0][:, c, :].bitcast(F32),
                                      ALU.subtract).then_inc(wl_rdy, 1)

                def turned(w):
                    for c in range(DC):
                        dve.wait_ge(xh_rdy, ONE + DC * w + c + 1)
                        dve.tensor_tensor(xt[1][:, c, :], bank_t[c][:, 0:SETW], xt[0][:, c, :].bitcast(F32),
                                          ALU.subtract).then_inc(xl_rdy, 1)

                def hidden_low(w, a, m):
                    dve.wait_ge(hh_rdy, ONE + HC * w + m + 1)
                    dve.tensor_tensor(ht[a][1][:, m, :], hid[m % 2][:], ht[a][0][:, m, :].bitcast(F32),
                                      ALU.subtract).then_inc(hl_rdy, 1)

                def item(w, a):
                    for m in range(HC):
                        job = HC * w + m
                        dve.wait_ge(sg_rdy, ONE + job + 1)
                        dve.wait_ge(u_done, ONE + job + 1)
                        if not isinstance(job, int) or job >= 2:
                            dve.wait_ge(hl_rdy, ONE + job - 1)
                        dve.tensor_tensor(hid[m % 2][:], sg[m % 2][:], bank_u[m % 2][:, 0:SETW], ALU.mult)\
                           .then_inc(hid_rdy, 1)
                        weights_low(w + 1, 1 - a, m)
                        if m:
                            hidden_low(w, a, m - 1)
                    hidden_low(w, a, HC - 1)
                    turned(w + 1)

                def copied(w, a, i):
                    if not isinstance(i, int) or i:
                        dve.wait_ge(stored[a], DMA + 16 * i)
                    for h in range(NP):
                        dve.wait_ge(d_done, ONE + NP * w + h + 1)
                        dve.tensor_copy(out[a][:, 2 * h:2 * h + 2, :],
                                        bank_d[h][0:RT, :].rearrange("p (t d) -> p t d", t=2)).then_inc(out_rdy, 1)

                def first():
                    for m in range(HC):
                        weights_low(0, 0, m)
                    turned(0)
                    item(0, 0)
                    item(1, 1)
                    copied(0, 0, 0)

                def again(i):
                    item(2 * i, 0)
                    copied(2 * i - 1, 1, i - 1)
                    item(2 * i + 1, 1)
                    copied(2 * i, 0, i)

                used, last = rounds(dve, first, again)
                dve.wait_ge(stored[1], DMA + 16 * (used - 1))
                for h in range(NP):
                    dve.wait_ge(d_done, ONE + NP * last + h + 1)
                    dve.tensor_copy(out[1][:, 2 * h:2 * h + 2, :],
                                    bank_d[h][0:RT, :].rearrange("p (t d) -> p t d", t=2)).then_inc(out_rdy, 1)


def combine_stage(nc, k, dram):
    with ExitStack() as ctx:
        p = Parts(nc, ctx, "f_")
        raw = [p.sb("raw_g", [P, DC, HID]), p.sb("raw_u", [P, DC, HID]), p.sb("raw_d", [P, HC, D])]
        wg, wu, wd = ([p.sb(f"w{n}{h}", raw[i].shape, F32R) for h in "hl"] for i, n in enumerate("gud"))
        idx = [p.sb(f"idx{i}", [P, TG, K], I32) for i in range(2)]
        row = [p.sb(f"row{i}", [P, TG, K, D]) for i in range(2)]
        res = [p.sb(f"res{i}", [P, TG, D]) for i in range(2)]
        xs, xt = p.sb("xs", [P, TG, D]), [p.sb(f"xt{h}", [P, DC, GW], F32R) for h in "hl"]
        sg, hid = ([p.sb(f"{n}{i}", [P, GW]) for i in range(2)] for n in ("sg", "hid"))
        ht = [p.sb(f"ht{h}", [P, HC, GW], F32R) for h in "hl"]
        stat, mv = p.sb("stat", [P, TG, 6]), p.sb("mv", [P, TG, 2])
        ve, rs = p.sb("ve", [P, TG]), p.sb("rs", [P, TG])
        bank_t = [p.bank(f"t{i}") for i in range(2)]
        bank_g = [p.bank(f"g{i}") for i in range(2)]
        bank_u = [p.bank(f"u{i}") for i in range(2)]
        bank_d = [p.bank(f"d{i}") for i in range(2)]
        w_in, xs_rdy, idx_rdy = p.sem("w_in"), p.sem("xs"), p.sem("idx")
        row_in = [p.sem(f"row_in{i}") for i in range(2)]
        wh_rdy, wl_rdy, xl_rdy, hh_rdy, hl_rdy = (p.sem(n) for n in ("wh", "wl", "xl", "hh", "hl"))
        t_done, xh_rdy, g_done, u_done = p.sem("t_done"), p.sem("xh"), p.sem("g_done"), p.sem("u_done")
        sg_rdy, hid_rdy, d_done, sum_rdy = p.sem("sg"), p.sem("h"), p.sem("d_done"), p.sem("sum")
        add_rdy, stat_rdy, mv_rdy, ve_rdy = p.sem("add"), p.sem("stat"), p.sem("mv"), p.sem("ve")
        rs_rdy, res_rdy = p.sem("rs"), p.sem("res")
        stored = [p.sem(f"stored{i}") for i in range(2)]
        out_d = dram["out"].rearrange("b t d -> t b d")

        with nc.Block() as block:
            @block.sync
            def _(sp):
                begin(sp, dma=(w_in, *stored,))
                for w, name in zip(raw, ("sg", "su", "sd")):
                    sp.dma_start(w[:], dram[name].rearrange("(c p) n -> p c n", p=P)).then_inc(w_in, 16)
                with sp.Fori(0, NG // 2) as i:
                    for a in range(2):
                        g = 2 * i + a
                        sp.wait_ge(res_rdy, ONE + g + 1)
                        sp.dma_start(out_d[:, bass.ds(g * TG, TG), :], res[a][:]).then_inc(stored[a], 16)
                for a in range(2):
                    sp.wait_ge(stored[a], DMA + 16 * (NG // 2))

            @block.gpsimd
            def _(pool):
                begin(pool, idx_rdy, ve_rdy, rs_rdy)
                def fetch(g, i, a, first=False):
                    if not first:
                        pool.wait_ge(row_in[a], 16 * TG * K * i)
                    pool.tensor_copy(idx[a][:].rearrange("p t q -> p (t q)"),
                                     k.slot[:, bass.ds(g * TG * K, TG * K)]).then_inc(idx_rdy, 1)
                    pool.wait_ge(idx_rdy, ONE + g + 1)
                    apart(pool, k.past_pool)
                    for j in range(TG):
                        for q in range(K):
                            pool.indirect_dma_start(row[a][:, j, q, :], None, k.out_d[0:SLOTS, :],
                                                    bass.IndirectOffsetOnAxis(ap=idx[a][:, j, q:q + 1], axis=0))\
                                .then_inc(row_in[a], 16)

                def rstd(g):
                    pool.wait_ge(mv_rdy, ONE + g + 1)
                    apart(pool, k.past_pool)
                    pool.tensor_scalar(ve[:], mv[:, :, 1], EPS, None, ALU.add).then_inc(ve_rdy, 1)
                    pool.wait_ge(ve_rdy, ONE + g + 1)
                    pool.tensor_tensor(rs[:], ve[:], k.mhalf[:], ALU.pow).then_inc(rs_rdy, 1)

                fetch(0, 0, 0, True)
                fetch(1, 0, 1, True)
                rstd(0)
                with pool.Fori(1, NG // 2) as i:
                    fetch(2 * i, i, 0)
                    rstd(2 * i - 1)
                    fetch(2 * i + 1, i, 1)
                    rstd(2 * i)
                rstd(NG - 1)

            @block.tensor
            def _(pe):
                begin(pe, t_done, g_done, u_done, d_done)
                def turn(g):
                    pe.wait_ge(xs_rdy, ONE + g + 1)
                    pe.wait_ge(xl_rdy, ONE + DC * g)
                    for c in range(DC):
                        for j in range(TG):
                            last = pe.transpose(bank_t[c][:, j * P:(j + 1) * P], xs[:, j, c * P:(c + 1) * P], k.ident[:])
                        last.then_inc(t_done, 1)

                def up(g):
                    pe.wait_ge(xl_rdy, ONE + DC * (g + 1))
                    for m in range(HC):
                        job = HC * g + m
                        cols = slice(m * P, (m + 1) * P)
                        for w, bank, used, done in ((wg, bank_g, sg_rdy, g_done), (wu, bank_u, hid_rdy, u_done)):
                            pe.wait_ge(used, ONE + job)
                            split_product(pe, bank[m % 2][:],
                                          [((w[0][:, c, cols], w[1][:, c, cols]), (xt[0][:, c, :], xt[1][:, c, :]))
                                           for c in range(DC)]).then_inc(done, 1)

                def down(g):
                    pe.wait_ge(hl_rdy, ONE + HC * (g + 1) + 1)
                    pe.wait_ge(sum_rdy, ONE + 2 * g)
                    for h in range(2):
                        for t in range(2):
                            toks = slice((2 * h + t) * T, (2 * h + t + 1) * T)
                            last = split_product(pe, bank_d[h][:, t * D:(t + 1) * D],
                                                 [((ht[0][:, c, toks], ht[1][:, c, toks]), (wd[0][:, c, :], wd[1][:, c, :]))
                                                  for c in range(HC)])
                        last.then_inc(d_done, 1)

                turn(0)
                pe.wait_ge(wl_rdy, 3)
                with pe.Fori(0, NG - 1) as g:
                    up(g)
                    turn(g + 1)
                    down(g)
                up(NG - 1)
                down(NG - 1)

            @block.scalar
            def _(act):
                begin(act, xs_rdy, xh_rdy, sg_rdy, hh_rdy)
                act.sem_inc(sg_rdy, 1)

                def stage(g):
                    act.wait_ge(t_done, ONE + DC * g)
                    act.activation(xs[:], grouped(rows(k.x, g)), ACT.Copy).then_inc(xs_rdy, 1)

                def turned(g):
                    act.wait_ge(u_done, ONE + HC * g)
                    for c in range(DC):
                        act.wait_ge(t_done, ONE + DC * g + c + 1)
                        act.activation(xt[0][:, c, :], bank_t[c][:], ACT.Copy).then_inc(xh_rdy, 1)

                def hidden_high(g, m):
                    act.wait_ge(hid_rdy, ONE + HC * g + m + 2)
                    if m == 0:
                        act.wait_ge(d_done, ONE + 2 * g)
                    act.activation(ht[0][:, m, :], hid[m % 2][:], ACT.Copy).then_inc(hh_rdy, 1)

                def gate(g):
                    for m in range(HC):
                        act.wait_ge(g_done, ONE + HC * g + m + 1)
                        act.wait_ge(hid_rdy, ONE + HC * g + m)
                        act.activation(sg[m % 2][:], bank_g[m % 2][:], ACT.Silu).then_inc(sg_rdy, 1)
                        if m:
                            hidden_high(g, m - 1)
                    hidden_high(g, HC - 1)

                stage(0)
                for i, w in enumerate((wg, wu, wd)):
                    act.wait_ge(w_in, DMA + 48)
                    act.activation(w[0][:], raw[i][:], ACT.Copy).then_inc(wh_rdy, 1)
                turned(0)
                stage(1)
                with act.Fori(0, NG - 2) as g:
                    gate(g)
                    turned(g + 1)
                    stage(g + 2)
                gate(NG - 2)
                turned(NG - 1)
                gate(NG - 1)

            @block.vector
            def _(dve):
                begin(dve, xl_rdy, hid_rdy, hl_rdy, sum_rdy, add_rdy, stat_rdy, mv_rdy, res_rdy)
                dve.sem_inc(hid_rdy, 1)
                dve.sem_inc(hl_rdy, 1)
                ADDS = TG * K

                def turned(g):
                    for c in range(DC):
                        dve.wait_ge(xh_rdy, ONE + DC * g + c + 1)
                        dve.tensor_tensor(xt[1][:, c, :], bank_t[c][:], xt[0][:, c, :].bitcast(F32), ALU.subtract)\
                           .then_inc(xl_rdy, 1)

                def hidden_low(g, m):
                    dve.wait_ge(hh_rdy, ONE + HC * g + m + 1)
                    dve.tensor_tensor(ht[1][:, m, :], hid[m % 2][:], ht[0][:, m, :].bitcast(F32), ALU.subtract)\
                       .then_inc(hl_rdy, 1)

                def adds(g, a, i, q):
                    if q == 0:
                        dve.wait_ge(row_in[a], 16 * TG * K * (i + 1))
                        dve.wait_ge(sum_rdy, ONE + 2 * g + 2)
                    for j in range(TG):
                        if q:
                            dve.wait_ge(add_rdy, ONE + ADDS * g + TG * (q - 1) + j + 1)
                        dve.scalar_tensor_tensor(res[a][:, j, :], row[a][:, j, q, :],
                                                 k.gate[:, bass.ds(g * TG * K + j * K + q, 1)],
                                                 res[a][:, j, :], ALU.mult, ALU.add).then_inc(add_rdy, 1)

                def moments(g, a):
                    for j in range(TG):
                        dve.wait_ge(add_rdy, ONE + ADDS * g + TG * (K - 1) + j + 1)
                        apart(dve, k.past_dve)
                        dve.bn_stats(stat[:, j, :], res[a][:, j, :]).then_inc(stat_rdy, 1)
                    for j in range(TG):
                        dve.wait_ge(stat_rdy, ONE + TG * g + j + 1)
                        apart(dve, k.past_dve)
                        last = dve.bn_aggr(mv[:, j, :], stat[:, j, :])
                    last.then_inc(mv_rdy, 1)

                def normed(g, a):
                    dve.wait_ge(rs_rdy, ONE + g + 1)
                    for j in range(TG):
                        last = dve.tensor_scalar(res[a][:, j, :], res[a][:, j, :], mv[:, j, 0:1], rs[:, j:j + 1],
                                                 ALU.subtract, ALU.mult)
                    last.then_inc(res_rdy, 1)

                def group(g, a, i):
                    before = (g - 1, 1 - a, i if a else i - 1)
                    finishes = not isinstance(g, int) or g > 0
                    for m in range(HC):
                        dve.wait_ge(sg_rdy, ONE + HC * g + m + 2)
                        dve.wait_ge(u_done, ONE + HC * g + m + 1)
                        dve.wait_ge(hl_rdy, ONE + HC * g + m)
                        dve.tensor_tensor(hid[m % 2][:], sg[m % 2][:], bank_u[m % 2][:], ALU.mult).then_inc(hid_rdy, 1)
                        if m:
                            hidden_low(g, m - 1)
                        if finishes:
                            adds(*before, m)
                    hidden_low(g, HC - 1)
                    if finishes:
                        moments(g - 1, 1 - a)
                    if not isinstance(g, int) or g < NG - 1:
                        turned(g + 1)
                    if finishes:
                        normed(g - 1, 1 - a)
                    if not isinstance(i, int) or i:
                        dve.wait_ge(stored[a], DMA + 16 * i)
                    for h in range(2):
                        dve.wait_ge(d_done, ONE + 2 * g + h + 1)
                        dve.tensor_tensor(res[a][:, 2 * h:2 * h + 2, :],
                                          bank_d[h][:].rearrange("p (t d) -> p t d", t=2),
                                          grouped(rows(k.x, g, 2 * h, 2), 2), ALU.add).then_inc(sum_rdy, 1)

                for i, w in enumerate((wg, wu, wd)):
                    dve.wait_ge(wh_rdy, i + 1)
                    dve.tensor_tensor(w[1][:], raw[i][:], w[0][:].bitcast(F32), ALU.subtract).then_inc(wl_rdy, 1)
                turned(0)
                group(0, 0, 0)
                group(1, 1, 0)
                with dve.Fori(1, NG // 2 - 1) as i:
                    group(2 * i, 0, i)
                    group(2 * i + 1, 1, i)
                group(NG - 2, 0, NG // 2 - 1)
                group(NG - 1, 1, NG // 2 - 1)
                for q in range(K):
                    adds(NG - 1, 1, NG // 2 - 1, q)
                moments(NG - 1, 1)
                normed(NG - 1, 1)


class Kept:
    pass


def build(nc, dram):
    with ExitStack() as ctx:
        def sb(name, shape, dt=F32):
            return ctx.enter_context(nc.sbuf_tensor(name, shape, dt))

        k = Kept()
        k.x = sb("x", [P, B * D])
        k.ident, k.before, k.ones = sb("ident", [P, P]), sb("before", [P, P]), sb("ones", [P, P])
        k.mhalf = sb("mhalf", [P, TG])
        k.td, k.tf, k.gam, k.bet = (sb(n, [P, DC]) for n in ("td", "tf", "gam", "bet"))
        k.decay, k.keep = sb("decay", [P, DC, T]), sb("keep", [P, GW])
        k.wkv_in = sb("wkv_in", [P, DC, GW + 1])
        k.bout, k.ebias = sb("bout", [P, D]), sb("ebias", [P, E])
        k.cent, k.iota_e = sb("cent", [P, DC, G + E]), sb("iota_e", [P, E])
        k.tok, k.count = sb("tok", [P, TG], I32), sb("count", [P, E])
        k.gate, k.slot = sb("gate", [P, B * K]), sb("slot", [P, B * K], I32)
        k.past_dve, k.past_pool, k.past_sp = (ctx.enter_context(nc.semaphore(f"past_{n}")) for n in ("dve", "pool", "sp"))
        k.x2_d = nc.dram_tensor("x2_rows", [B * T, D], F32).ap()
        k.out_d = nc.dram_tensor("expert_rows", [SLOTS + SETW, D], F32).ap()
        k.plan = sb("plan", [1, 4 * P], I32)
        k.plan_d = nc.dram_tensor("item_list", [P, 4], I32).ap()
        k.slot_tok = nc.dram_tensor("slot_token", [SLOTS + SETW, 1], I32).ap()
        setup_stage(nc, k, dram)
        mixer_stage(nc, k, dram)
        attention_stage(nc, k, dram)
        expert_stage(nc, k, dram)
        combine_stage(nc, k, dram)


_AS_THEY_ARE = {
    "x": "x", "td": "L0_attn_time_decay", "tf": "L0_attn_time_first", "gam": "L0_attn_ln_gamma",
    "bet": "L0_attn_ln_beta", "wq": "L0_xattn_Wq", "wxk": "L0_xattn_Wk", "wxv": "L0_xattn_Wv",
    "wout": "L0_xattn_Wout", "bout": "L0_xattn_bout", "gcen": "L0_ffn_group_centroids",
    "ecen": "L0_ffn_expert_centroids", "ebias": "L0_ffn_bias", "eg": "L0_ffn_wg", "eu": "L0_ffn_wu",
    "ed": "L0_ffn_wd", "sg": "L0_ffn_sg", "su": "L0_ffn_su", "sd": "L0_ffn_sd",
}
_TRANSPOSED = {"wk": "L0_attn_Wk", "wv": "L0_attn_Wv", "wr": "L0_attn_Wr", "wo": "L0_attn_Wo"}


def kernel(**inputs):
    import numpy as np
    import concourse.bacc as bacc
    from concourse.bass_utils import run_bass_kernel_spmd

    arrays = {n: np.ascontiguousarray(inputs[key]) for n, key in _AS_THEY_ARE.items()}
    arrays.update({n: np.ascontiguousarray(np.transpose(inputs[key])) for n, key in _TRANSPOSED.items()})
    context = np.asarray(inputs["ctx_768"])
    arrays["ctx"] = np.ascontiguousarray(np.transpose(context, (2, 0, 1)).reshape(CD, B * T))

    nc = bacc.Bacc("TRN2", target_bir_lowering=False, num_devices=1)
    dram = {n: nc.dram_tensor(f"in_{n}", a.shape, mybir.dt.from_np(a.dtype), kind="ExternalInput").ap()
            for n, a in arrays.items()}
    dram["out"] = nc.dram_tensor("out_rows", (B, T, D), F32, kind="ExternalOutput").ap()
    build(nc, dram)
    result = run_bass_kernel_spmd(nc, [{f"in_{n}": a for n, a in arrays.items()}], core_ids=[0])
    return result.results[0]["out_rows"]
```
